# Optimizing a Trainium2 kernel written in Bass

```python
import numpy as np
import jax
import jax.numpy as jnp

def _softmax(x, axis=-1):
    return jax.nn.softmax(x, axis=axis)

def _gelu(x):
    return jax.nn.gelu(x, approximate=True)

def _silu(x):
    return jax.nn.silu(x)

def _sigmoid(x):
    return jax.nn.sigmoid(x)

def _layernorm(x, axis=-1, eps=1e-05):
    m = jnp.mean(x, axis=axis, keepdims=True)
    v = jnp.var(x, axis=axis, keepdims=True)
    return (x - m) / jnp.sqrt(v + eps)

def _scatter_add(tgt, idx, src, axis=0):
    return tgt.at[idx].add(src)

def _segment_sum(src, seg, n):
    return jax.ops.segment_sum(src, seg, n)
kernel_name = 'mk_hybrid_d1_jaxref_r4_f2c84c'

def setup_inputs(seed: int=0):
    np.random.seed(seed)
    _w = jnp.asarray

    def _L0_attn_a_setup():
        import jax, jax.numpy as jnp
        import numpy as np
        D_MODEL = 256
        NUM_HEADS = 16
        BATCH = 2
        SEQ = 512

        def _trunc_normal(key, shape, std):
            return jax.random.truncated_normal(key, -3.0, 3.0, shape, dtype=jnp.float32) * std
        key = jax.random.key(seed)
        kx, kq, kk, kv, ko = jax.random.split(key, 5)
        std = (2.0 / (D_MODEL + D_MODEL)) ** 0.5
        return {'X': jax.random.normal(kx, (BATCH, SEQ, D_MODEL), dtype=jnp.float32), 'q_proj': _trunc_normal(kq, (D_MODEL, D_MODEL), std), 'k_proj': _trunc_normal(kk, (D_MODEL, D_MODEL), std), 'v_proj': _trunc_normal(kv, (D_MODEL, D_MODEL), std), 'o_proj': _trunc_normal(ko, (D_MODEL, D_MODEL), std)}
    _L0_attn_a_in = _L0_attn_a_setup()

    def _L0_attn_b_setup():
        import math
        import jax, jax.numpy as jnp
        import numpy as np
        EXP_SCALING = 10.0
        KEY_SCALE_MAX = math.log(2 ** 16 - 1)
        key = jax.random.key(seed)
        ks = jax.random.split(key, 5)
        B, T, C, nh = (2, 512, 256, 16)
        x = jax.random.normal(ks[0], (B, T, C), dtype=jnp.float32)
        W_k = jax.random.normal(ks[1], (C, C), dtype=jnp.float32) * 0.02
        W_v = jax.random.normal(ks[2], (C, C), dtype=jnp.float32) * 0.02
        W_c = jax.random.normal(ks[3], (C, C), dtype=jnp.float32) * 0.02
        leaky_key_beta = (jnp.linspace(0.5, 5.0, nh).reshape(1, nh, 1, 1) / EXP_SCALING).astype(jnp.float32)
        key_scale = jnp.ones((1, nh, 1, 1), jnp.float32) / EXP_SCALING
        v_coef = jax.random.uniform(ks[4], (1, nh, 1, 1), dtype=jnp.float32)
        val_scale = jnp.full((1, nh, 1, 1), -0.5 / EXP_SCALING, jnp.float32)
        return dict(x=x, W_k=W_k, W_v=W_v, W_c=W_c, leaky_key_beta=leaky_key_beta, key_scale=key_scale, v_coef=v_coef, val_scale=val_scale)
    _L0_attn_b_in = _L0_attn_b_setup()

    def _L0_ffn_setup():
        import jax, jax.numpy as jnp
        import numpy as np
        DIM = 256

        def _reference_tuple_inner(x, W_r, W_k, W_v, mu_r, mu_k):
            B, T, C = x.shape
            x_prev = jnp.concatenate([jnp.zeros((B, 1, C), x.dtype), x[:, :-1, :]], axis=1)
            xr = mu_r * x + (1.0 - mu_r) * x_prev
            xk = mu_k * x + (1.0 - mu_k) * x_prev
            r = jax.nn.sigmoid(jnp.einsum('btc,dc->btd', xr, W_r))
            k = jnp.einsum('btc,dc->btd', xk, W_k)
            k_act = jnp.square(jax.nn.relu(k))
            out = r * jnp.einsum('btc,dc->btd', k_act, W_v)
            new_state = x[:, -1, :]
            return (out, new_state)
        key = jax.random.key(seed)
        ks = jax.random.split(key, 6)
        B, T, C = (8, 512, DIM)
        x = jax.random.normal(ks[0], (B, T, C), dtype=jnp.float32)
        s = 1.0 / np.sqrt(C)
        W_r = jax.random.uniform(ks[1], (C, C), jnp.float32, -s, s)
        W_k = jax.random.uniform(ks[2], (C, C), jnp.float32, -s, s)
        W_v = jax.random.uniform(ks[3], (C, C), jnp.float32, -s, s)
        mu_r = jax.random.uniform(ks[4], (C,), jnp.float32)
        mu_k = jax.random.uniform(ks[5], (C,), jnp.float32)
        return {'x': x, 'W_r': W_r, 'W_k': W_k, 'W_v': W_v, 'mu_r': mu_r, 'mu_k': mu_k}
    _L0_ffn_in = _L0_ffn_setup()
    _d = {'L0_attn_a_X': _L0_attn_a_in['X'], 'L0_attn_a_q_proj': _L0_attn_a_in['q_proj'], 'L0_attn_a_k_proj': _L0_attn_a_in['k_proj'], 'L0_attn_a_v_proj': _L0_attn_a_in['v_proj'], 'L0_attn_a_o_proj': _L0_attn_a_in['o_proj'], 'L0_attn_b_W_k': _L0_attn_b_in['W_k'], 'L0_attn_b_W_v': _L0_attn_b_in['W_v'], 'L0_attn_b_W_c': _L0_attn_b_in['W_c'], 'L0_attn_b_leaky_key_beta': _L0_attn_b_in['leaky_key_beta'], 'L0_attn_b_key_scale': _L0_attn_b_in['key_scale'], 'L0_attn_b_v_coef': _L0_attn_b_in['v_coef'], 'L0_attn_b_val_scale': _L0_attn_b_in['val_scale'], 'L0_ffn_W_r': _L0_ffn_in['W_r'], 'L0_ffn_W_k': _L0_ffn_in['W_k'], 'L0_ffn_W_v': _L0_ffn_in['W_v'], 'L0_ffn_mu_r': _L0_ffn_in['mu_r'], 'L0_ffn_mu_k': _L0_ffn_in['mu_k']}
    _x0 = _d['L0_attn_a_X']
    _d['L0_attn_a_X'] = jax.random.normal(jax.random.fold_in(jax.random.key(seed), 1), (4, 2048, 256), dtype=_x0.dtype)
    del _x0
    return _d

def reference(L0_attn_a_X, L0_attn_a_q_proj, L0_attn_a_k_proj, L0_attn_a_v_proj, L0_attn_a_o_proj, L0_attn_b_W_k, L0_attn_b_W_v, L0_attn_b_W_c, L0_attn_b_leaky_key_beta, L0_attn_b_key_scale, L0_attn_b_v_coef, L0_attn_b_val_scale, L0_ffn_W_r, L0_ffn_W_k, L0_ffn_W_v, L0_ffn_mu_r, L0_ffn_mu_k):

    def _L0_attn_a_ref(X, q_proj, k_proj, v_proj, o_proj):
        import jax, jax.numpy as jnp
        import numpy as np
        D_MODEL = 256
        NUM_HEADS = 16
        BATCH = 2
        SEQ = 512

        def _trunc_normal(key, shape, std):
            return jax.random.truncated_normal(key, -3.0, 3.0, shape, dtype=jnp.float32) * std
        B, S, D = X.shape
        H = NUM_HEADS
        d_k = D // H
        q_w = q_proj.reshape(H, d_k, D)
        k_w = k_proj.reshape(H, d_k, D)
        v_w = v_proj.reshape(H, d_k, D)
        o_w = o_proj.reshape(D, H, d_k).transpose(1, 0, 2)
        q = jnp.einsum('hkd,bsd->bhsk', q_w, X)
        k = jnp.einsum('hkd,bsd->bhsk', k_w, X)
        v = jnp.einsum('hkd,bsd->bhsk', v_w, X)
        scale = 1.0 / jnp.sqrt(jnp.asarray(d_k, dtype=X.dtype))
        scores = jnp.einsum('bhqk,bhsk->bhqs', q, k) * scale
        causal = jnp.tril(jnp.ones((S, S), dtype=bool))
        scores = jnp.where(causal, scores, jnp.asarray(-jnp.inf, dtype=scores.dtype))
        attn = jax.nn.softmax(scores, axis=-1)
        attn_out = jnp.einsum('bhqs,bhsk->bhqk', attn, v)
        return jnp.einsum('hdv,bhsv->bsd', o_w, attn_out)

    def _L0_attn_b_ref(x, W_k, W_v, W_c, leaky_key_beta, key_scale, v_coef, val_scale):
        import math
        import jax, jax.numpy as jnp
        import numpy as np
        EXP_SCALING = 10.0
        KEY_SCALE_MAX = math.log(2 ** 16 - 1)
        B, T, C = x.shape
        nh = leaky_key_beta.shape[1]
        hs = C // nh
        k = (x @ W_k.T).reshape(B, T, nh, hs).transpose(0, 2, 1, 3)
        t = jnp.arange(T)
        dec = t[:, None] - t[None, :]
        causal = dec >= 0
        dec_f = jnp.where(causal, dec, 0).astype(x.dtype)
        beta = jnp.abs(leaky_key_beta).reshape(nh, 1, 1) * EXP_SCALING
        coef = jnp.where(causal[None], jnp.exp(-dec_f[None] * beta), 0.0)
        k = jnp.einsum('hij,bhjd->bhid', coef, k)
        k = k / (jnp.linalg.norm(k, axis=-1, keepdims=True) + 1e-10)
        k = k * jnp.exp(jnp.minimum(EXP_SCALING * key_scale, KEY_SCALE_MAX))
        v = (x @ W_v.T).reshape(B, T, nh, hs).transpose(0, 2, 1, 3)
        v_shift = jnp.concatenate([v[:, :, 1:], jnp.zeros_like(v[:, :, :1])], axis=2)
        v = (1.0 - v_coef) * v_shift + v_coef * v
        v = v / (jnp.linalg.norm(v, axis=-1, keepdims=True) + 1e-10)
        v = v * jnp.exp(EXP_SCALING * val_scale)
        q = k[:, :, 1:]
        att = jnp.einsum('bhqd,bhkd->bhqk', q, k)
        mask = t[None, :] <= t[:T - 1, None]
        att = jnp.where(mask[None, None], att, -jnp.inf)
        att = jax.nn.softmax(att, axis=-1)
        y1 = jnp.einsum('bhqk,bhkd->bhqd', att, v)
        y = jnp.concatenate([jnp.zeros_like(y1[:, :, :1]), y1], axis=2)
        y = y.transpose(0, 2, 1, 3).reshape(B, T, C)
        return y @ W_c.T

    def _L0_ffn_ref(x, W_r, W_k, W_v, mu_r, mu_k):
        import jax, jax.numpy as jnp
        import numpy as np
        DIM = 256

        def _reference_tuple_inner(x, W_r, W_k, W_v, mu_r, mu_k):
            B, T, C = x.shape
            x_prev = jnp.concatenate([jnp.zeros((B, 1, C), x.dtype), x[:, :-1, :]], axis=1)
            xr = mu_r * x + (1.0 - mu_r) * x_prev
            xk = mu_k * x + (1.0 - mu_k) * x_prev
            r = jax.nn.sigmoid(jnp.einsum('btc,dc->btd', xr, W_r))
            k = jnp.einsum('btc,dc->btd', xk, W_k)
            k_act = jnp.square(jax.nn.relu(k))
            out = r * jnp.einsum('btc,dc->btd', k_act, W_v)
            new_state = x[:, -1, :]
            return (out, new_state)
        return _reference_tuple_inner(x, W_r, W_k, W_v, mu_r, mu_k)[0]
    x = L0_attn_a_X
    x = x + _L0_attn_a_ref(_layernorm(x, axis=-1), L0_attn_a_q_proj, L0_attn_a_k_proj, L0_attn_a_v_proj, L0_attn_a_o_proj)
    x = x + _L0_ffn_ref(_layernorm(x, axis=-1), L0_ffn_W_r, L0_ffn_W_k, L0_ffn_W_v, L0_ffn_mu_r, L0_ffn_mu_k)
    x = x + _L0_attn_b_ref(_layernorm(x, axis=-1), L0_attn_b_W_k, L0_attn_b_W_v, L0_attn_b_W_c, L0_attn_b_leaky_key_beta, L0_attn_b_key_scale, L0_attn_b_v_coef, L0_attn_b_val_scale)
    x = x + _L0_ffn_ref(_layernorm(x, axis=-1), L0_ffn_W_r, L0_ffn_W_k, L0_ffn_W_v, L0_ffn_mu_r, L0_ffn_mu_k)
    return x

_drawn_inputs = setup_inputs


def setup_inputs(seed=0):
    import zlib

    import numpy as np

    out = dict(_drawn_inputs(seed))
    spreads = {'L0_attn_b_key_scale': (0.10000000149011612, 0.6),
     'L0_attn_b_val_scale': (-0.05000000074505806, 0.6)}
    factors = {'L0_attn_b_W_k': 5.495,
     'L0_attn_b_W_v': 4.756,
     'L0_attn_b_W_c': 4.783,
     'L0_attn_b_leaky_key_beta': 64.0,
     'L0_attn_b_v_coef': 8.0,
     'L0_ffn_mu_r': 3.248}
    for name, (base, spread) in spreads.items():
        noise = np.random.default_rng([zlib.crc32(name.encode()), seed]).standard_normal(out[name].shape)
        drawn = base * np.exp(spread * noise) if base else spread * noise
        out[name] = jnp.asarray(drawn.astype(out[name].dtype))
    for name, factor in factors.items():
        out[name] = (out[name] * factor).astype(out[name].dtype)
    return out
```

```python
from contextlib import ExitStack

import concourse.bass as bass
from concourse import mybir

F32 = mybir.dt.float32
BF16 = mybir.dt.bfloat16
I32 = mybir.dt.int32
ACT = mybir.ActivationFunctionType
ALU = mybir.AluOpType
AX_X = mybir.AxisListType.X

P = 128
B, S, D, H = 4, 2048, 256, 16
DK = D // H
KT = D // P
NT = S // P
CH = 512
NCH = S // CH
TB = CH // P
HG = 4
NHG = H // HG
HS = 32
EPS = 1e-5
NORM_EPS = 1e-10
SCALE = {"A": DK ** -0.5, "B": 1.0}
EXP_SCALING = 10.0
KEY_SCALE_MAX = 11.090339630053647
SAFE = 64.0
NEG = -1.0e30
FLOOR = -1.0e20
K_PART = (0, 0, 0, 1, 1, 2)
Q_PART = (0, 1, 2, 0, 1, 0)
MROW = DK * len(K_PART)
KROWS = MROW + 3
RSQRT_MAGIC = 0x5F3759DF

WQ, WK, WV, WO, FR, FK, FV, BK, BV, BC = range(10)



def score_banks():
    banks = []
    for qc in range(NCH):
        for kb in range(TB * qc):
            for j in range(HG):
                banks.append([(qc, kb, j, 0, CH, 0)])
        d = TB * qc
        for j in range(HG):
            banks.append([(qc, d, j, 0, CH, 0)])
        for j in range(HG):
            banks.append([(qc, d + 1, j, P, 3 * P, 0), (qc, d + 3, j, 3 * P, P, 3 * P)])
        for j in range(0, HG, 2):
            banks.append([(qc, d + 2, j, 2 * P, 2 * P, 0), (qc, d + 2, j + 1, 2 * P, 2 * P, 2 * P)])
    return banks


GB = 3
BANKS = score_banks()
GROUPS = [BANKS[i:i + GB] for i in range(0, len(BANKS), GB)]
NG = len(GROUPS)
NP_BUF = 4
P_FREE_0 = 2 * NG
LAST_GROUP = [max(g for g, grp in enumerate(GROUPS) for bk in grp for u in bk if u[0] == qc) for qc in range(NCH)]


assert NG % 2 == 0 and 2 * NG % NP_BUF == 0

MAX_PIECES = []
for _qb in range(NT):
    _n = _qb // TB + 1
    MAX_PIECES.append((_qb, 0, min(_n, GB)))
    if _n > GB:
        MAX_PIECES.append((_qb, GB, _n - GB))
NMP = len(MAX_PIECES)

DVE_STEPS = 1024


def hybrid_kernel(nc, t, out):
    with ExitStack() as ctx:
        def sb(name, shape, dt=F32):
            return ctx.enter_context(nc.sbuf_tensor(name, shape, dt))

        def sem(name):
            return ctx.enter_context(nc.semaphore(name))

        part_d = {"A": nc.dram_tensor("part_a", (2, 3, D, S), BF16, kind="Internal").ap(),
                  "B": nc.dram_tensor("part_b", (1, 3, D, S), BF16, kind="Internal").ap()}
        rows_d = nc.dram_tensor("max_rows", (2, 3, HG * S), BF16, kind="Internal").ap()

        wT = sb("wT", [P, 10, KT, D])
        x_res = sb("x_res", [P, NT, D])
        xnT = sb("xnT", [P, KT, S + 4])
        v_all = sb("v_all", [P, NT, D])
        o_tok = sb("o_tok", [P, NT, D])
        stage = sb("stage", [P, 4, HG * S], BF16)
        v_st = sb("v_st", [P, 2, NT, HG, HS])
        probs = sb("probs", [P, NP_BUF, GB * CH])
        o_ev = sb("o_ev", [P, 2, CH])
        ident = sb("ident", [P, P])
        ident_b = sb("ident_b", [P, P], BF16)
        mask_qk = {a: sb(f"mask_qk_{a}", [P, P], BF16) for a in "AB"}
        mask_kq = {a: sb(f"mask_kq_{a}", [P, P], BF16) for a in "AB"}
        head_sel = sb("head_sel", [P, KT, H], BF16)
        sel_ch = sb("sel_ch", [H, D])
        ones_row = sb("ones_row", [1, P])
        head_col = sb("head_col", [H, 2])
        head_row = sb("head_row", [1, 3, H])
        scale_row = sb("scale_row", [P, 2, H])
        decay = sb("decay", [P, KT])
        v_coef = sb("v_coef", [P, KT])
        mu = sb("mu", [P, 2, KT])
        ln_st = sb("ln_st", [P, TB, 6])
        ln_mv = sb("ln_mv", [P, TB, 2])
        nw_v = sb("nw_v", [P, P])
        nw_y = sb("nw_y", [P, P])
        nw_u = sb("nw_u", [P, P])
        n_max = sb("n_max", [H, 2, NCH])
        n_top = sb("n_top", [H, 2])
        fl_prod = sb("fl_prod", [H, 1])
        fl_col = sb("fl_col", [H, 1])
        flags = {"A": sb("flags_a", [1, H], I32), "B": sb("flags_b", [1, H], I32)}
        den = sb("den", [P, TB, HG])
        rec = sb("rec", [P, TB, HG])
        pmax = sb("pmax", [P, 2, NT])
        row_max = sb("row_max", [P, NT])
        m_part = [sb(f"m_part{i}", [NT, P], BF16) for i in range(3)]
        m_rest = sb("m_rest", [NT, P])

        def f32_view(ap):
            return ap.bitcast(F32)

        low = f32_view(stage[:, 0:2, :].rearrange("p a n -> p (a n)"))
        high = f32_view(stage[:, 2:4, :].rearrange("p a n -> p (a n)"))

        def low_buf(i):
            return low[:, i * 1024:(i + 1) * 1024]

        xnt = [low_buf(i).rearrange("p (t d) -> p t d", t=TB) for i in range(2)]
        x_r = low_buf(2).rearrange("p (k n) -> p k n", k=KT)
        x_k = low_buf(3).rearrange("p (k n) -> p k n", k=KT)
        k_act = low_buf(4).rearrange("p (k n) -> p k n", k=KT)
        r_gate = low_buf(5).rearrange("p (t d) -> p t d", t=TB)
        x_diff = low_buf(6).rearrange("p (k n) -> p k n", k=KT)
        xn3T = low_buf(7).rearrange("p (k n) -> p k n", k=KT)
        sq_k, sq_v = low_buf(2), low_buf(3)
        kn_tok = low_buf(4).rearrange("p (t d) -> p t d", t=TB)
        v_mix = low_buf(5).rearrange("p (k n) -> p k n", k=KT)
        v_diff = low_buf(6).rearrange("p (k n) -> p k n", k=KT)
        kT = high[:, 0:KT * S].rearrange("p (k n) -> p k n", k=KT)
        vT = high[:, KT * S:2 * KT * S].rearrange("p (k n) -> p k n", k=KT)
        w_nat = high[:, 0:10 * 512].rearrange("p (w m d) -> p w m d", w=10, m=KT)

        pf = probs[:, :, :].rearrange("p a n -> p (a n)")
        parts = [pf[:, i * 768:(i + 1) * 768].bitcast(BF16).rearrange("p (r n) -> p r n", r=3) for i in range(4)]
        rest = [pf[:, 3072 + i * CH:3072 + (i + 1) * CH] for i in range(2)]
        oT = pf[:, 4096:5120].rearrange("p (k n) -> p k n", k=KT)
        sq_b = [pf[:, 5120 + i * 256:5376 + i * 256].bitcast(BF16) for i in range(4)]

        ps = ctx.enter_context(nc.psum_tensor("ps", [P, 8, CH], F32))

        def bank2(i):
            return ps[:, i:i + 2, :].rearrange("p a n -> p (a n)")

        def tok_bank(bk0, tb):
            return ps[:, bk0 + tb // 2, (tb % 2) * D:(tb % 2 + 1) * D]

        s_w = sem("weights_loaded")
        s_par = sem("params_loaded")
        s_rows_set = sem("max_rows_set")
        s_rows = sem("max_rows_stored")
        s_const = sem("constants_built")
        s_pool = sem("pool_step")
        s_wt_ps = sem("weight_transposed")
        s_wt = sem("weight_copied")
        s_hp_ps = sem("head_params_in_psum")
        s_hp = sem("head_params_step")
        s_setup = sem("setup_done")
        s_x = [sem(f"x_loaded{c}") for c in range(NCH)]
        s_dve = sem("vector_step")
        s_xnt = sem("ln_ready")
        s_T = sem("ln_transposed")
        s_xnT = sem("ln_channel_major")
        s_qk = sem("qk_in_psum")
        s_h = sem("qk_high_part")
        s_r1 = sem("qk_rest")
        s_ml = sem("qk_low_parts")
        s_parts = [sem(f"qk_stored{i}") for i in range(4)]
        s_v = sem("v_in_psum")
        s_vcopy = sem("v_copied")
        s_nrm = sem("norms_in_psum")
        s_nmax = sem("norm_max")
        s_flc = sem("flag_column")
        s_flr = sem("flag_row")
        s_fl = sem("flags_ready")
        s_oTp = sem("o_transposed")
        s_oTc = sem("o_channel_major")
        s_oproj = sem("o_projected")
        s_res = sem("attention_residual")
        s_diff = sem("shift_difference")
        s_xr = sem("x_r_ready")
        s_xk = sem("x_k_ready")
        s_rp = sem("r_in_psum")
        s_sig = sem("r_gate_ready")
        s_kp = sem("k_in_psum")
        s_relu = sem("k_relu")
        s_kact = sem("k_squared")
        s_fv = sem("ffn_in_psum")
        s_x2 = sem("ffn_residual")
        s_kb = sem("b_keys_in_psum")
        s_kraw = sem("b_keys_copied")
        s_vb = sem("b_values_in_psum")
        s_vraw = sem("b_values_copied")
        s_scan = sem("b_keys_decayed")
        s_vd = sem("b_value_difference")
        s_vm = sem("b_values_mixed")
        s_kt = sem("b_keys_token_major")
        s_vt = sem("b_values_token_major")
        s_sqk = sem("b_key_squares")
        s_sqv = sem("b_value_squares")
        s_kn = sem("b_keys_normed")
        s_vall = sem("b_values_normed")
        s_knT = sem("b_keys_channel_major")
        s_hB = sem("b_key_high_part")
        s_r1B = sem("b_key_rest")
        s_mlB = sem("b_key_low_parts")
        s_partsB = [sem(f"b_key_stored{i}") for i in range(2)]
        s_out = sem("out_stored")
        s_held = sem("wait_passed")
        att = {}
        for a in "AB":
            att[a] = {n: sem(f"{n}_{a}") for n in (
                "kq0", "kq1", "scores", "probs", "p_free", "vst",
                "o_ev", "o_T", "o_free", "o_step", "mx_scores", "mx_used", "mx_col", "mx_T", "mx_step", "mx_row",
                "mx_dma")}

        def held(eng):
            eng.sem_inc(s_held, 1)

        block = ctx.enter_context(nc.Block())

        @block.sync
        def _(sp):
            for i, name in enumerate(t["weights"]):
                sp.dma_start(w_nat[:, i], name.rearrange("(m p) d -> p m d", p=P)).then_inc(s_w, 16)
            sp.dma_start(mu[:, 0, :], t["mu_r"].rearrange("(k p) -> p k", p=P),
                         allow_slow_non_contiguous=True).then_inc(s_par, 16)
            sp.dma_start(mu[:, 1, :], t["mu_k"].rearrange("(k p) -> p k", p=P),
                         allow_slow_non_contiguous=True).then_inc(s_par, 16)
            col = "a h b c -> h (a b c)"
            row = "a h b c -> (a b c) h"
            sp.dma_start(head_col[:, 0:1], t["beta"].rearrange(col)).then_inc(s_par, 16)
            sp.dma_start(head_col[:, 1:2], t["v_coef"].rearrange(col)).then_inc(s_par, 16)
            sp.dma_start(head_row[:, 0, :], t["key_scale"].rearrange(row)).then_inc(s_par, 16)
            sp.dma_start(head_row[:, 1, :], t["val_scale"].rearrange(row)).then_inc(s_par, 16)
            sp.wait_ge(s_rows_set, 1)
            sp.dma_start(rows_d[0], stage[0:3, 0, :]).then_inc(s_rows, 16)
            sp.dma_start(rows_d[1], stage[0:3, 1, :]).then_inc(s_rows, 16)
            sp.wait_ge(s_rows, 32)

            def stage_loads(a, b, g):
                sm = att[a]
                d = part_d[a]
                for u in range(2):
                    inst = b * NHG + g * 2 + u
                    sp.wait_ge(sm["p_free"], (inst + 1) * NG)
                    for r in range(len(K_PART)):
                        for side, part in ((0, K_PART[r]), (1, Q_PART[r])):
                            src = d[(1 - side) if a == "A" else 0, part].rearrange(
                                "(q j e) n -> e q j n", j=HG, e=DK)[:, bass.ds(g * 2 + u, 1)]
                            dst = stage[r * DK:(r + 1) * DK, 2 * u + side, :].rearrange(
                                "e (q j n) -> e q j n", q=1, j=HG)
                            sp.dma_start(dst, src).then_inc(sm[f"kq{u}"], 16)
                    for side in range(2):
                        sp.dma_start(stage[MROW:KROWS, 2 * u + side, :], rows_d[side]).then_inc(sm[f"kq{u}"], 16)

            x_d = t["X"].rearrange("b (c t p) d -> b c p t d", p=P, t=TB)
            out_d = out.rearrange("b (c t p) d -> b c p t d", p=P, t=TB)
            with sp.Fori(0, B) as b:
                for c in range(NCH):
                    sp.dma_start(x_res[:, TB * c:TB * (c + 1), :],
                                 x_d[bass.ds(b, 1), c].rearrange("o p t d -> (o p) t d")).then_inc(s_x[c], 16)
                for c in range(NCH):
                    for i in range(4):
                        sp.wait_ge(s_ml, (b * NCH + c) * 8 + 2 * i + 2)
                        sp.dma_start(part_d["A"][i // 2, :, (i % 2) * P:(i % 2 + 1) * P, c * CH:(c + 1) * CH]
                                     .rearrange("r p n -> p r n"), parts[i]).then_inc(s_parts[i], 16)
                for i in range(4):
                    sp.wait_ge(s_parts[i], (b + 1) * 16 * NCH)
                held(sp)
                with sp.Fori(0, NHG // 2) as g:
                    stage_loads("A", b, g)
                for c in range(NCH):
                    for i in range(2):
                        sp.wait_ge(s_mlB, (b * NCH + c) * 4 + 2 * i + 2)
                        sp.dma_start(part_d["B"][0, :, i * P:(i + 1) * P, c * CH:(c + 1) * CH]
                                     .rearrange("r p n -> p r n"), parts[i]).then_inc(s_partsB[i], 16)
                for i in range(2):
                    sp.wait_ge(s_partsB[i], (b + 1) * 16 * NCH)
                    held(sp)
                sp.wait_ge(s_vall, (b + 1) * NCH)
                held(sp)
                with sp.Fori(0, NHG // 2) as g:
                    stage_loads("B", b, g)
                for c in range(NCH):
                    sp.wait_ge(s_x2, b * 2 * NCH + NCH + c + 1)
                    sp.dma_start(out_d[bass.ds(b, 1), c].rearrange("o p t d -> (o p) t d"),
                                 x_res[:, TB * c:TB * (c + 1), :]).then_inc(s_out, 16)
                sp.wait_ge(s_out, (b + 1) * 16 * NCH)
                held(sp)

        @block.gpsimd
        def _(pool):
            steps = [0]

            def step(ins):
                steps[0] += 1
                ins.then_inc(s_pool, 1)

            def settle():
                pool.wait_ge(s_pool, steps[0])

            step(pool.memset(stage[0:3, 0, :], 1.0))
            step(pool.memset(stage[0:3, 1, :], 0.0))
            settle()
            pool.sem_inc(s_rows_set, 1)
            step(pool.memset(ident[:, :], 0.0))
            for m in (mask_qk, mask_kq):
                for a in "AB":
                    step(pool.memset(m[a][:, :], 0.0))
            step(pool.memset(head_sel[:, :, :], 1.0))
            step(pool.memset(sel_ch[:, :], 1.0))
            step(pool.memset(ones_row[:, :], 1.0))
            step(pool.memset(xnT[:, :, 0:1], 0.0))
            step(pool.memset(pmax[:, :, :], FLOOR))
            step(pool.memset(v_st[:, :, :, :, :].rearrange("p u t j e -> p (u t j) e"), 0.0))
            settle()
            step(pool.affine_select(out=ident[:, :], in_=ident[:, :], compare_op=ALU.not_equal, fill=1.0, base=0,
                                    pattern=[[-1, P]], channel_multiplier=1))
            for m, sign in ((mask_qk, 1), (mask_kq, -1)):
                for a, op in (("A", ALU.is_ge), ("B", ALU.is_gt)):
                    step(pool.affine_select(out=m[a][:, :], in_=m[a][:, :], compare_op=op, fill=NEG, base=0,
                                            pattern=[[-sign, P]], channel_multiplier=sign))
            step(pool.memset(v_st[:, :, :, :, DK:DK + 1].rearrange("p u t j e -> p (u t j) e"), 1.0))
            step(pool.affine_select(out=head_sel[:, :, :], in_=head_sel[:, :, :], compare_op=ALU.is_ge, fill=0.0,
                                    base=0, pattern=[[P, KT], [-DK, H]], channel_multiplier=1))
            step(pool.affine_select(out=sel_ch[:, :], in_=sel_ch[:, :], compare_op=ALU.is_ge, fill=0.0, base=0,
                                    pattern=[[1, D]], channel_multiplier=-DK))
            settle()
            step(pool.affine_select(out=head_sel[:, :, :], in_=head_sel[:, :, :], compare_op=ALU.is_ge, fill=0.0,
                                    base=DK - 1, pattern=[[-P, KT], [DK, H]], channel_multiplier=-1))
            step(pool.affine_select(out=sel_ch[:, :], in_=sel_ch[:, :], compare_op=ALU.is_ge, fill=0.0,
                                    base=DK - 1, pattern=[[-1, D]], channel_multiplier=DK))
            step(pool.tensor_copy(ident_b[:, :], ident[:, :]))
            settle()
            pool.sem_inc(s_const, 1)

            def low_parts(done, rest_ready, base, i):
                pool.wait_ge(rest_ready, base + i + 1)
                held(pool)
                pool.tensor_copy(parts[i][:, 1, :], rest[i % 2]).then_inc(done, 1)
                pool.wait_ge(done, 2 * (base + i) + 1)
                pool.tensor_tensor(parts[i][:, 2, :], rest[i % 2], parts[i][:, 1, :],
                                   ALU.subtract).then_inc(done, 1)

            def attend(a, b, g):
                sm = att[a]
                for u in range(2):
                    inst = b * NHG + g * 2 + u
                    pool.wait_ge(sm["p_free"], (inst + 1) * NG)
                    held(pool)
                    pool.tensor_copy(
                        v_st[:, u, :, :, 0:DK],
                        v_all[:, :, bass.ds((g * 2 + u) * HG * DK, HG * DK)]
                        .rearrange("p t (j e) -> p t j e", j=HG)).then_inc(sm["vst"], 1)

            def mix(b, p):
                for c in range(NCH):
                    f = b * 2 * NCH + p * NCH + c
                    ln = b * 4 * NCH + (NCH + 2 * c if p == 0 else 3 * NCH + c)
                    pool.wait_ge(s_xnT, ln + 1)
                    now, before = xnT[:, :, c * CH + 1:c * CH + 1 + CH], xnT[:, :, c * CH:c * CH + CH]
                    if c >= 1:
                        pool.wait_ge(s_xr, f)
                    pool.tensor_tensor(x_diff, now, before, ALU.subtract).then_inc(s_diff, 1)
                    pool.wait_ge(s_relu, f + 1)
                    pool.tensor_tensor(k_act, k_act, k_act, ALU.mult).then_inc(s_kact, 1)

            with pool.Fori(0, B) as b:
                for c in range(NCH):
                    for i in range(4):
                        low_parts(s_ml, s_r1, (b * NCH + c) * 4, i)
                pool.wait_ge(s_vcopy, (b + 1) * NCH)
                held(pool)
                with pool.Fori(0, NHG // 2) as g:
                    attend("A", b, g)
                mix(b, 0)
                for c in range(NCH):
                    e = b * NCH + c
                    pool.wait_ge(s_vraw, b * NCH + min(c + 2, NCH))
                    held(pool)
                    if c == 0:
                        pool.wait_ge(s_xr, b * 2 * NCH + NCH)
                        held(pool)
                    else:
                        pool.wait_ge(s_vm, e)
                        held(pool)
                    n = CH if c + 1 < NCH else CH - 1
                    if c + 1 == NCH:
                        pool.tensor_copy(v_diff[:, :, n:CH], vT[:, :, S - 1:S])
                    pool.tensor_tensor(v_diff[:, :, 0:n], vT[:, :, c * CH:c * CH + n],
                                       vT[:, :, c * CH + 1:c * CH + 1 + n], ALU.subtract).then_inc(s_vd, 1)
                    for i in range(2):
                        low_parts(s_mlB, s_r1B, e * 2, i)
                pool.wait_ge(s_vall, (b + 1) * NCH)
                held(pool)
                with pool.Fori(0, NHG // 2) as g:
                    attend("B", b, g)
                mix(b, 1)

        @block.scalar
        def _(act):
            for i in range(10):
                act.wait_ge(s_wt_ps, i + 1)
                nc.scalar.copy(wT[:, i].rearrange("p k n -> p (k n)"), ps[:, i % 8, :]).then_inc(s_wt, 1)
            act.wait_ge(s_par, 6 * 16)
            nc.scalar.activation(head_col[:, 0:1], head_col[:, 0:1], ACT.Abs).then_inc(s_hp, 1)
            act.wait_ge(s_hp, 2)
            nc.scalar.activation(head_col[:, 0:1], head_col[:, 0:1], ACT.Exp, scale=-EXP_SCALING).then_inc(s_hp, 1)
            nc.scalar.activation(head_row[:, 0:2, :], head_row[:, 0:2, :], ACT.Exp,
                                 scale=EXP_SCALING).then_inc(s_hp, 1)

            def channel_major(dst, pair, ready, want, done):
                act.wait_ge(ready, want)
                nc.scalar.copy(dst, ps[:, pair:pair + 2, :]).then_inc(done, 1)

            def ln_copy(ln, pair, dst):
                channel_major(dst, pair, s_T, ln + 1, s_xnT)

            def attend(a, b, g):
                sm = att[a]
                for u in range(2):
                    inst = b * NHG + g * 2 + u
                    for j in range(HG):
                        n = inst * HG + j
                        flag = act.value_load(flags[a][0:1, bass.ds((g * 2 + u) * HG + j, 1)])
                        with act.If(flag > 0):
                            act.wait_ge(sm["mx_row"], n + 1)
                            for r in range(3):
                                act.dma_start(stage[MROW + r:MROW + r + 1, 2 * u + 1, j * S:(j + 1) * S]
                                              .rearrange("o (t q) -> o t q", t=NT),
                                              m_part[r][:, :]).then_inc(sm["mx_dma"], 16)
                        with act.Else():
                            act.sem_inc(sm["mx_dma"], 48)
                    for gi, grp in enumerate(GROUPS):
                        act.wait_ge(sm["scores"], inst * NG + gi + 1)
                        act.wait_ge(sm["p_free"], P_FREE_0 + inst * NG + gi + 1 - NP_BUF)
                        w = len(grp) * CH
                        nc.scalar.activation(
                            probs[:, (u * NG + gi) % NP_BUF, 0:w],
                            ps[:, GB * (gi % 2):GB * (gi % 2) + len(grp), :].rearrange("p a n -> p (a n)"),
                            ACT.Exp, scale=SCALE[a]).then_inc(sm["probs"], 1)

            def mix(b, p):
                for c in range(NCH):
                    f = b * 2 * NCH + p * NCH + c
                    ln = b * 4 * NCH + (NCH + 2 * c if p == 0 else 3 * NCH + c)
                    channel_major(oT, 0, s_oTp, f + 1, s_oTc)
                    ln_copy(ln, 4, xnT[:, :, c * CH + 1:c * CH + 1 + CH])
                    act.wait_ge(s_kp, f + 1)
                    nc.scalar.activation(k_act, ps[:, 0:2, :], ACT.Relu).then_inc(s_relu, 1)
                    act.wait_ge(s_rp, f + 1)
                    nc.scalar.activation(r_gate.rearrange("p t d -> p (t d)"), bank2(6),
                                         ACT.Sigmoid).then_inc(s_sig, 1)
                    if p == 0:
                        ln_copy(ln + 1, 4, xn3T)
                        channel_major(kT[:, :, c * CH:(c + 1) * CH], 6, s_kb, b * NCH + c + 1, s_kraw)
                        channel_major(vT[:, :, c * CH:(c + 1) * CH], 0, s_vb, b * NCH + c + 1, s_vraw)

            with act.Fori(0, B) as b:
                for c in range(NCH):
                    e = b * NCH + c
                    ln_copy(b * 4 * NCH + c, 0, xnT[:, :, c * CH + 1:c * CH + 1 + CH])
                    if c >= 1:
                        act.wait_ge(s_nrm, e)
                    for i in range(4):
                        act.wait_ge(s_qk, e * 4 + i + 1)
                        if c >= 1:
                            act.wait_ge(s_parts[i], e * 16)
                        nc.scalar.copy(parts[i][:, 0, :], ps[:, 2 + i, :])
                        nc.scalar.activation(sq_b[i], ps[:, 2 + i, :], ACT.Square).then_inc(s_h, 1)
                    act.wait_ge(s_v, e + 1)
                    nc.scalar.copy(v_all[:, TB * c:TB * (c + 1), :].rearrange("p t d -> p (t d)"),
                                   bank2(6)).then_inc(s_vcopy, 1)
                act.wait_ge(s_fl, b + 1)
                held(act)
                with act.Fori(0, NHG // 2) as g:
                    attend("A", b, g)
                mix(b, 0)
                for c in range(NCH):
                    e = b * NCH + c
                    act.wait_ge(s_kt, e + 1)
                    nc.scalar.activation(sq_k, bank2(0), ACT.Square).then_inc(s_sqk, 1)
                    act.wait_ge(s_vt, e + 1)
                    nc.scalar.activation(sq_v, bank2(2), ACT.Square).then_inc(s_sqv, 1)
                    for i in range(2):
                        act.wait_ge(s_knT, e * 2 + i + 1)
                        if c >= 1:
                            act.wait_ge(s_partsB[i], e * 16)
                        nc.scalar.copy(parts[i][:, 0, :], ps[:, 4 + i, :]).then_inc(s_hB, 1)
                with act.Fori(0, NHG // 2) as g:
                    attend("B", b, g)
                mix(b, 1)

        @block.tensor
        def _(pe):
            for a in "AB":
                pe.sem_inc(att[a]["p_free"], P_FREE_0)
            pe.wait_ge(s_const, 1)
            pe.wait_ge(s_w, 160)
            for i in range(10):
                if i >= 8:
                    pe.wait_ge(s_wt, i - 7)
                for kt in range(KT):
                    for m in range(KT):
                        last = pe.transpose(ps[:, i % 8, kt * D + m * P:kt * D + (m + 1) * P],
                                            w_nat[:, i, m, kt * P:(kt + 1) * P], ident[:, :])
                last.then_inc(s_wt_ps, 1)
            pe.wait_ge(s_wt, 10)
            pe.wait_ge(s_hp, 4)
            for kt in range(KT):
                pe.matmul(ps[:, 0, 2 * kt:2 * kt + 2], sel_ch[:, kt * P:(kt + 1) * P], head_col[:, :],
                          start=True, stop=True)
            pe.matmul(ps[:, 1, 0:2 * H], ones_row[:, :], head_row[:, 0:2, :].rearrange("o k h -> o (k h)"),
                      start=True, stop=True).then_inc(s_hp_ps, 1)
            pe.wait_ge(s_setup, 1)

            def to_channels(bk, src):
                for kt in range(KT):
                    for tb in range(TB):
                        last = pe.transpose(ps[:, bk + kt, tb * P:(tb + 1) * P], src[:, tb, kt * P:(kt + 1) * P],
                                            ident[:, :])
                return last

            def to_tokens(bk, src):
                for tb in range(TB):
                    for kt in range(KT):
                        last = pe.transpose(tok_bank(bk, tb)[:, kt * P:(kt + 1) * P],
                                            src[:, kt, tb * P:(tb + 1) * P], ident[:, :])
                return last

            def project_channels(bk, w, m, src):
                for kt in range(KT):
                    last = pe.matmul(ps[:, bk, :], wT[:, w, kt, m * P:(m + 1) * P], src[:, kt, :],
                                     start=(kt == 0), stop=(kt == KT - 1))
                return last

            def project_tokens(bk, w, src):
                for tb in range(TB):
                    for kt in range(KT):
                        last = pe.matmul(tok_bank(bk, tb), src[:, kt, tb * P:(tb + 1) * P], wT[:, w, kt, :],
                                         start=(kt == 0), stop=(kt == KT - 1))
                return last

            def row_maxima(a, u, j, n):
                sm = att[a]
                kk, qq = (stage[0:KROWS, 2 * u + s, j * S:(j + 1) * S] for s in range(2))
                for i, (qb, b0, nb) in enumerate(MAX_PIECES):
                    if i >= 2:
                        pe.wait_ge(sm["mx_used"], n * NMP + i - 1)
                    for bk in range(b0, b0 + nb):
                        o = ps[:, GB * (i % 2) + bk - b0, :]
                        w = min(CH, (qb + 1) * P - bk * CH)
                        diag = (bk == qb // TB)
                        last = pe.matmul(o[:, 0:w], qq[:, qb * P:(qb + 1) * P], kk[:, bk * CH:bk * CH + w],
                                         start=True, stop=True)
                        if diag:
                            last = pe.matmul(o[:, w - P:w], ident_b[:, :], mask_qk[a][:, :], start=False, stop=True,
                                             skip_group_check=True)
                    last.then_inc(sm["mx_scores"], 1)
                pe.wait_ge(sm["mx_col"], n + 1)
                pe.transpose(ps[0:NT, 6, 0:P], row_max[:, :], ident[:, :]).then_inc(sm["mx_T"], 1)
                pe.wait_ge(sm["mx_dma"], (n + 1) * 48)

            def attend(a, b, g):
                sm = att[a]
                for u in range(2):
                    inst = b * NHG + g * 2 + u
                    pe.wait_ge(sm[f"kq{u}"], (b * (NHG // 2) + g + 1) * 16 * 14)
                    for j in range(HG):
                        n = inst * HG + j
                        flag = pe.value_load(flags[a][0:1, bass.ds((g * 2 + u) * HG + j, 1)])
                        with pe.If(flag > 0):
                            row_maxima(a, u, j, n)
                        with pe.Else():
                            pe.sem_inc(sm["mx_scores"], NMP)
                            pe.sem_inc(sm["mx_T"], 1)
                    kk = stage[0:KROWS, 2 * u, :].rearrange("r (j n) -> r j n", j=HG)
                    qq = stage[0:KROWS, 2 * u + 1, :].rearrange("r (j n) -> r j n", j=HG)

                    def scores(gi):
                        if gi >= 2:
                            pe.wait_ge(sm["probs"], inst * NG + gi - 1)
                        for n, bk in enumerate(GROUPS[gi]):
                            for qc, kb, j, q0, w, col in bk:
                                o = ps[:, GB * (gi % 2) + n, col:col + w]
                                last = pe.matmul(o, kk[:, j, kb * P:(kb + 1) * P],
                                                 qq[:, j, qc * CH + q0:qc * CH + q0 + w], start=True, stop=True)
                                if kb >= TB * qc:
                                    last = pe.matmul(o[:, 0:P], ident_b[:, :], mask_kq[a][:, :], start=False,
                                                     stop=True, skip_group_check=True)
                        last.then_inc(sm["scores"], 1)

                    def products(gi):
                        pe.wait_ge(sm["probs"], inst * NG + gi + 1)
                        slot = (u * NG + gi) % NP_BUF
                        for n, bk in enumerate(GROUPS[gi]):
                            for qc, kb, j, q0, w, col in bk:
                                if kb == 0 and j == 0:
                                    pe.wait_ge(sm["o_free"], inst * NCH + qc + 1)
                                last = pe.matmul(ps[HS * j:HS * (j + 1), 6 + qc % 2, q0:q0 + w],
                                                 v_st[:, u, kb, j, :], probs[:, slot, n * CH + col:n * CH + col + w],
                                                 start=(kb == 0), stop=(kb >= TB * qc), skip_group_check=True)
                        last.then_inc(sm["p_free"], 1)

                    def turn(qc):
                        pe.wait_ge(sm["o_ev"], inst * NCH + qc + 1)
                        for tb in range(TB):
                            last = pe.transpose(ps[:, 6 + qc % 2, tb * P:(tb + 1) * P],
                                                o_ev[:, qc % 2, tb * P:(tb + 1) * P], ident[:, :])
                        last.then_inc(sm["o_T"], 1)

                    scores(0)
                    scores(1)
                    pe.wait_ge(sm["vst"], inst + 1)
                    for gi in range(NG):
                        products_first = gi + 2 >= NG
                        if not products_first:
                            scores(gi + 2)
                        products(gi)
                        for qc in range(NCH):
                            if gi == min(LAST_GROUP[qc] + 2, NG - 1):
                                turn(qc)

            def mix(b, p):
                for c in range(NCH):
                    f = b * 2 * NCH + p * NCH + c
                    ln = b * 4 * NCH + (NCH + 2 * c if p == 0 else 3 * NCH + c)
                    xc = xnT[:, :, c * CH + 1:c * CH + 1 + CH]
                    if c == 0:
                        pe.wait_ge(att["AB"[p]]["o_free"], (b + 1) * NHG * NCH + 2)
                    elif p == 0:
                        pe.wait_ge(s_vraw, b * NCH + c)
                    to_channels(0, o_tok[:, TB * c:TB * (c + 1), :]).then_inc(s_oTp, 1)
                    pe.wait_ge(s_oTc, f + 1)
                    if c >= 1:
                        pe.wait_ge(s_x2, f)
                    project_tokens(2, WO if p == 0 else BC, oT).then_inc(s_oproj, 1)
                    pe.wait_ge(s_xnt, ln + 1)
                    to_channels(4, xnt[(c if p else 2 * c) % 2]).then_inc(s_T, 1)
                    pe.wait_ge(s_xk, f + 1)
                    project_channels(0, FK, 0, x_k)
                    project_channels(1, FK, 1, x_k).then_inc(s_kp, 1)
                    pe.wait_ge(s_xr, f + 1)
                    if c >= 1:
                        if p == 0:
                            pe.wait_ge(s_kraw, b * NCH + c)
                        else:
                            pe.wait_ge(s_sig, f)
                    project_tokens(6, FR, x_r).then_inc(s_rp, 1)
                    pe.wait_ge(s_kact, f + 1)
                    pe.wait_ge(s_res, f + 1)
                    project_tokens(2, FV, k_act).then_inc(s_fv, 1)
                    if p == 0:
                        pe.wait_ge(s_xnt, ln + 2)
                        to_channels(4, xnt[1]).then_inc(s_T, 1)
                        pe.wait_ge(s_xnT, ln + 2)
                        pe.wait_ge(s_sig, f + 1)
                        project_channels(6, BK, 0, xn3T)
                        project_channels(7, BK, 1, xn3T).then_inc(s_kb, 1)
                        project_channels(0, BV, 0, xn3T)
                        project_channels(1, BV, 1, xn3T).then_inc(s_vb, 1)

            with pe.Fori(0, B) as b:
                for c in range(NCH):
                    e = b * NCH + c
                    ln = b * 4 * NCH + c
                    xc = xnT[:, :, c * CH + 1:c * CH + 1 + CH]
                    pe.wait_ge(s_xnt, ln + 1)
                    if c >= 1:
                        pe.wait_ge(s_nmax, e)
                    to_channels(0, xnt[c % 2]).then_inc(s_T, 1)
                    pe.wait_ge(s_xnT, ln + 1)
                    for i in range(4):
                        if c >= 1:
                            pe.wait_ge(s_r1, (e - 1) * 4 + i + 1)
                        project_channels(2 + i, WQ + i // 2, i % 2, xc).then_inc(s_qk, 1)
                    if c >= 1:
                        pe.wait_ge(s_vcopy, e)
                    project_tokens(6, WV, xc).then_inc(s_v, 1)
                    pe.wait_ge(s_h, e * 4 + 4)
                    for side in range(2):
                        for kt in range(KT):
                            last = pe.matmul(ps[0:H, side, :], head_sel[:, kt, :], sq_b[side * 2 + kt],
                                             start=(kt == 0), stop=(kt == KT - 1))
                    last.then_inc(s_nrm, 1)
                pe.wait_ge(s_flc, b + 1)
                held(pe)
                pe.matmul(ps[0:1, 0, 0:H], fl_col[:, :], ident[0:H, 0:H], start=True, stop=True).then_inc(s_flr, 1)
                pe.wait_ge(s_fl, b + 1)
                held(pe)
                with pe.Fori(0, NHG // 2) as g:
                    attend("A", b, g)
                mix(b, 0)
                for c in range(NCH):
                    e = b * NCH + c
                    cols = slice(c * CH, (c + 1) * CH)
                    pe.wait_ge(s_scan, e + 1)
                    if c == 0:
                        pe.wait_ge(s_vraw, (b + 1) * NCH)
                        pe.wait_ge(s_x2, b * 2 * NCH + NCH)
                    else:
                        pe.wait_ge(s_kn, e)
                    to_tokens(0, kT[:, :, cols]).then_inc(s_kt, 1)
                    pe.wait_ge(s_vm, e + 1)
                    if c >= 1:
                        pe.wait_ge(s_vall, e)
                    to_tokens(2, v_mix).then_inc(s_vt, 1)
                    pe.wait_ge(s_kn, e + 1)
                    for kt in range(KT):
                        if c >= 1:
                            pe.wait_ge(s_r1B, (e - 1) * 2 + kt + 1)
                        for tb in range(TB):
                            last = pe.transpose(ps[:, 4 + kt, tb * P:(tb + 1) * P],
                                                kn_tok[:, tb, kt * P:(kt + 1) * P], ident[:, :])
                        last.then_inc(s_knT, 1)
                with pe.Fori(0, NHG // 2) as g:
                    attend("B", b, g)
                mix(b, 1)

        @block.vector
        def _(dve):
            for a in "AB":
                dve.sem_inc(att[a]["o_free"], 2)
            dve.wait_ge(s_par, 6 * 16)
            nc.vector.tensor_scalar(head_row[:, 0, :], head_row[:, 0, :], KEY_SCALE_MAX / EXP_SCALING, None,
                                    ALU.min).then_inc(s_hp, 1)
            dve.wait_ge(s_hp, 4)
            nc.vector.tensor_tensor(head_row[:, 2, :], head_row[:, 0, :], head_row[:, 0, :],
                                    ALU.mult).then_inc(s_hp, 1)
            dve.wait_ge(s_hp, 5)
            nc.vector.tensor_scalar(flags["B"][:, :], head_row[:, 2, :], SAFE, None, ALU.is_gt)
            dve.wait_ge(s_hp_ps, 1)
            for kt in range(KT):
                nc.vector.tensor_copy(decay[:, kt:kt + 1], ps[:, 0, 2 * kt:2 * kt + 1])
                nc.vector.tensor_copy(v_coef[:, kt:kt + 1], ps[:, 0, 2 * kt + 1:2 * kt + 2])
            nc.vector.tensor_copy(scale_row[:, :, :].rearrange("p k h -> p (k h)"),
                                  ps[:, 1, 0:2 * H]).then_inc(s_setup, 1)
            dve.wait_ge(s_setup, 1)

            with dve.Fori(0, B) as b:
                steps = [0]

                def step(ins):
                    steps[0] += 1
                    ins.then_inc(s_dve, 1)

                def settle():
                    dve.wait_ge(s_dve, b * DVE_STEPS + steps[0])

                def rsqrt(n):
                    v, y, w = nw_v[:, 0:n], nw_y[:, 0:n], nw_u[:, 0:n]
                    step(nc.vector.tensor_scalar(y.bitcast(I32), v.bitcast(I32), 1, None, ALU.arith_shift_right))
                    settle()
                    step(nc.vector.tensor_scalar(y.bitcast(I32), y.bitcast(I32), -1.0, float(RSQRT_MAGIC), ALU.mult,
                                                 ALU.add))
                    settle()
                    for _ in range(3):
                        step(nc.vector.tensor_tensor(w, y, y, ALU.mult))
                        settle()
                        step(nc.vector.scalar_tensor_tensor(w, w, -0.5, v, ALU.mult, ALU.mult))
                        settle()
                        step(nc.vector.scalar_tensor_tensor(y, w, 1.5, y, ALU.add, ALU.mult))
                        settle()

                def layernorm(c, k):
                    for tb in range(TB):
                        step(nc.vector.bn_stats(ln_st[:, tb, :], x_res[:, TB * c + tb, :]))
                    settle()
                    held(dve)
                    for tb in range(TB):
                        step(nc.vector.bn_aggr(ln_mv[:, tb, :], ln_st[:, tb, :]))
                    settle()
                    step(nc.vector.tensor_scalar(nw_v[:, 0:TB], ln_mv[:, :, 1], EPS, None, ALU.add))
                    settle()
                    rsqrt(TB)
                    if k >= 2:
                        dve.wait_ge(s_T, b * 4 * NCH + k - 1)
                    for tb in range(TB):
                        last = nc.vector.tensor_scalar(xnt[k % 2][:, tb, :], x_res[:, TB * c + tb, :],
                                                       ln_mv[:, tb, 0:1], nw_y[:, tb:tb + 1], ALU.subtract, ALU.mult)
                    last.then_inc(s_xnt, 1)
                    dve.wait_ge(s_xnt, b * 4 * NCH + k + 1)

                def split_rest(bk, high_ready, base, i, done, low_done):
                    dve.wait_ge(high_ready, base + i + 1)
                    if i >= 2:
                        dve.wait_ge(low_done, 2 * (base + i) - 2)
                    nc.vector.tensor_tensor(rest[i % 2], ps[:, bk, :], parts[i][:, 0, :],
                                            ALU.subtract).then_inc(done, 1)

                def row_maxima(a, n):
                    sm = att[a]
                    for i, (qb, b0, nb) in enumerate(MAX_PIECES):
                        dve.wait_ge(sm["mx_scores"], n * NMP + i + 1)
                        w = min((b0 + nb) * CH, (qb + 1) * P) - b0 * CH
                        src = ps[:, GB * (i % 2):GB * (i % 2) + nb, :].rearrange("p a n -> p (a n)")[:, 0:w]
                        nc.vector.tensor_reduce(pmax[:, 1 if b0 else 0, qb:qb + 1], src, AX_X,
                                                ALU.max).then_inc(sm["mx_used"], 1)
                    dve.wait_ge(sm["mx_used"], (n + 1) * NMP)
                    nc.vector.tensor_tensor(row_max[:, :], pmax[:, 0, :], pmax[:, 1, :],
                                            ALU.max).then_inc(sm["mx_col"], 1)
                    dve.wait_ge(sm["mx_T"], n + 1)
                    mt = ps[0:NT, 6, 0:P]
                    nc.vector.tensor_scalar(m_part[0][:, :], mt, -1.0, None, ALU.mult).then_inc(sm["mx_step"], 1)
                    dve.wait_ge(sm["mx_step"], n * 3 + 1)
                    nc.vector.scalar_tensor_tensor(m_rest[:, :], mt, -1.0, m_part[0][:, :], ALU.mult,
                                                   ALU.subtract).then_inc(sm["mx_step"], 1)
                    dve.wait_ge(sm["mx_step"], n * 3 + 2)
                    nc.vector.tensor_copy(m_part[1][:, :], m_rest[:, :]).then_inc(sm["mx_step"], 1)
                    dve.wait_ge(sm["mx_step"], n * 3 + 3)
                    nc.vector.tensor_tensor(m_part[2][:, :], m_rest[:, :], m_part[1][:, :],
                                            ALU.subtract).then_inc(sm["mx_row"], 1)

                def attend(a, g):
                    sm = att[a]
                    for u in range(2):
                        inst = b * NHG + g * 2 + u
                        for j in range(HG):
                            n = inst * HG + j
                            flag = dve.value_load(flags[a][0:1, bass.ds((g * 2 + u) * HG + j, 1)])
                            with dve.If(flag > 0):
                                row_maxima(a, n)
                            with dve.Else():
                                dve.sem_inc(sm["mx_used"], NMP)
                                dve.sem_inc(sm["mx_col"], 1)
                                dve.sem_inc(sm["mx_step"], 3)
                                dve.sem_inc(sm["mx_row"], 1)
                        for qc in range(NCH):
                            k = inst * NCH + qc
                            dve.wait_ge(sm["p_free"], P_FREE_0 + inst * NG + LAST_GROUP[qc] + 1)
                            nc.vector.tensor_copy(o_ev[:, qc % 2, :], ps[:, 6 + qc % 2, :]).then_inc(sm["o_ev"], 1)
                            dve.wait_ge(sm["o_T"], k + 1)
                            o = ps[:, 6 + qc % 2, :].rearrange("p (t j e) -> p t j e", t=TB, j=HG)
                            nc.vector.tensor_scalar(den[:, :, :], o[:, :, :, DK], 1.0e-37, None,
                                                    ALU.max).then_inc(sm["o_step"], 1)
                            dve.wait_ge(sm["o_step"], k * 2 + 1)
                            nc.vector.reciprocal(rec[:, :, :], den[:, :, :]).then_inc(sm["o_step"], 1)
                            dve.wait_ge(sm["o_step"], k * 2 + 2)
                            dst = o_tok[:, TB * qc:TB * (qc + 1), bass.ds((g * 2 + u) * HG * DK, HG * DK)]
                            nc.vector.tensor_tensor(
                                dst.rearrange("p t (j e) -> p t j e", j=HG), o[:, :, :, 0:DK],
                                rec[:, :, :].unsqueeze(3).to_broadcast([P, TB, HG, DK]),
                                ALU.mult).then_inc(sm["o_free"], 1)

                def mix(p):
                    for c in range(NCH):
                        f = b * 2 * NCH + p * NCH + c
                        k = NCH + 2 * c if p == 0 else 3 * NCH + c
                        res = x_res[:, TB * c:TB * (c + 1), :].rearrange("p t d -> p (t d)")
                        dve.wait_ge(s_oproj, f + 1)
                        nc.vector.tensor_tensor(res, res, bank2(2), ALU.add).then_inc(s_res, 1)
                        dve.wait_ge(s_res, f + 1)
                        layernorm(c, k)
                        dve.wait_ge(s_diff, f + 1)
                        before = xnT[:, :, c * CH:c * CH + CH]
                        if c >= 1:
                            dve.wait_ge(s_rp, f)
                        for kt in range(KT):
                            last = nc.vector.scalar_tensor_tensor(x_k[:, kt, :], x_diff[:, kt, :], mu[:, 1, kt:kt + 1],
                                                                  before[:, kt, :], ALU.mult, ALU.add)
                        last.then_inc(s_xk, 1)
                        for kt in range(KT):
                            last = nc.vector.scalar_tensor_tensor(x_r[:, kt, :], x_diff[:, kt, :], mu[:, 0, kt:kt + 1],
                                                                  before[:, kt, :], ALU.mult, ALU.add)
                        last.then_inc(s_xr, 1)
                        dve.wait_ge(s_fv, f + 1)
                        dve.wait_ge(s_sig, f + 1)
                        gate = r_gate.rearrange("p t d -> p (t d)")
                        step(nc.vector.tensor_tensor(gate, gate, bank2(2), ALU.mult))
                        settle()
                        nc.vector.tensor_tensor(res, res, gate, ALU.add).then_inc(s_x2, 1)
                        dve.wait_ge(s_x2, f + 1)
                        if p == 0:
                            layernorm(c, k + 1)

                for c in range(2):
                    dve.wait_ge(s_x[c], (b + 1) * 16)
                    layernorm(c, c)
                for c in range(NCH):
                    e = b * NCH + c
                    for i in range(4):
                        if i < 2 and c >= 1:
                            dve.wait_ge(s_ml, 8 * e + 2 * i - 2)
                        split_rest(2 + i, s_h, e * 4, i, s_r1, s_ml)
                    dve.wait_ge(s_nrm, e + 1)
                    nc.vector.tensor_reduce(n_max[:, :, c:c + 1], ps[0:H, 0:2, :], AX_X, ALU.max).then_inc(s_nmax, 1)
                    if c + 2 < NCH:
                        dve.wait_ge(s_x[c + 2], (b + 1) * 16)
                        layernorm(c + 2, c + 2)
                dve.wait_ge(s_nmax, (b + 1) * NCH)
                step(nc.vector.tensor_reduce(n_top[:, :], n_max[:, :, :], AX_X, ALU.max))
                settle()
                step(nc.vector.tensor_tensor(fl_prod[:, :], n_top[:, 0:1], n_top[:, 1:2], ALU.mult))
                settle()
                nc.vector.tensor_scalar(fl_col[:, :], fl_prod[:, :], 1.1 * SCALE["A"] ** 2, SAFE * SAFE, ALU.mult,
                                        ALU.is_gt).then_inc(s_flc, 1)
                dve.wait_ge(s_flr, b + 1)
                nc.vector.tensor_copy(flags["A"][:, :], ps[0:1, 0, 0:H]).then_inc(s_fl, 1)
                dve.wait_ge(s_fl, b + 1)
                held(dve)
                with dve.Fori(0, NHG // 2) as g:
                    attend("A", g)
                mix(0)
                for c in range(NCH):
                    e = b * NCH + c
                    cols = slice(c * CH, (c + 1) * CH)
                    dve.wait_ge(s_kraw, e + 1)
                    if c >= 1:
                        dve.wait_ge(s_scan, e)
                    for kt in range(KT):
                        last = nc.vector.tensor_tensor_scan(
                            kT[:, kt, cols], decay[:, kt:kt + 1].to_broadcast([P, CH]), kT[:, kt, cols],
                            0.0 if c == 0 else kT[:, kt, c * CH - 1:c * CH], ALU.mult, ALU.add)
                    last.then_inc(s_scan, 1)
                    dve.wait_ge(s_vd, e + 1)
                    if c >= 1:
                        dve.wait_ge(s_vt, e)
                    n = CH if c + 1 < NCH else CH - 1
                    for kt in range(KT):
                        last = nc.vector.scalar_tensor_tensor(
                            v_mix[:, kt, 0:n], v_diff[:, kt, 0:n], v_coef[:, kt:kt + 1],
                            vT[:, kt, c * CH + 1:c * CH + 1 + n], ALU.mult, ALU.add)
                        if n < CH:
                            last = nc.vector.tensor_scalar(v_mix[:, kt, n:CH], v_diff[:, kt, n:CH],
                                                           v_coef[:, kt:kt + 1], None, ALU.mult)
                    last.then_inc(s_vm, 1)
                    nh = TB * H
                    for side, (ready, sq) in enumerate(((s_sqk, sq_k), (s_sqv, sq_v))):
                        dve.wait_ge(ready, e + 1)
                        step(nc.vector.tensor_reduce(nw_v[:, side * nh:(side + 1) * nh],
                                                     sq.rearrange("p (g e) -> p g e", e=DK), AX_X, ALU.add))
                    settle()
                    step(nc.vector.tensor_scalar(nw_v[:, :], nw_v[:, :], 1.0e-30, None, ALU.max))
                    settle()
                    rsqrt(P)
                    step(nc.vector.tensor_tensor(nw_u[:, :], nw_v[:, :], nw_y[:, :], ALU.mult))
                    settle()
                    step(nc.vector.tensor_scalar(nw_u[:, :], nw_u[:, :], NORM_EPS, None, ALU.add))
                    settle()
                    step(nc.vector.reciprocal(nw_y[:, :], nw_u[:, :]))
                    settle()
                    for side in range(2):
                        fac = nw_y[:, side * nh:(side + 1) * nh].rearrange("p (t h) -> p t h", t=TB)
                        step(nc.vector.tensor_tensor(fac, fac, scale_row[:, side, :].unsqueeze(1)
                                                     .to_broadcast([P, TB, H]), ALU.mult))
                    settle()
                    for side, (dst, done) in enumerate(((kn_tok, s_kn), (v_all[:, TB * c:TB * (c + 1), :], s_vall))):
                        last = nc.vector.tensor_tensor(
                            dst.rearrange("p t (h e) -> p (t h) e", e=DK),
                            bank2(2 * side).rearrange("p (g e) -> p g e", e=DK),
                            nw_y[:, side * nh:(side + 1) * nh].unsqueeze(2).to_broadcast([P, nh, DK]), ALU.mult)
                        last.then_inc(done, 1)
                    for i in range(2):
                        if c >= 1:
                            dve.wait_ge(s_mlB, 4 * e + 2 * i - 2)
                        split_rest(4 + i, s_hB, e * 2, i, s_r1B, s_mlB)
                with dve.Fori(0, NHG // 2) as g:
                    attend("B", g)
                mix(1)
                assert steps[0] <= DVE_STEPS
                dve.sem_inc(s_dve, DVE_STEPS - steps[0])


_WEIGHTS = ["L0_attn_a_q_proj", "L0_attn_a_k_proj", "L0_attn_a_v_proj", "L0_attn_a_o_proj", "L0_ffn_W_r", "L0_ffn_W_k",
            "L0_ffn_W_v", "L0_attn_b_W_k", "L0_attn_b_W_v", "L0_attn_b_W_c"]
_OTHERS = {"X": "L0_attn_a_X", "beta": "L0_attn_b_leaky_key_beta", "key_scale": "L0_attn_b_key_scale",
           "v_coef": "L0_attn_b_v_coef", "val_scale": "L0_attn_b_val_scale", "mu_r": "L0_ffn_mu_r",
           "mu_k": "L0_ffn_mu_k"}


def kernel(**inputs):
    import numpy as _np
    import concourse.bacc as _bacc
    from concourse import mybir as _mybir
    from concourse.bass_utils import run_bass_kernel_spmd as _run

    nc = _bacc.Bacc("TRN2", target_bir_lowering=False, num_devices=1)
    arrays, aps = {}, {}
    for name in _WEIGHTS + list(_OTHERS.values()):
        a = _np.ascontiguousarray(inputs[name])
        arrays[f"in_{name}"] = a
        aps[name] = nc.dram_tensor(f"in_{name}", a.shape, _mybir.dt.from_np(a.dtype), kind="ExternalInput").ap()
    out = nc.dram_tensor("out_0", (B, S, D), F32, kind="ExternalOutput").ap()
    tensors = {short: aps[name] for short, name in _OTHERS.items()}
    tensors["weights"] = [aps[name] for name in _WEIGHTS]
    hybrid_kernel(nc, tensors, out)
    r = _run(nc, [arrays], core_ids=[0])
    return r.results[0]["out_0"]
```

```python
from contextlib import ExitStack

import concourse.bass as bass
from concourse import mybir

F32 = mybir.dt.float32
BF16 = mybir.dt.bfloat16
I32 = mybir.dt.int32
ACT = mybir.ActivationFunctionType
ALU = mybir.AluOpType
AX_X = mybir.AxisListType.X

P = 128
B, S, D, H = 4, 2048, 256, 16
DK = D // H
KT = D // P
NT = S // P
CH = 512
NCH = S // CH
TB = CH // P
HG = 4
NHG = H // HG
HS = 32
EPS = 1e-5
NORM_EPS = 1e-10
SCALE = {"A": DK ** -0.5, "B": 1.0}
EXP_SCALING = 10.0
KEY_SCALE_MAX = 11.090339630053647
SAFE = 64.0
NEG = -1.0e30
FLOOR = -1.0e20
K_PART = (0, 1, 2, 0, 1, 0)
Q_PART = (0, 0, 0, 1, 1, 2)
PART_RUNS = ((0, 0, 0, 3), (0, 3, 0, 2), (0, 5, 0, 1), (1, 0, 0, 1), (1, 1, 0, 1), (1, 2, 0, 2), (1, 4, 1, 2))
assert all((K_PART, Q_PART)[_s][_r:_r + _n] == tuple(range(_p, _p + _n)) for _s, _r, _p, _n in PART_RUNS)
MROW = DK * len(K_PART)
KROWS = MROW + 3
RSQRT_MAGIC = 0x5F3759DF

WQ, WK, WV, WO, FR, FK, FV, BK, BV, BC = range(10)



def score_banks():
    banks = []
    for qc in range(NCH):
        for kb in range(TB * qc):
            for j in range(HG):
                banks.append([(qc, kb, j, 0, CH, 0)])
        d = TB * qc
        for j in range(HG):
            banks.append([(qc, d, j, 0, CH, 0)])
        for j in range(HG):
            banks.append([(qc, d + 1, j, P, 3 * P, 0), (qc, d + 3, j, 3 * P, P, 3 * P)])
        for j in range(0, HG, 2):
            banks.append([(qc, d + 2, j, 2 * P, 2 * P, 0), (qc, d + 2, j + 1, 2 * P, 2 * P, 2 * P)])
    return banks


GB = 3
BANKS = score_banks()
GROUPS = [BANKS[i:i + GB] for i in range(0, len(BANKS), GB)]
NG = len(GROUPS)
NP_BUF = 4
P_FREE_0 = 2 * NG


def value_sets():
    sets = {}
    for i, bk in enumerate(BANKS):
        for unit in bk:
            sets.setdefault(unit[0:2], []).append((i, unit))
    order = sorted(sets.values(), key=lambda st: (st[-1][0], st[0][1][1]))
    result, freed = [], 0
    for n, st in enumerate(order):
        left = min([i for later in order[n + 1:] for i, _ in later], default=NG * GB)
        result.append((st, st[-1][0] // GB, left // GB - freed))
        freed = left // GB
    return result


VALUE_SETS = value_sets()
LAST_GROUP = [max(i // GB for st, _, _ in VALUE_SETS for i, u in st if u[0] == qc) for qc in range(NCH)]
TURN_GROUP = [min(g + 3, NG - 1) for g in LAST_GROUP]
LOADS = len(PART_RUNS) + 2
LOADS_0 = NCH * len(PART_RUNS) + 2
KQ0 = 16 * (LOADS_0 + (NHG // 2 - 1) * LOADS)


assert NG % 2 == 0 and 2 * NG % NP_BUF == 0

MAX_PIECES = []
for _qb in range(NT):
    _n = _qb // TB + 1
    MAX_PIECES.append((_qb, 0, min(_n, GB)))
    if _n > GB:
        MAX_PIECES.append((_qb, GB, _n - GB))
NMP = len(MAX_PIECES)

DVE_STEPS = 1024


def hybrid_kernel(nc, t, out):
    with ExitStack() as ctx:
        def sb(name, shape, dt=F32):
            return ctx.enter_context(nc.sbuf_tensor(name, shape, dt))

        def sem(name):
            return ctx.enter_context(nc.semaphore(name))

        part_d = {"A": nc.dram_tensor("part_a", (2, 3 * DK, H, S), BF16, kind="Internal").ap(),
                  "B": nc.dram_tensor("part_b", (1, 3 * DK, H, S), BF16, kind="Internal").ap()}
        rows_d = nc.dram_tensor("max_rows", (2, 3, HG * S), BF16, kind="Internal").ap()

        wT = sb("wT", [P, 10, KT, D])
        x_res = sb("x_res", [P, NT, D])
        xnT = sb("xnT", [P, KT, S + 4])
        v_all = sb("v_all", [P, NT, D])
        o_tok = sb("o_tok", [P, NT, D])
        stage = sb("stage", [P, 4, HG * S], BF16)
        v_st = sb("v_st", [P, 2, NT, HG, HS])
        probs = sb("probs", [P, NP_BUF, GB * CH])
        o_ev = sb("o_ev", [P, 2, CH])
        ident = sb("ident", [P, P])
        ident_b = sb("ident_b", [P, P], BF16)
        mask_qk = {a: sb(f"mask_qk_{a}", [P, P], BF16) for a in "AB"}
        mask_kq = {a: sb(f"mask_kq_{a}", [P, P], BF16) for a in "AB"}
        head_sel = sb("head_sel", [P, KT, H], BF16)
        sel_ch = sb("sel_ch", [H, D])
        ones_row = sb("ones_row", [1, P])
        head_col = sb("head_col", [H, 2])
        head_row = sb("head_row", [1, 3, H])
        scale_row = sb("scale_row", [P, 2, H])
        decay = sb("decay", [P, KT])
        v_coef = sb("v_coef", [P, KT])
        mu = sb("mu", [P, 2, KT])
        ln_st = sb("ln_st", [P, TB, 6])
        ln_mv = sb("ln_mv", [P, TB, 2])
        nw_v = sb("nw_v", [P, P])
        nw_y = sb("nw_y", [P, P])
        nw_u = sb("nw_u", [P, P])
        n_max = sb("n_max", [H, 2, NCH])
        n_top = sb("n_top", [H, 2])
        fl_prod = sb("fl_prod", [H, 1])
        fl_col = sb("fl_col", [H, 1])
        fl_any = sb("fl_any", [1, NHG])
        flags = {a: sb(f"flags_{a}", [1, H + NHG], I32) for a in "AB"}
        den = sb("den", [P, TB, HG])
        rec = sb("rec", [P, TB, HG])
        pmax = sb("pmax", [P, 2, NT])
        row_max = sb("row_max", [P, NT])
        m_part = [sb(f"m_part{i}", [NT, P], BF16) for i in range(3)]
        m_rest = sb("m_rest", [NT, P])

        def f32_view(ap):
            return ap.bitcast(F32)

        low = f32_view(stage[:, 0:2, :].rearrange("p a n -> p (a n)"))
        high = f32_view(stage[:, 2:4, :].rearrange("p a n -> p (a n)"))

        def low_buf(i):
            return low[:, i * 1024:(i + 1) * 1024]

        xnt = [low_buf(i).rearrange("p (t d) -> p t d", t=TB) for i in range(2)]
        x_r = low_buf(2).rearrange("p (k n) -> p k n", k=KT)
        x_k = low_buf(3).rearrange("p (k n) -> p k n", k=KT)
        k_act = low_buf(4).rearrange("p (k n) -> p k n", k=KT)
        r_gate = low_buf(5).rearrange("p (t d) -> p t d", t=TB)
        x_diff = low_buf(6).rearrange("p (k n) -> p k n", k=KT)
        xn3T = low_buf(7).rearrange("p (k n) -> p k n", k=KT)
        kT = high[:, 0:KT * S].rearrange("p (k n) -> p k n", k=KT)
        vT = high[:, KT * S:2 * KT * S].rearrange("p (k n) -> p k n", k=KT)
        w_nat = high[:, 0:10 * 512].rearrange("p (w m d) -> p w m d", w=10, m=KT)

        xnt_a = [o_tok[:, TB * i:TB * (i + 1), :] for i in range(2)]
        sq_k, sq_v = (o_tok[:, TB * i:TB * (i + 1), :].rearrange("p t d -> p (t d)") for i in range(2))
        kn_tok = o_tok[:, 2 * TB:3 * TB, :]
        v_mix = o_tok[:, 3 * TB:4 * TB, :].rearrange("p t d -> p (t d)").rearrange("p (k n) -> p k n", k=KT)

        pf = probs[:, :, :].rearrange("p a n -> p (a n)")
        parts = [pf[:, i * 768:(i + 1) * 768].bitcast(BF16).rearrange("p (r n) -> p r n", r=3) for i in range(4)]
        rest = [pf[:, 3072 + i * CH:3072 + (i + 1) * CH] for i in range(2)]
        oT = pf[:, 4096:5120].rearrange("p (k n) -> p k n", k=KT)
        v_diff = oT
        sq_b = [pf[:, 5120 + i * 256:5376 + i * 256].bitcast(BF16) for i in range(4)]

        ps = ctx.enter_context(nc.psum_tensor("ps", [P, 8, CH], F32))

        def bank2(i):
            return ps[:, i:i + 2, :].rearrange("p a n -> p (a n)")

        def tok_bank(bk0, tb):
            return ps[:, bk0 + tb // 2, (tb % 2) * D:(tb % 2 + 1) * D]

        s_w = sem("weights_loaded")
        s_par = sem("params_loaded")
        s_rows_set = sem("max_rows_set")
        s_rows = sem("max_rows_stored")
        s_const = sem("constants_built")
        s_pool = sem("pool_step")
        s_wt_ps = sem("weight_transposed")
        s_wt = sem("weight_copied")
        s_hp_ps = sem("head_params_in_psum")
        s_hp = sem("head_params_step")
        s_setup = sem("setup_done")
        s_x = [sem(f"x_loaded{c}") for c in range(NCH)]
        s_dve = sem("vector_step")
        s_ln = {k: sem(f"ln_{k}_ready") for k in ("a", "ffn", "b")}
        s_lnT = {k: sem(f"ln_{k}_transposed") for k in ("a", "ffn", "b")}
        s_lnC = {k: sem(f"ln_{k}_channel_major") for k in ("a", "ffn", "b")}
        s_qk = sem("qk_in_psum")
        s_h = sem("qk_high_part")
        s_r1 = sem("qk_rest")
        s_ml = sem("qk_low_parts")
        s_parts = [sem(f"qk_stored{i}") for i in range(4)]
        s_v = sem("v_in_psum")
        s_vcopy = sem("v_copied")
        s_nrm = sem("norms_in_psum")
        s_nmax = sem("norm_max")
        s_flc = sem("flag_column")
        s_flr = sem("flag_row")
        s_fl = sem("flags_ready")
        s_oTp = sem("o_transposed")
        s_oTc = sem("o_channel_major")
        s_oproj = sem("o_projected")
        s_res = sem("attention_residual")
        s_diff = sem("shift_difference")
        s_xr = sem("x_r_ready")
        s_xk = sem("x_k_ready")
        s_rp = sem("r_in_psum")
        s_sig = sem("r_gate_ready")
        s_kp = sem("k_in_psum")
        s_relu = sem("k_relu")
        s_kact = sem("k_squared")
        s_fv = sem("ffn_in_psum")
        s_x2 = sem("ffn_residual")
        s_kb = sem("b_keys_in_psum")
        s_kraw = sem("b_keys_copied")
        s_vb = sem("b_values_in_psum")
        s_vraw = sem("b_values_copied")
        s_scan = sem("b_keys_decayed")
        s_vd = sem("b_value_difference")
        s_vm = sem("b_values_mixed")
        s_kt = sem("b_keys_token_major")
        s_vt = sem("b_values_token_major")
        s_sqk = sem("b_key_squares")
        s_sqv = sem("b_value_squares")
        s_kn = sem("b_keys_normed")
        s_vall = sem("b_values_normed")
        s_knT = sem("b_keys_channel_major")
        s_hB = sem("b_key_high_part")
        s_r1B = sem("b_key_rest")
        s_mlB = sem("b_key_low_parts")
        s_partsB = [sem(f"b_key_stored{i}") for i in range(2)]
        s_out = [sem(f"out_stored{c}") for c in range(NCH)]
        s_held = sem("wait_passed")
        att = {}
        for a in "AB":
            att[a] = {n: sem(f"{n}_{a}") for n in (
                "kq0", "kq1", "scores", "probs", "p_free", "vst",
                "o_ev", "o_T", "o_free", "o_step", "mx_scores", "mx_used", "mx_col", "mx_T", "mx_step", "mx_row",
                "mx_dma")}

        def held(eng):
            eng.sem_inc(s_held, 1)

        def at_most(value, high):
            return nc.s_assert_within(value, 0, high, skip_runtime_bounds_check_because="the branch excludes the last pass")

        block = ctx.enter_context(nc.Block())

        @block.sync
        def _(sp):
            for i, name in enumerate(t["weights"]):
                sp.dma_start(w_nat[:, i], name.rearrange("(m p) d -> p m d", p=P)).then_inc(s_w, 16)
            sp.dma_start(mu[:, 0, :], t["mu_r"].rearrange("(k p) -> p k", p=P),
                         allow_slow_non_contiguous=True).then_inc(s_par, 16)
            sp.dma_start(mu[:, 1, :], t["mu_k"].rearrange("(k p) -> p k", p=P),
                         allow_slow_non_contiguous=True).then_inc(s_par, 16)
            col = "a h b c -> h (a b c)"
            row = "a h b c -> (a b c) h"
            sp.dma_start(head_col[:, 0:1], t["beta"].rearrange(col)).then_inc(s_par, 16)
            sp.dma_start(head_col[:, 1:2], t["v_coef"].rearrange(col)).then_inc(s_par, 16)
            sp.dma_start(head_row[:, 0, :], t["key_scale"].rearrange(row)).then_inc(s_par, 16)
            sp.dma_start(head_row[:, 1, :], t["val_scale"].rearrange(row)).then_inc(s_par, 16)
            sp.wait_ge(s_rows_set, 1)
            sp.dma_start(rows_d[0], stage[0:3, 0, :]).then_inc(s_rows, 16)
            sp.dma_start(rows_d[1], stage[0:3, 1, :]).then_inc(s_rows, 16)
            sp.wait_ge(s_rows, 32)

            def load_parts(a, u, hg, cols):
                for side, r, part, n in PART_RUNS:
                    src = part_d[a][(1 - side) if a == "A" else 0, part * DK:(part + n) * DK,
                                    bass.ds(hg * HG, HG), cols]
                    dst = stage[r * DK:(r + n) * DK, 2 * u + side, :].rearrange("e (j n) -> e j n", j=HG)[:, :, cols]
                    sp.dma_start(dst, src).then_inc(att[a][f"kq{u}"], 16)

            def load_rows(a, u):
                for side in range(2):
                    sp.dma_start(stage[MROW:KROWS, 2 * u + side, :], rows_d[side]).then_inc(att[a][f"kq{u}"], 16)

            def load_group(a, u, hg, inst):
                sp.wait_ge(att[a]["p_free"], (inst + 1) * NG)
                held(sp)
                load_parts(a, u, hg, slice(0, S))
                load_rows(a, u)

            def maxima_rows(a, u, hg, inst):
                sm = att[a]
                grp = sp.value_load(flags[a][0:1, bass.ds(H + hg, 1)])
                with sp.If(grp > 0):
                    for j in range(HG):
                        flag = sp.value_load(flags[a][0:1, bass.ds(hg * HG + j, 1)])
                        with sp.If(flag > 0):
                            sp.wait_ge(sm["mx_row"], inst * HG + j + 1)
                            for r in range(3):
                                sp.dma_start(stage[MROW + r:MROW + r + 1, 2 * u + 1, j * S:(j + 1) * S]
                                             .rearrange("o (t q) -> o t q", t=NT),
                                             m_part[r][:, :]).then_inc(sm["mx_dma"], 16)
                        with sp.Else():
                            sp.sem_inc(sm["mx_dma"], 48)
                with sp.Else():
                    sp.sem_inc(sm["mx_dma"], 48 * HG)

            def attend(a, b):
                with sp.Fori(0, NHG // 2) as g:
                    inst = b * NHG + g * 2
                    maxima_rows(a, 0, g * 2, inst)
                    load_group(a, 1, g * 2 + 1, inst + 1)
                    maxima_rows(a, 1, g * 2 + 1, inst + 1)
                    with sp.If(g < NHG // 2 - 1):
                        load_group(a, 0, at_most(g * 2 + 2, NHG - 1), inst + 2)

            def store_part(a, side, m, i, c, done):
                for r in range(3):
                    sp.dma_start(part_d[a][side, r * DK:(r + 1) * DK, m * (H // KT):(m + 1) * (H // KT),
                                           c * CH:(c + 1) * CH].rearrange("e h n -> h e n"),
                                 parts[i][:, r, :]).then_inc(done, 16)

            def load_x(b, c):
                sp.dma_start(x_res[:, TB * c:TB * (c + 1), :],
                             x_d[bass.ds(b, 1), c].rearrange("o p t d -> (o p) t d")).then_inc(s_x[c], 16)

            x_d = t["X"].rearrange("b (c t p) d -> b c p t d", p=P, t=TB)
            out_d = out.rearrange("b (c t p) d -> b c p t d", p=P, t=TB)
            for c in range(NCH):
                load_x(0, c)
            with sp.Fori(0, B) as b:
                load_rows("A", 0)
                for c in range(NCH):
                    for i in range(4):
                        sp.wait_ge(s_ml, (b * NCH + c) * 8 + 2 * i + 2)
                        store_part("A", i // 2, i % 2, i, c, s_parts[i])
                    for i in range(4):
                        sp.wait_ge(s_parts[i], (b * NCH + c + 1) * 48)
                    load_parts("A", 0, 0, slice(c * CH, (c + 1) * CH))
                sp.wait_ge(s_fl, b + 1)
                held(sp)
                attend("A", b)
                sp.wait_ge(s_vraw, (b + 1) * NCH)
                sp.wait_ge(s_x2, b * 2 * NCH + NCH)
                held(sp)
                load_rows("B", 0)
                for c in range(NCH):
                    for i in range(2):
                        sp.wait_ge(s_mlB, (b * NCH + c) * 4 + 2 * i + 2)
                        store_part("B", 0, i, 2 * (c % 2) + i, c, s_partsB[i])
                    for i in range(2):
                        sp.wait_ge(s_partsB[i], (b * NCH + c + 1) * 48)
                    load_parts("B", 0, 0, slice(c * CH, (c + 1) * CH))
                sp.wait_ge(s_vall, (b + 1) * NCH)
                held(sp)
                attend("B", b)
                for c in range(NCH):
                    sp.wait_ge(s_x2, b * 2 * NCH + NCH + c + 1)
                    sp.dma_start(out_d[bass.ds(b, 1), c].rearrange("o p t d -> (o p) t d"),
                                 x_res[:, TB * c:TB * (c + 1), :]).then_inc(s_out[c], 16)
                    with sp.If(b < B - 1):
                        sp.wait_ge(s_out[c], (b + 1) * 16)
                        load_x(at_most(b + 1, B - 1), c)
            for c in range(NCH):
                sp.wait_ge(s_out[c], B * 16)

        @block.gpsimd
        def _(pool):
            steps = [0]

            def step(ins):
                steps[0] += 1
                ins.then_inc(s_pool, 1)

            def settle():
                pool.wait_ge(s_pool, steps[0])

            step(pool.memset(stage[0:3, 0, :], 1.0))
            step(pool.memset(stage[0:3, 1, :], 0.0))
            settle()
            pool.sem_inc(s_rows_set, 1)
            step(pool.memset(ident[:, :], 0.0))
            for m in (mask_qk, mask_kq):
                for a in "AB":
                    step(pool.memset(m[a][:, :], 0.0))
            step(pool.memset(head_sel[:, :, :], 1.0))
            step(pool.memset(sel_ch[:, :], 1.0))
            step(pool.memset(ones_row[:, :], 1.0))
            step(pool.memset(xnT[:, :, 0:1], 0.0))
            step(pool.memset(pmax[:, :, :], FLOOR))
            step(pool.memset(v_st[:, :, :, :, :].rearrange("p u t j e -> p (u t j) e"), 0.0))
            settle()
            step(pool.affine_select(out=ident[:, :], in_=ident[:, :], compare_op=ALU.not_equal, fill=1.0, base=0,
                                    pattern=[[-1, P]], channel_multiplier=1))
            for m, sign in ((mask_qk, 1), (mask_kq, -1)):
                for a, op in (("A", ALU.is_ge), ("B", ALU.is_gt)):
                    step(pool.affine_select(out=m[a][:, :], in_=m[a][:, :], compare_op=op, fill=NEG, base=0,
                                            pattern=[[-sign, P]], channel_multiplier=sign))
            step(pool.memset(v_st[:, :, :, :, DK:DK + 1].rearrange("p u t j e -> p (u t j) e"), 1.0))
            step(pool.affine_select(out=head_sel[:, :, :], in_=head_sel[:, :, :], compare_op=ALU.is_ge, fill=0.0,
                                    base=0, pattern=[[P, KT], [-DK, H]], channel_multiplier=1))
            step(pool.affine_select(out=sel_ch[:, :], in_=sel_ch[:, :], compare_op=ALU.is_ge, fill=0.0, base=0,
                                    pattern=[[1, D]], channel_multiplier=-DK))
            settle()
            step(pool.affine_select(out=head_sel[:, :, :], in_=head_sel[:, :, :], compare_op=ALU.is_ge, fill=0.0,
                                    base=DK - 1, pattern=[[-P, KT], [DK, H]], channel_multiplier=-1))
            step(pool.affine_select(out=sel_ch[:, :], in_=sel_ch[:, :], compare_op=ALU.is_ge, fill=0.0,
                                    base=DK - 1, pattern=[[-1, D]], channel_multiplier=DK))
            step(pool.tensor_copy(ident_b[:, :], ident[:, :]))
            settle()
            pool.sem_inc(s_const, 1)

            def low_parts(done, rest_ready, base, i, buf):
                pool.wait_ge(rest_ready, base + i + 1)
                held(pool)
                pool.tensor_copy(parts[buf][:, 1, :], rest[i % 2]).then_inc(done, 1)
                pool.wait_ge(done, 2 * (base + i) + 1)
                pool.tensor_tensor(parts[buf][:, 2, :], rest[i % 2], parts[buf][:, 1, :],
                                   ALU.subtract).then_inc(done, 1)

            def attend(a, b, g):
                sm = att[a]
                for u in range(2):
                    inst = b * NHG + g * 2 + u
                    pool.wait_ge(sm["p_free"], (inst + 1) * NG)
                    held(pool)
                    pool.tensor_copy(
                        v_st[:, u, :, :, 0:DK],
                        v_all[:, :, bass.ds((g * 2 + u) * HG * DK, HG * DK)]
                        .rearrange("p t (j e) -> p t j e", j=HG)).then_inc(sm["vst"], 1)

            def mix(b, p):
                for c in range(NCH):
                    f = b * 2 * NCH + p * NCH + c
                    pool.wait_ge(s_lnC["ffn"], f + 1)
                    now, before = xnT[:, :, c * CH + 1:c * CH + 1 + CH], xnT[:, :, c * CH:c * CH + CH]
                    if c >= 1:
                        pool.wait_ge(s_xr, f)
                    pool.tensor_tensor(x_diff, now, before, ALU.subtract).then_inc(s_diff, 1)
                    pool.wait_ge(s_relu, f + 1)
                    pool.tensor_tensor(k_act, k_act, k_act, ALU.mult).then_inc(s_kact, 1)

            with pool.Fori(0, B) as b:
                def low_keys(c):
                    for i in range(2):
                        low_parts(s_mlB, s_r1B, (b * NCH + c) * 2, i, 2 * (c % 2) + i)

                for c in range(NCH):
                    for i in range(4):
                        low_parts(s_ml, s_r1, (b * NCH + c) * 4, i, i)
                pool.wait_ge(s_vcopy, (b + 1) * NCH)
                held(pool)
                with pool.Fori(0, NHG // 2) as g:
                    attend("A", b, g)
                mix(b, 0)
                for c in range(NCH):
                    e = b * NCH + c
                    pool.wait_ge(s_vraw, b * NCH + min(c + 2, NCH))
                    held(pool)
                    if c >= 1:
                        pool.wait_ge(s_vm, e)
                        held(pool)
                    n = CH if c + 1 < NCH else CH - 1
                    if c + 1 == NCH:
                        pool.tensor_copy(v_diff[:, :, n:CH], vT[:, :, S - 1:S])
                    pool.tensor_tensor(v_diff[:, :, 0:n], vT[:, :, c * CH:c * CH + n],
                                       vT[:, :, c * CH + 1:c * CH + 1 + n], ALU.subtract).then_inc(s_vd, 1)
                    if c >= 2:
                        low_keys(c - 2)
                low_keys(NCH - 2)
                low_keys(NCH - 1)
                pool.wait_ge(s_vall, (b + 1) * NCH)
                held(pool)
                with pool.Fori(0, NHG // 2) as g:
                    attend("B", b, g)
                mix(b, 1)

        @block.scalar
        def _(act):
            for i in range(10):
                act.wait_ge(s_wt_ps, i + 1)
                nc.scalar.copy(wT[:, i].rearrange("p k n -> p (k n)"), ps[:, i % 8, :]).then_inc(s_wt, 1)
            act.wait_ge(s_par, 6 * 16)
            nc.scalar.activation(head_col[:, 0:1], head_col[:, 0:1], ACT.Abs).then_inc(s_hp, 1)
            act.wait_ge(s_hp, 2)
            nc.scalar.activation(head_col[:, 0:1], head_col[:, 0:1], ACT.Exp, scale=-EXP_SCALING).then_inc(s_hp, 1)
            nc.scalar.activation(head_row[:, 0:2, :], head_row[:, 0:2, :], ACT.Exp,
                                 scale=EXP_SCALING).then_inc(s_hp, 1)

            def channel_major(dst, pair, ready, want, done):
                act.wait_ge(ready, want)
                nc.scalar.copy(dst, ps[:, pair:pair + 2, :]).then_inc(done, 1)

            def ln_copy(kind, n, pair, dst):
                channel_major(dst, pair, s_lnT[kind], n + 1, s_lnC[kind])

            def attend(a, b, g):
                sm = att[a]
                for u in range(2):
                    inst = b * NHG + g * 2 + u
                    for gi, grp in enumerate(GROUPS):
                        act.wait_ge(sm["scores"], inst * NG + gi + 1)
                        act.wait_ge(sm["p_free"], P_FREE_0 + inst * NG + gi + 1 - NP_BUF)
                        w = len(grp) * CH
                        nc.scalar.activation(
                            probs[:, (u * NG + gi) % NP_BUF, 0:w],
                            ps[:, GB * (gi % 2):GB * (gi % 2) + len(grp), :].rearrange("p a n -> p (a n)"),
                            ACT.Exp, scale=SCALE[a]).then_inc(sm["probs"], 1)

            def mix(b, p):
                f0 = b * 2 * NCH + p * NCH
                e0 = b * NCH

                def o_copy(c):
                    channel_major(oT, 0, s_oTp, f0 + c + 1, s_oTc)

                def b_inputs(c):
                    cols = slice(c * CH, (c + 1) * CH)
                    ln_copy("b", e0 + c, 4, xn3T)
                    channel_major(kT[:, :, cols], 4, s_kb, e0 + c + 1, s_kraw)
                    channel_major(vT[:, :, cols], 6, s_vb, e0 + c + 1, s_vraw)

                o_copy(0)
                for c in range(NCH):
                    f = f0 + c
                    if c + 1 < NCH:
                        o_copy(c + 1)
                    ln_copy("ffn", f, 4, xnT[:, :, c * CH + 1:c * CH + 1 + CH])
                    act.wait_ge(s_kp, f + 1)
                    nc.scalar.activation(k_act, ps[:, 0:2, :], ACT.Relu).then_inc(s_relu, 1)
                    act.wait_ge(s_rp, f + 1)
                    if c >= 1:
                        act.wait_ge(s_x2, f)
                    nc.scalar.activation(r_gate.rearrange("p t d -> p (t d)"), bank2(6),
                                         ACT.Sigmoid).then_inc(s_sig, 1)
                    if p == 0 and c >= 1:
                        b_inputs(c - 1)
                if p == 0:
                    b_inputs(NCH - 1)

            with act.Fori(0, B) as b:
                ln_copy("a", b * NCH, 0, xnT[:, :, 1:1 + CH])
                for c in range(NCH):
                    e = b * NCH + c
                    if c >= 1:
                        act.wait_ge(s_nrm, e)
                    for i in range(4):
                        act.wait_ge(s_qk, e * 4 + i + 1)
                        if c >= 1:
                            act.wait_ge(s_parts[i], e * 48)
                        nc.scalar.copy(parts[i][:, 0, :], ps[:, 2 + i, :])
                        nc.scalar.activation(sq_b[i], ps[:, 2 + i, :], ACT.Square).then_inc(s_h, 1)
                    if c + 1 < NCH:
                        ln_copy("a", e + 1, 0, xnT[:, :, (c + 1) * CH + 1:(c + 2) * CH + 1])
                    act.wait_ge(s_v, e + 1)
                    nc.scalar.copy(v_all[:, TB * c:TB * (c + 1), :].rearrange("p t d -> p (t d)"),
                                   bank2(6)).then_inc(s_vcopy, 1)
                act.wait_ge(s_fl, b + 1)
                held(act)
                with act.Fori(0, NHG // 2) as g:
                    attend("A", b, g)
                mix(b, 0)
                for c in range(NCH + 1):
                    e = b * NCH + c
                    if c < NCH:
                        act.wait_ge(s_kt, e + 1)
                        nc.scalar.activation(sq_k, bank2(0), ACT.Square).then_inc(s_sqk, 1)
                        act.wait_ge(s_vt, e + 1)
                        nc.scalar.activation(sq_v, bank2(2), ACT.Square).then_inc(s_sqv, 1)
                    if c >= 1:
                        side = 2 * ((c - 1) % 2)
                        for i in range(2):
                            act.wait_ge(s_knT, (e - 1) * 2 + i + 1)
                            if c >= 3:
                                act.wait_ge(s_partsB[i], (e - 2) * 48)
                            nc.scalar.copy(parts[side + i][:, 0, :], ps[:, 4 + side + i, :]).then_inc(s_hB, 1)
                with act.Fori(0, NHG // 2) as g:
                    attend("B", b, g)
                mix(b, 1)

        @block.tensor
        def _(pe):
            for a in "AB":
                pe.sem_inc(att[a]["p_free"], P_FREE_0)
            pe.wait_ge(s_const, 1)
            pe.wait_ge(s_w, 160)
            for i in range(10):
                if i >= 8:
                    pe.wait_ge(s_wt, i - 7)
                for kt in range(KT):
                    for m in range(KT):
                        last = pe.transpose(ps[:, i % 8, kt * D + m * P:kt * D + (m + 1) * P],
                                            w_nat[:, i, m, kt * P:(kt + 1) * P], ident[:, :])
                last.then_inc(s_wt_ps, 1)
            pe.wait_ge(s_wt, 10)
            pe.wait_ge(s_hp, 4)
            for kt in range(KT):
                pe.matmul(ps[:, 0, 2 * kt:2 * kt + 2], sel_ch[:, kt * P:(kt + 1) * P], head_col[:, :],
                          start=True, stop=True)
            pe.matmul(ps[:, 1, 0:2 * H], ones_row[:, :], head_row[:, 0:2, :].rearrange("o k h -> o (k h)"),
                      start=True, stop=True).then_inc(s_hp_ps, 1)
            pe.wait_ge(s_setup, 1)

            def to_channels(bk, src):
                for kt in range(KT):
                    for tb in range(TB):
                        last = pe.transpose(ps[:, bk + kt, tb * P:(tb + 1) * P], src[:, tb, kt * P:(kt + 1) * P],
                                            ident[:, :])
                return last

            def to_tokens(bk, src):
                for tb in range(TB):
                    for kt in range(KT):
                        last = pe.transpose(tok_bank(bk, tb)[:, kt * P:(kt + 1) * P],
                                            src[:, kt, tb * P:(tb + 1) * P], ident[:, :])
                return last

            def project_channels(bk, w, m, src):
                for kt in range(KT):
                    last = pe.matmul(ps[:, bk, :], wT[:, w, kt, m * P:(m + 1) * P], src[:, kt, :],
                                     start=(kt == 0), stop=(kt == KT - 1))
                return last

            def project_tokens(bk, w, src):
                for tb in range(TB):
                    for kt in range(KT):
                        last = pe.matmul(tok_bank(bk, tb), src[:, kt, tb * P:(tb + 1) * P], wT[:, w, kt, :],
                                         start=(kt == 0), stop=(kt == KT - 1))
                return last

            def row_maxima(a, u, j, n):
                sm = att[a]
                kk, qq = (stage[0:KROWS, 2 * u + s, j * S:(j + 1) * S] for s in range(2))
                for i, (qb, b0, nb) in enumerate(MAX_PIECES):
                    if i >= 2:
                        pe.wait_ge(sm["mx_used"], n * NMP + i - 1)
                    for bk in range(b0, b0 + nb):
                        o = ps[:, GB * (i % 2) + bk - b0, :]
                        w = min(CH, (qb + 1) * P - bk * CH)
                        diag = (bk == qb // TB)
                        last = pe.matmul(o[:, 0:w], qq[:, qb * P:(qb + 1) * P], kk[:, bk * CH:bk * CH + w],
                                         start=True, stop=True)
                        if diag:
                            last = pe.matmul(o[:, w - P:w], ident_b[:, :], mask_qk[a][:, :], start=False, stop=True,
                                             skip_group_check=True)
                    last.then_inc(sm["mx_scores"], 1)
                pe.wait_ge(sm["mx_col"], n + 1)
                pe.transpose(ps[0:NT, 6, 0:P], row_max[:, :], ident[:, :]).then_inc(sm["mx_T"], 1)
                pe.wait_ge(sm["mx_dma"], (n + 1) * 48)

            def attend(a, b):
                sm = att[a]

                def begin(u, hg, inst, kq, fresh):
                    pe.wait_ge(sm[f"kq{u}"], kq)
                    held(pe)
                    grp = pe.value_load(flags[a][0:1, bass.ds(H + hg, 1)])
                    with pe.If(grp > 0):
                        if not fresh:
                            pe.wait_ge(sm["probs"], inst * NG)
                            held(pe)
                        for j in range(HG):
                            flag = pe.value_load(flags[a][0:1, bass.ds(hg * HG + j, 1)])
                            with pe.If(flag > 0):
                                row_maxima(a, u, j, inst * HG + j)
                            with pe.Else():
                                pe.sem_inc(sm["mx_scores"], NMP)
                                pe.sem_inc(sm["mx_T"], 1)
                    with pe.Else():
                        pe.sem_inc(sm["mx_scores"], NMP * HG)
                        pe.sem_inc(sm["mx_T"], HG)

                def scores(u, inst, gi, fresh=False):
                    kk = stage[0:KROWS, 2 * u, :].rearrange("r (j n) -> r j n", j=HG)
                    qq = stage[0:KROWS, 2 * u + 1, :].rearrange("r (j n) -> r j n", j=HG)
                    if not fresh:
                        pe.wait_ge(sm["probs"], inst * NG + gi - 1)
                    for n, bk in enumerate(GROUPS[gi]):
                        for qc, kb, j, q0, w, col in bk:
                            o = ps[:, GB * (gi % 2) + n, col:col + w]
                            last = pe.matmul(o, kk[:, j, kb * P:(kb + 1) * P],
                                             qq[:, j, qc * CH + q0:qc * CH + q0 + w], start=True, stop=True)
                            if kb >= TB * qc:
                                last = pe.matmul(o[:, 0:P], ident_b[:, :], mask_kq[a][:, :], start=False,
                                                 stop=True, skip_group_check=True)
                    last.then_inc(sm["scores"], 1)

                def products(u, inst, gi):
                    pe.wait_ge(sm["probs"], inst * NG + gi + 1)
                    for units, last_group, freed in VALUE_SETS:
                        if last_group != gi:
                            continue
                        qc, kb = units[0][1][0:2]
                        if kb == 0:
                            pe.wait_ge(sm["o_free"], inst * NCH + qc + 1)
                        for bank, (_, _, j, q0, w, col) in units:
                            slot = (u * NG + bank // GB) % NP_BUF
                            at = bank % GB * CH + col
                            last = pe.matmul(ps[HS * j:HS * (j + 1), 6 + qc % 2, q0:q0 + w],
                                             v_st[:, u, kb, j, :], probs[:, slot, at:at + w],
                                             start=(kb == 0), stop=(kb >= TB * qc), skip_group_check=True)
                        if freed:
                            last.then_inc(sm["p_free"], freed)

                def turn(inst, qc):
                    pe.wait_ge(sm["o_ev"], inst * NCH + qc + 1)
                    for tb in range(TB):
                        last = pe.transpose(ps[:, 6 + qc % 2, tb * P:(tb + 1) * P],
                                            o_ev[:, qc % 2, tb * P:(tb + 1) * P], ident[:, :])
                    last.then_inc(sm["o_T"], 1)

                kq0 = b * KQ0 + 16 * LOADS_0
                begin(0, 0, b * NHG, kq0, fresh=True)
                for gi in range(2):
                    scores(0, b * NHG, gi, fresh=True)
                with pe.Fori(0, NHG // 2) as g:
                    for u in range(2):
                        hg = g * 2 + u
                        inst = b * NHG + hg

                        def ahead(gi):
                            n = gi + 2 - NG
                            if n < 0:
                                scores(u, inst, gi + 2)
                            elif u == 0:
                                if n == 0:
                                    begin(1, hg + 1, inst + 1, (b * (NHG // 2) + g + 1) * 16 * LOADS, fresh=False)
                                scores(1, inst + 1, n)
                            else:
                                with pe.If(g < NHG // 2 - 1):
                                    if n == 0:
                                        begin(0, at_most(hg + 1, NHG - 1), inst + 1, kq0 + (g + 1) * 16 * LOADS, fresh=False)
                                    scores(0, inst + 1, n)

                        pe.wait_ge(sm["vst"], inst + 1)
                        for gi in range(NG):
                            ahead(gi)
                            products(u, inst, gi)
                            for qc in range(NCH):
                                if gi == TURN_GROUP[qc]:
                                    turn(inst, qc)

            def mix(b, p):
                f0 = b * 2 * NCH + p * NCH
                e0 = b * NCH

                def o_turn(c):
                    pe.wait_ge(att["AB"[p]]["o_free"], ((b + 1) * NHG - 1) * NCH + c + 3)
                    if c >= 2:
                        pe.wait_ge(s_x2, f0 + c - 1)
                    to_channels(0, o_tok[:, TB * c:TB * (c + 1), :]).then_inc(s_oTp, 1)

                def o_project(c):
                    pe.wait_ge(s_oTc, f0 + c + 1)
                    if c >= 1:
                        pe.wait_ge(s_res, f0 + c)
                    project_tokens(2, WO if p == 0 else BC, oT).then_inc(s_oproj, 1)

                def ln_turn(c):
                    pe.wait_ge(s_ln["ffn"], f0 + c + 1)
                    if p == 0 and c >= 2:
                        pe.wait_ge(s_kraw, e0 + c - 1)
                    to_channels(4, xnt[0]).then_inc(s_lnT["ffn"], 1)

                def hidden(c):
                    pe.wait_ge(s_xk, f0 + c + 1)
                    if c + 1 == NCH:
                        pe.wait_ge(s_x2, f0 + c)
                    project_channels(0, FK, 0, x_k)
                    project_channels(1, FK, 1, x_k).then_inc(s_kp, 1)
                    pe.wait_ge(s_xr, f0 + c + 1)
                    if p == 0 and c >= 2:
                        pe.wait_ge(s_vraw, e0 + c - 1)
                    project_tokens(6, FR, x_r).then_inc(s_rp, 1)

                def ffn_out(c):
                    pe.wait_ge(s_kact, f0 + c + 1)
                    project_tokens(0, FV, k_act).then_inc(s_fv, 1)

                def b_turn(c):
                    pe.wait_ge(s_ln["b"], e0 + c + 1)
                    if c + 1 == NCH:
                        pe.wait_ge(s_kraw, e0 + c)
                    to_channels(4, xnt[1]).then_inc(s_lnT["b"], 1)

                def b_project(c):
                    pe.wait_ge(s_lnC["b"], e0 + c + 1)
                    project_channels(4, BK, 0, xn3T)
                    project_channels(5, BK, 1, xn3T).then_inc(s_kb, 1)
                    if c + 1 < NCH:
                        pe.wait_ge(s_sig, f0 + c + 2)
                    else:
                        pe.wait_ge(s_vraw, e0 + c)
                    project_channels(6, BV, 0, xn3T)
                    project_channels(7, BV, 1, xn3T).then_inc(s_vb, 1)

                o_turn(0)
                o_project(0)
                o_turn(1)
                o_project(1)
                for c in range(NCH):
                    if 2 <= c + 1 < NCH:
                        o_turn(c + 1)
                    ln_turn(c)
                    if 2 <= c + 1 < NCH:
                        o_project(c + 1)
                    hidden(c)
                    if p == 0 and c >= 1:
                        b_turn(c - 1)
                    ffn_out(c)
                    if p == 0 and c >= 1:
                        b_project(c - 1)
                if p == 0:
                    b_turn(NCH - 1)
                    b_project(NCH - 1)

            with pe.Fori(0, B) as b:
                def a_turn(c):
                    e = b * NCH + c
                    pe.wait_ge(s_ln["a"], e + 1)
                    if c >= 2:
                        pe.wait_ge(s_nmax, e - 1)
                    to_channels(0, xnt_a[c % 2]).then_inc(s_lnT["a"], 1)

                a_turn(0)
                for c in range(NCH):
                    e = b * NCH + c
                    xc = xnT[:, :, c * CH + 1:c * CH + 1 + CH]
                    pe.wait_ge(s_lnC["a"], e + 1)
                    for i in range(4):
                        if c >= 1:
                            pe.wait_ge(s_r1, (e - 1) * 4 + i + 1)
                        project_channels(2 + i, WQ + i // 2, i % 2, xc).then_inc(s_qk, 1)
                    if c + 1 < NCH:
                        a_turn(c + 1)
                    if c >= 1:
                        pe.wait_ge(s_vcopy, e)
                    project_tokens(6, WV, xc).then_inc(s_v, 1)
                    pe.wait_ge(s_h, e * 4 + 4)
                    if c + 1 < NCH:
                        pe.wait_ge(s_lnC["a"], e + 2)
                    else:
                        pe.wait_ge(s_nmax, e)
                    for side in range(2):
                        for kt in range(KT):
                            last = pe.matmul(ps[0:H, side, :], head_sel[:, kt, :], sq_b[side * 2 + kt],
                                             start=(kt == 0), stop=(kt == KT - 1))
                    last.then_inc(s_nrm, 1)
                pe.wait_ge(s_flc, b + 1)
                held(pe)
                pe.matmul(ps[0:1, 0, 0:H], fl_col[:, :], ident[0:H, 0:H], start=True, stop=True).then_inc(s_flr, 1)
                pe.wait_ge(s_fl, b + 1)
                held(pe)
                attend("A", b)
                mix(b, 0)
                for c in range(NCH + 1):
                    e = b * NCH + c
                    if c < NCH:
                        pe.wait_ge(s_scan, e + 1)
                        if c == 0:
                            pe.wait_ge(s_x2, b * 2 * NCH + NCH)
                        else:
                            pe.wait_ge(s_kn, e)
                        to_tokens(0, kT[:, :, c * CH:(c + 1) * CH]).then_inc(s_kt, 1)
                        pe.wait_ge(s_vm, e + 1)
                        if c >= 1:
                            pe.wait_ge(s_vall, e)
                        to_tokens(2, v_mix).then_inc(s_vt, 1)
                    if c >= 1:
                        pe.wait_ge(s_kn, e)
                        if c == 1:
                            pe.wait_ge(s_vraw, (b + 1) * NCH)
                        for kt in range(KT):
                            if c >= 3:
                                pe.wait_ge(s_r1B, (e - 3) * 2 + kt + 1)
                            bk = 4 + 2 * ((c - 1) % 2) + kt
                            for tb in range(TB):
                                last = pe.transpose(ps[:, bk, tb * P:(tb + 1) * P],
                                                    kn_tok[:, tb, kt * P:(kt + 1) * P], ident[:, :])
                            last.then_inc(s_knT, 1)
                attend("B", b)
                mix(b, 1)

        @block.vector
        def _(dve):
            for a in "AB":
                dve.sem_inc(att[a]["o_free"], 2)
            dve.wait_ge(s_par, 6 * 16)
            nc.vector.tensor_scalar(head_row[:, 0, :], head_row[:, 0, :], KEY_SCALE_MAX / EXP_SCALING, None,
                                    ALU.min).then_inc(s_hp, 1)
            dve.wait_ge(s_hp, 4)
            nc.vector.tensor_tensor(head_row[:, 2, :], head_row[:, 0, :], head_row[:, 0, :],
                                    ALU.mult).then_inc(s_hp, 1)
            dve.wait_ge(s_hp, 5)
            nc.vector.tensor_scalar(flags["B"][:, 0:H], head_row[:, 2, :], SAFE, None, ALU.is_gt)
            nc.vector.tensor_reduce(fl_any[:, :], head_row[:, 2, :].rearrange("o (g j) -> o g j", j=HG), AX_X,
                                    ALU.max).then_inc(s_hp, 1)
            dve.wait_ge(s_hp, 6)
            nc.vector.tensor_scalar(flags["B"][:, H:H + NHG], fl_any[:, :], SAFE, None, ALU.is_gt)
            dve.wait_ge(s_hp_ps, 1)
            for kt in range(KT):
                nc.vector.tensor_copy(decay[:, kt:kt + 1], ps[:, 0, 2 * kt:2 * kt + 1])
                nc.vector.tensor_copy(v_coef[:, kt:kt + 1], ps[:, 0, 2 * kt + 1:2 * kt + 2])
            nc.vector.tensor_copy(scale_row[:, :, :].rearrange("p k h -> p (k h)"),
                                  ps[:, 1, 0:2 * H]).then_inc(s_setup, 1)
            dve.wait_ge(s_setup, 1)

            with dve.Fori(0, B) as b:
                steps = [0]

                def step(ins):
                    steps[0] += 1
                    ins.then_inc(s_dve, 1)

                def settle():
                    dve.wait_ge(s_dve, b * DVE_STEPS + steps[0])

                def rsqrt(n):
                    v, y, w = nw_v[:, 0:n], nw_y[:, 0:n], nw_u[:, 0:n]
                    step(nc.vector.tensor_scalar(y.bitcast(I32), v.bitcast(I32), 1, None, ALU.arith_shift_right))
                    settle()
                    step(nc.vector.tensor_scalar(y.bitcast(I32), y.bitcast(I32), -1.0, float(RSQRT_MAGIC), ALU.mult,
                                                 ALU.add))
                    settle()
                    for _ in range(3):
                        step(nc.vector.tensor_tensor(w, y, y, ALU.mult))
                        settle()
                        step(nc.vector.scalar_tensor_tensor(w, w, -0.5, v, ALU.mult, ALU.mult))
                        settle()
                        step(nc.vector.scalar_tensor_tensor(y, w, 1.5, y, ALU.add, ALU.mult))
                        settle()

                def layernorm(c, kind, n, dst, before):
                    for tb in range(TB):
                        step(nc.vector.bn_stats(ln_st[:, tb, :], x_res[:, TB * c + tb, :]))
                    settle()
                    held(dve)
                    for tb in range(TB):
                        step(nc.vector.bn_aggr(ln_mv[:, tb, :], ln_st[:, tb, :]))
                    settle()
                    step(nc.vector.tensor_scalar(nw_v[:, 0:TB], ln_mv[:, :, 1], EPS, None, ALU.add))
                    settle()
                    rsqrt(TB)
                    if before:
                        dve.wait_ge(s_lnT[kind], n + 1 - before)
                    for tb in range(TB):
                        last = nc.vector.tensor_scalar(dst[:, tb, :], x_res[:, TB * c + tb, :],
                                                       ln_mv[:, tb, 0:1], nw_y[:, tb:tb + 1], ALU.subtract, ALU.mult)
                    last.then_inc(s_ln[kind], 1)
                    dve.wait_ge(s_ln[kind], n + 1)

                def split_rest(bk, buf, high_ready, base, i, done, low_done, low_before):
                    dve.wait_ge(high_ready, base + i + 1)
                    if low_before:
                        dve.wait_ge(low_done, 2 * (base + i) - 2)
                    nc.vector.tensor_tensor(rest[i % 2], ps[:, bk, :], parts[buf][:, 0, :],
                                            ALU.subtract).then_inc(done, 1)

                def row_maxima(a, n):
                    sm = att[a]
                    for i, (qb, b0, nb) in enumerate(MAX_PIECES):
                        dve.wait_ge(sm["mx_scores"], n * NMP + i + 1)
                        w = min((b0 + nb) * CH, (qb + 1) * P) - b0 * CH
                        src = ps[:, GB * (i % 2):GB * (i % 2) + nb, :].rearrange("p a n -> p (a n)")[:, 0:w]
                        nc.vector.tensor_reduce(pmax[:, 1 if b0 else 0, qb:qb + 1], src, AX_X,
                                                ALU.max).then_inc(sm["mx_used"], 1)
                    dve.wait_ge(sm["mx_used"], (n + 1) * NMP)
                    nc.vector.tensor_tensor(row_max[:, :], pmax[:, 0, :], pmax[:, 1, :],
                                            ALU.max).then_inc(sm["mx_col"], 1)
                    dve.wait_ge(sm["mx_T"], n + 1)
                    mt = ps[0:NT, 6, 0:P]
                    nc.vector.tensor_scalar(m_part[0][:, :], mt, -1.0, None, ALU.mult).then_inc(sm["mx_step"], 1)
                    dve.wait_ge(sm["mx_step"], n * 3 + 1)
                    nc.vector.scalar_tensor_tensor(m_rest[:, :], mt, -1.0, m_part[0][:, :], ALU.mult,
                                                   ALU.subtract).then_inc(sm["mx_step"], 1)
                    dve.wait_ge(sm["mx_step"], n * 3 + 2)
                    nc.vector.tensor_copy(m_part[1][:, :], m_rest[:, :]).then_inc(sm["mx_step"], 1)
                    dve.wait_ge(sm["mx_step"], n * 3 + 3)
                    nc.vector.tensor_tensor(m_part[2][:, :], m_rest[:, :], m_part[1][:, :],
                                            ALU.subtract).then_inc(sm["mx_row"], 1)

                def attend(a):
                    sm = att[a]

                    def begin(hg):
                        inst = b * NHG + hg
                        grp = dve.value_load(flags[a][0:1, bass.ds(H + hg, 1)])
                        with dve.If(grp > 0):
                            for j in range(HG):
                                flag = dve.value_load(flags[a][0:1, bass.ds(hg * HG + j, 1)])
                                with dve.If(flag > 0):
                                    row_maxima(a, inst * HG + j)
                                with dve.Else():
                                    dve.sem_inc(sm["mx_used"], NMP)
                                    dve.sem_inc(sm["mx_col"], 1)
                                    dve.sem_inc(sm["mx_step"], 3)
                                    dve.sem_inc(sm["mx_row"], 1)
                        with dve.Else():
                            dve.sem_inc(sm["mx_used"], NMP * HG)
                            dve.sem_inc(sm["mx_col"], HG)
                            dve.sem_inc(sm["mx_step"], 3 * HG)
                            dve.sem_inc(sm["mx_row"], HG)

                    def output(hg, qc):
                        inst = b * NHG + hg
                        k = inst * NCH + qc
                        dve.wait_ge(sm["p_free"], P_FREE_0 + inst * NG + LAST_GROUP[qc] + 1)
                        nc.vector.tensor_copy(o_ev[:, qc % 2, :], ps[:, 6 + qc % 2, :]).then_inc(sm["o_ev"], 1)
                        dve.wait_ge(sm["o_T"], k + 1)
                        o = ps[:, 6 + qc % 2, :].rearrange("p (t j e) -> p t j e", t=TB, j=HG)
                        nc.vector.tensor_scalar(den[:, :, :], o[:, :, :, DK], 1.0e-37, None,
                                                ALU.max).then_inc(sm["o_step"], 1)
                        dve.wait_ge(sm["o_step"], k * 2 + 1)
                        nc.vector.reciprocal(rec[:, :, :], den[:, :, :]).then_inc(sm["o_step"], 1)
                        dve.wait_ge(sm["o_step"], k * 2 + 2)
                        dst = o_tok[:, TB * qc:TB * (qc + 1), bass.ds(hg * HG * DK, HG * DK)]
                        nc.vector.tensor_tensor(
                            dst.rearrange("p t (j e) -> p t j e", j=HG), o[:, :, :, 0:DK],
                            rec[:, :, :].unsqueeze(3).to_broadcast([P, TB, HG, DK]),
                            ALU.mult).then_inc(sm["o_free"], 1)

                    begin(0)
                    with dve.Fori(0, NHG // 2) as g:
                        for u in range(2):
                            hg = g * 2 + u
                            for qc in range(NCH - 1):
                                output(hg, qc)
                            if u == 0:
                                begin(hg + 1)
                            else:
                                with dve.If(g < NHG // 2 - 1):
                                    begin(at_most(hg + 1, NHG - 1))
                            output(hg, NCH - 1)

                def mix(p):
                    f0 = b * 2 * NCH + p * NCH

                    def chunk(c):
                        return x_res[:, TB * c:TB * (c + 1), :].rearrange("p t d -> p (t d)")

                    def attention_residual(c):
                        dve.wait_ge(s_oproj, f0 + c + 1)
                        nc.vector.tensor_tensor(chunk(c), chunk(c), bank2(2), ALU.add).then_inc(s_res, 1)
                        dve.wait_ge(s_res, f0 + c + 1)
                        layernorm(c, "ffn", f0 + c, xnt[0], min(c, 1))

                    def token_shift(c):
                        f = f0 + c
                        dve.wait_ge(s_diff, f + 1)
                        before = xnT[:, :, c * CH:c * CH + CH]
                        if c >= 1:
                            dve.wait_ge(s_rp, f)
                        for kt in range(KT):
                            last = nc.vector.scalar_tensor_tensor(x_k[:, kt, :], x_diff[:, kt, :], mu[:, 1, kt:kt + 1],
                                                                  before[:, kt, :], ALU.mult, ALU.add)
                        last.then_inc(s_xk, 1)
                        for kt in range(KT):
                            last = nc.vector.scalar_tensor_tensor(x_r[:, kt, :], x_diff[:, kt, :], mu[:, 0, kt:kt + 1],
                                                                  before[:, kt, :], ALU.mult, ALU.add)
                        last.then_inc(s_xr, 1)

                    def ffn_residual(c):
                        f = f0 + c
                        dve.wait_ge(s_fv, f + 1)
                        dve.wait_ge(s_sig, f + 1)
                        gate = r_gate.rearrange("p t d -> p (t d)")
                        step(nc.vector.tensor_tensor(gate, gate, bank2(0), ALU.mult))
                        settle()
                        nc.vector.tensor_tensor(chunk(c), chunk(c), gate, ALU.add).then_inc(s_x2, 1)
                        dve.wait_ge(s_x2, f + 1)

                    def b_layernorm(c):
                        layernorm(c, "b", b * NCH + c, xnt[1], min(c, 1))

                    attention_residual(0)
                    attention_residual(1)
                    for c in range(NCH):
                        token_shift(c)
                        if p == 0 and c >= 1:
                            b_layernorm(c - 1)
                        if 2 <= c + 1 < NCH:
                            attention_residual(c + 1)
                        ffn_residual(c)
                    if p == 0:
                        b_layernorm(NCH - 1)

                def a_layernorm(c):
                    dve.wait_ge(s_x[c], (b + 1) * 16)
                    layernorm(c, "a", b * NCH + c, xnt_a[c % 2], 2 if c >= 2 else 0)

                a_layernorm(0)
                a_layernorm(1)
                for c in range(NCH):
                    e = b * NCH + c
                    for i in range(4):
                        split_rest(2 + i, i, s_h, e * 4, i, s_r1, s_ml, low_before=(c >= 1 or i >= 2))
                    if c + 2 < NCH:
                        a_layernorm(c + 2)
                    dve.wait_ge(s_nrm, e + 1)
                    nc.vector.tensor_reduce(n_max[:, :, c:c + 1], ps[0:H, 0:2, :], AX_X, ALU.max).then_inc(s_nmax, 1)
                dve.wait_ge(s_nmax, (b + 1) * NCH)
                step(nc.vector.tensor_reduce(n_top[:, :], n_max[:, :, :], AX_X, ALU.max))
                settle()
                step(nc.vector.tensor_tensor(fl_prod[:, :], n_top[:, 0:1], n_top[:, 1:2], ALU.mult))
                settle()
                nc.vector.tensor_scalar(fl_col[:, :], fl_prod[:, :], 1.1 * SCALE["A"] ** 2, SAFE * SAFE, ALU.mult,
                                        ALU.is_gt).then_inc(s_flc, 1)
                dve.wait_ge(s_flr, b + 1)
                nc.vector.tensor_copy(flags["A"][:, 0:H], ps[0:1, 0, 0:H])
                step(nc.vector.tensor_reduce(fl_any[:, :], ps[0:1, 0, 0:H].rearrange("o (g j) -> o g j", j=HG), AX_X,
                                             ALU.max))
                settle()
                held(dve)
                nc.vector.tensor_copy(flags["A"][:, H:H + NHG], fl_any[:, :]).then_inc(s_fl, 1)
                dve.wait_ge(s_fl, b + 1)
                held(dve)
                attend("A")
                mix(0)
                def scan(c):
                    e = b * NCH + c
                    cols = slice(c * CH, (c + 1) * CH)
                    dve.wait_ge(s_kraw, e + 1)
                    if c >= 1:
                        dve.wait_ge(s_scan, e)
                    for kt in range(KT):
                        last = nc.vector.tensor_tensor_scan(
                            kT[:, kt, cols], decay[:, kt:kt + 1].to_broadcast([P, CH]), kT[:, kt, cols],
                            0.0 if c == 0 else kT[:, kt, c * CH - 1:c * CH], ALU.mult, ALU.add)
                    last.then_inc(s_scan, 1)

                def mix_values(c):
                    e = b * NCH + c
                    dve.wait_ge(s_vd, e + 1)
                    if c >= 1:
                        dve.wait_ge(s_vt, e)
                    n = CH if c + 1 < NCH else CH - 1
                    for kt in range(KT):
                        last = nc.vector.scalar_tensor_tensor(
                            v_mix[:, kt, 0:n], v_diff[:, kt, 0:n], v_coef[:, kt:kt + 1],
                            vT[:, kt, c * CH + 1:c * CH + 1 + n], ALU.mult, ALU.add)
                        if n < CH:
                            last = nc.vector.tensor_scalar(v_mix[:, kt, n:CH], v_diff[:, kt, n:CH],
                                                           v_coef[:, kt:kt + 1], None, ALU.mult)
                    last.then_inc(s_vm, 1)

                def norm(c):
                    e = b * NCH + c
                    nh = TB * H
                    for side, (ready, sq) in enumerate(((s_sqk, sq_k), (s_sqv, sq_v))):
                        dve.wait_ge(ready, e + 1)
                        step(nc.vector.tensor_reduce(nw_v[:, side * nh:(side + 1) * nh],
                                                     sq.rearrange("p (g e) -> p g e", e=DK), AX_X, ALU.add))
                    settle()
                    step(nc.vector.tensor_scalar(nw_v[:, :], nw_v[:, :], 1.0e-30, None, ALU.max))
                    settle()
                    rsqrt(P)
                    step(nc.vector.tensor_tensor(nw_u[:, :], nw_v[:, :], nw_y[:, :], ALU.mult))
                    settle()
                    step(nc.vector.tensor_scalar(nw_u[:, :], nw_u[:, :], NORM_EPS, None, ALU.add))
                    settle()
                    step(nc.vector.reciprocal(nw_y[:, :], nw_u[:, :]))
                    settle()
                    for side in range(2):
                        fac = nw_y[:, side * nh:(side + 1) * nh].rearrange("p (t h) -> p t h", t=TB)
                        step(nc.vector.tensor_tensor(fac, fac, scale_row[:, side, :].unsqueeze(1)
                                                     .to_broadcast([P, TB, H]), ALU.mult))
                    settle()
                    if c >= 1:
                        dve.wait_ge(s_knT, 2 * e)
                    for side, (dst, done) in enumerate(((kn_tok, s_kn), (v_all[:, TB * c:TB * (c + 1), :], s_vall))):
                        last = nc.vector.tensor_tensor(
                            dst.rearrange("p t (h e) -> p (t h) e", e=DK),
                            bank2(2 * side).rearrange("p (g e) -> p g e", e=DK),
                            nw_y[:, side * nh:(side + 1) * nh].unsqueeze(2).to_broadcast([P, nh, DK]), ALU.mult)
                        last.then_inc(done, 1)

                def split_keys(c):
                    e = b * NCH + c
                    buf = 2 * (c % 2)
                    for i in range(2):
                        split_rest(4 + buf + i, buf + i, s_hB, e * 2, i, s_r1B, s_mlB, low_before=(c >= 1))

                scan(0)
                mix_values(0)
                scan(1)
                mix_values(1)
                for c in range(NCH):
                    norm(c)
                    if c + 2 < NCH:
                        scan(c + 2)
                    if c >= 1:
                        split_keys(c - 1)
                    if c + 2 < NCH:
                        mix_values(c + 2)
                split_keys(NCH - 1)
                attend("B")
                mix(1)
                assert steps[0] <= DVE_STEPS
                dve.sem_inc(s_dve, DVE_STEPS - steps[0])


_WEIGHTS = ["L0_attn_a_q_proj", "L0_attn_a_k_proj", "L0_attn_a_v_proj", "L0_attn_a_o_proj", "L0_ffn_W_r", "L0_ffn_W_k",
            "L0_ffn_W_v", "L0_attn_b_W_k", "L0_attn_b_W_v", "L0_attn_b_W_c"]
_OTHERS = {"X": "L0_attn_a_X", "beta": "L0_attn_b_leaky_key_beta", "key_scale": "L0_attn_b_key_scale",
           "v_coef": "L0_attn_b_v_coef", "val_scale": "L0_attn_b_val_scale", "mu_r": "L0_ffn_mu_r",
           "mu_k": "L0_ffn_mu_k"}


def kernel(**inputs):
    import numpy as _np
    import concourse.bacc as _bacc
    from concourse import mybir as _mybir
    from concourse.bass_utils import run_bass_kernel_spmd as _run

    nc = _bacc.Bacc("TRN2", target_bir_lowering=False, num_devices=1)
    arrays, aps = {}, {}
    for name in _WEIGHTS + list(_OTHERS.values()):
        a = _np.ascontiguousarray(inputs[name])
        arrays[f"in_{name}"] = a
        aps[name] = nc.dram_tensor(f"in_{name}", a.shape, _mybir.dt.from_np(a.dtype), kind="ExternalInput").ap()
    out = nc.dram_tensor("out_0", (B, S, D), F32, kind="ExternalOutput").ap()
    tensors = {short: aps[name] for short, name in _OTHERS.items()}
    tensors["weights"] = [aps[name] for name in _WEIGHTS]
    hybrid_kernel(nc, tensors, out)
    r = _run(nc, [arrays], core_ids=[0])
    return r.results[0]["out_0"]
```

```python
from contextlib import ExitStack

import concourse.bass as bass
from concourse import mybir

F32 = mybir.dt.float32
BF16 = mybir.dt.bfloat16
I32 = mybir.dt.int32
ACT = mybir.ActivationFunctionType
ALU = mybir.AluOpType
AX_X = mybir.AxisListType.X

P = 128
B, S, D, H = 4, 2048, 256, 16
DK = D // H
KT = D // P
NT = S // P
CH = 512
NCH = S // CH
TB = CH // P
HG = 4
NHG = H // HG
HS = 32
EPS = 1e-5
NORM_EPS = 1e-10
SCALE = {"A": DK ** -0.5, "B": 1.0}
EXP_SCALING = 10.0
KEY_SCALE_MAX = 11.090339630053647
SAFE = 64.0
NEG = -1.0e30
FLOOR = -1.0e20
K_PART = (0, 1, 2, 0, 1, 0)
Q_PART = (0, 0, 0, 1, 1, 2)
PART_RUNS = ((0, 0, 0, 3), (0, 3, 0, 2), (0, 5, 0, 1), (1, 0, 0, 1), (1, 1, 0, 1), (1, 2, 0, 2), (1, 4, 1, 2))
assert all((K_PART, Q_PART)[_s][_r:_r + _n] == tuple(range(_p, _p + _n)) for _s, _r, _p, _n in PART_RUNS)
MROW = DK * len(K_PART)
KROWS = MROW + 3
RSQRT_MAGIC = 0x5F3759DF

WQ, WK, WV, WO, FR, FK, FV, BK, BV, BC = range(10)



def score_banks():
    banks = []
    for qc in range(NCH):
        for kb in range(TB * qc):
            for j in range(HG):
                banks.append([(qc, kb, j, 0, CH, 0)])
        d = TB * qc
        for j in range(HG):
            banks.append([(qc, d, j, 0, CH, 0)])
        for j in range(HG):
            banks.append([(qc, d + 1, j, P, 3 * P, 0), (qc, d + 3, j, 3 * P, P, 3 * P)])
        for j in range(0, HG, 2):
            banks.append([(qc, d + 2, j, 2 * P, 2 * P, 0), (qc, d + 2, j + 1, 2 * P, 2 * P, 2 * P)])
    return banks


GB = 2
NS_BUF = 3
NP_BUF = 6
BANKS = score_banks()
GROUPS = [BANKS[0:1], BANKS[1:2]] + [BANKS[i:i + GB] for i in range(2, len(BANKS), GB)]
NG = len(GROUPS)
GROUP_END = [sum(len(grp) for grp in GROUPS[:g + 1]) for g in range(NG)]
BANK_AT = [(g, n) for g, grp in enumerate(GROUPS) for n in range(len(grp))]
DIAG = [[(g, grp[0][-1][5], len(grp[0])) for g, grp in enumerate(GROUPS) if grp[0][0][0] == qc and grp[0][0][1] >= TB * qc]
        for qc in range(NCH)]
DIAG_GROUPS = [g for groups in DIAG for g, _, _ in groups]
ND = len(DIAG_GROUPS)
P_FREE_0 = 2 * NG


def value_sets():
    sets = {}
    for i, bk in enumerate(BANKS):
        for unit in bk:
            sets.setdefault(unit[0:2], []).append((i, unit))
    order = sorted(sets.values(), key=lambda st: (st[-1][0], st[0][1][1]))
    result, freed = [], 0
    for n, st in enumerate(order):
        left = min([i for later in order[n + 1:] for i, _ in later], default=len(BANKS))
        used = sum(end <= left for end in GROUP_END)
        result.append((st, BANK_AT[st[-1][0]][0], used - freed))
        freed = used
    return result


VALUE_SETS = value_sets()
LAST_GROUP = [max(BANK_AT[i][0] for st, _, _ in VALUE_SETS for i, u in st if u[0] == qc) for qc in range(NCH)]
TURN_GROUP = [g + 4 for g in LAST_GROUP]
LOADS = len(PART_RUNS) + 2
FIRST_LOADS = [LOADS] + [len(PART_RUNS)] * (NCH - 1)


assert NG % NS_BUF == 0 and 2 * NG % NP_BUF == 0

MAX_GB = 2
MAX_BUF = NS_BUF * GB // MAX_GB
assert MAX_GB == GB
MAX_PIECES = []
for _qb in range(NT):
    _n = _qb // TB + 1
    MAX_PIECES.append((_qb, 0, min(_n, MAX_GB)))
    if _n > MAX_GB:
        MAX_PIECES.append((_qb, MAX_GB, _n - MAX_GB))
NMP = len(MAX_PIECES)

FIRST_O = [LAST_GROUP[NCH - 2] + 6, LAST_GROUP[NCH - 2] + 9]
FIRST_PROJ = [LAST_GROUP[NCH - 2] + 12, LAST_GROUP[NCH - 2] + 14]
FIRST_LN = [LAST_GROUP[NCH - 2] + 24, LAST_GROUP[NCH - 2] + 27]
FIRST_BANK = 6 + NCH % 2
assert FIRST_LN[1] + 2 < NG

DVE_STEPS = 1024


def hybrid_kernel(nc, t, out):
    with ExitStack() as ctx:
        def sb(name, shape, dt=F32):
            return ctx.enter_context(nc.sbuf_tensor(name, shape, dt))

        def sem(name):
            return ctx.enter_context(nc.semaphore(name))

        part_d = {"A": nc.dram_tensor("part_a", (2, 3 * DK, H, S), BF16, kind="Internal").ap(),
                  "B": nc.dram_tensor("part_b", (1, 3 * DK, H, S), BF16, kind="Internal").ap()}
        rows_d = nc.dram_tensor("max_rows", (2, 3, HG * S), BF16, kind="Internal").ap()

        wT = sb("wT", [P, 10, KT, D])
        x_res = sb("x_res", [P, NT, D])
        xnT = sb("xnT", [P, KT, S + 4])
        v_all = sb("v_all", [P, NT, D])
        o_tok = sb("o_tok", [P, NT, D])
        stage = sb("stage", [P, 4, HG * S], BF16)
        v_st = sb("v_st", [P, 2, NT, HG, HS])
        probs = sb("probs", [P, NP_BUF, GB * CH])
        last_parts = sb("last_parts", [P, 2, 3, CH], BF16)
        o_ev = sb("o_ev", [P, 2, CH])
        ident = sb("ident", [P, P])
        ident_b = sb("ident_b", [P, P], BF16)
        mask_qk = {a: sb(f"mask_qk_{a}", [P, P], BF16) for a in "AB"}
        mask_kq = {a: sb(f"mask_kq_{a}", [P, P], BF16) for a in "AB"}
        head_sel = sb("head_sel", [P, KT, H], BF16)
        sel_ch = sb("sel_ch", [H, D])
        ones_row = sb("ones_row", [1, P])
        head_col = sb("head_col", [H, 2])
        head_row = sb("head_row", [1, 3, H])
        scale_row = sb("scale_row", [P, 2, H])
        decay = sb("decay", [P, KT])
        v_coef = sb("v_coef", [P, KT])
        mu = sb("mu", [P, 2, KT])
        ln_st = sb("ln_st", [P, TB, 6])
        ln_mv = sb("ln_mv", [P, TB, 2])
        nw_v = sb("nw_v", [P, P])
        nw_y = sb("nw_y", [P, P])
        v_fac = sb("v_fac", [P, 2, TB * H])
        nw_u = sb("nw_u", [P, P])
        n_max = sb("n_max", [H, 2, NCH])
        n_top = sb("n_top", [H, 2])
        fl_prod = sb("fl_prod", [H, 1])
        fl_col = sb("fl_col", [H, 1])
        fl_any = sb("fl_any", [1, NHG])
        flags = {a: sb(f"flags_{a}", [1, H + NHG], I32) for a in "AB"}
        den = sb("den", [P, TB, HG])
        rec = sb("rec", [P, TB, HG])
        pmax = sb("pmax", [P, 2, NT])
        row_max = sb("row_max", [P, NT])
        m_part = [sb(f"m_part{i}", [NT, P], BF16) for i in range(3)]
        m_rest = sb("m_rest", [NT, P])

        def f32_view(ap):
            return ap.bitcast(F32)

        low = f32_view(stage[:, 0:2, :].rearrange("p a n -> p (a n)"))
        high = f32_view(stage[:, 2:4, :].rearrange("p a n -> p (a n)"))

        def low_buf(i):
            return low[:, i * 1024:(i + 1) * 1024]

        xnt = [low_buf(i).rearrange("p (t d) -> p t d", t=TB) for i in range(2)]
        x_r = low_buf(2).rearrange("p (k n) -> p k n", k=KT)
        first_oT = x_r
        x_k = low_buf(3).rearrange("p (k n) -> p k n", k=KT)
        k_act = low_buf(4).rearrange("p (k n) -> p k n", k=KT)
        r_gate = low_buf(5).rearrange("p (t d) -> p t d", t=TB)
        x_diff = low_buf(6).rearrange("p (k n) -> p k n", k=KT)
        xn3T = low_buf(7).rearrange("p (k n) -> p k n", k=KT)
        kT = high[:, 0:KT * S].rearrange("p (k n) -> p k n", k=KT)
        vT = high[:, KT * S:2 * KT * S].rearrange("p (k n) -> p k n", k=KT)
        w_nat = high[:, 0:10 * 512].rearrange("p (w m d) -> p w m d", w=10, m=KT)

        xnt_a = [o_tok[:, TB * i:TB * (i + 1), :] for i in range(2)]
        sq_k, sq_v = (o_tok[:, TB * i:TB * (i + 1), :].rearrange("p t d -> p (t d)") for i in range(2))
        v_mix = o_tok[:, 3 * TB:4 * TB, :].rearrange("p t d -> p (t d)").rearrange("p (k n) -> p k n", k=KT)

        pf = probs[:, :, :].rearrange("p a n -> p (a n)")
        parts = [pf[:, at:at + 768].bitcast(BF16).rearrange("p (r n) -> p r n", r=3) for at in (0, 768)]
        parts += [last_parts[:, i] for i in range(2)]
        oT = pf[:, 1536:2560].rearrange("p (k n) -> p k n", k=KT)
        v_diff = oT
        sq_b = [pf[:, 3072 + i * 256:3328 + i * 256].bitcast(BF16) for i in range(4)]
        kn_tok = [o_tok[:, 2 * TB:3 * TB, :],
                  pf[:, 3072:4096].rearrange("p (t d) -> p t d", t=TB)]
        rest = [pf[:, 4096 + i * CH:4096 + (i + 1) * CH] for i in range(2)]

        ps = ctx.enter_context(nc.psum_tensor("ps", [P, 8, CH], F32))

        def bank2(i):
            return ps[:, i:i + 2, :].rearrange("p a n -> p (a n)")

        def ffn_bank(p, c):
            return 6 if p == 1 and c + 1 < NCH else 2

        def tok_bank(bk0, tb):
            return ps[:, bk0 + tb // 2, (tb % 2) * D:(tb % 2 + 1) * D]

        s_w = [sem(f"weight_loaded{i}") for i in range(10)]
        s_par = sem("params_loaded")
        s_rows_set = sem("max_rows_set")
        s_rows = sem("max_rows_stored")
        s_ident = sem("identity_built")
        s_const = sem("constants_built")
        s_pool = sem("pool_step")
        s_wt_ps = sem("weight_transposed")
        s_wt = sem("weight_copied")
        s_hp_ps = sem("head_params_in_psum")
        s_hp = sem("head_params_step")
        s_setup = sem("setup_done")
        s_x = [sem(f"x_loaded{c}") for c in range(NCH)]
        s_dve = sem("vector_step")
        s_ln = {k: sem(f"ln_{k}_ready") for k in ("a", "ffn", "b")}
        s_lnT = {k: sem(f"ln_{k}_transposed") for k in ("a", "ffn", "b")}
        s_lnC = {k: sem(f"ln_{k}_channel_major") for k in ("a", "ffn", "b")}
        s_qk = sem("qk_in_psum")
        s_h = sem("qk_high_part")
        s_r1 = sem("qk_rest")
        s_mid = sem("qk_mid_part")
        s_low = sem("qk_low_part")
        s_parts = [sem(f"qk_stored{i}") for i in range(4)]
        s_v = sem("v_in_psum")
        s_vcopy = sem("v_copied")
        s_nrm = sem("norms_in_psum")
        s_nmax = sem("norm_max")
        s_flc = sem("flag_column")
        s_flr = sem("flag_row")
        s_fl = sem("flags_ready")
        s_first_oT = sem("first_o_transposed")
        s_first_oC = sem("first_o_channel_major")
        s_first_proj = sem("first_o_projected")
        s_first_res = sem("first_residual")
        s_first_lnT = sem("first_ln_transposed")
        s_first_lnC = sem("first_ln_channel_major")
        s_oTp = sem("o_transposed")
        s_oTc = sem("o_channel_major")
        s_oproj = sem("o_projected")
        s_res = sem("attention_residual")
        s_diff = sem("shift_difference")
        s_xr = sem("x_r_ready")
        s_xk = sem("x_k_ready")
        s_rp = sem("r_in_psum")
        s_sig = sem("r_gate_ready")
        s_kp = sem("k_in_psum")
        s_relu = sem("k_relu")
        s_kact = sem("k_squared")
        s_fv = sem("ffn_in_psum")
        s_gated = sem("ffn_gated")
        s_x2 = sem("ffn_residual")
        s_kb = sem("b_keys_in_psum")
        s_kraw = sem("b_keys_copied")
        s_vb = sem("b_values_in_psum")
        s_vraw = sem("b_values_copied")
        s_scan = sem("b_keys_decayed")
        s_vd = sem("b_value_difference")
        s_vm = sem("b_values_mixed")
        s_kt = sem("b_keys_token_major")
        s_vt = sem("b_values_token_major")
        s_sqk = sem("b_key_squares")
        s_sqv = sem("b_value_squares")
        s_kn = sem("b_keys_normed")
        s_vall = sem("b_values_normed")
        s_vtok = sem("b_values_in_place")
        s_ktok = sem("b_keys_in_place")
        s_len = sem("b_lengths")
        s_vfac = sem("b_value_factors")
        s_knT = sem("b_keys_channel_major")
        s_hB = sem("b_key_high_part")
        s_r1B = sem("b_key_rest")
        s_midB = sem("b_key_mid_part")
        s_lowB = sem("b_key_low_part")
        s_partsB = [sem(f"b_key_stored{i}") for i in range(4)]
        s_out = [sem(f"out_stored{c}") for c in range(NCH)]
        s_held = sem("wait_passed")
        att = {}
        for a in "AB":
            att[a] = {n: sem(f"{n}_{a}") for n in (
                "kq0", "kq1", *(f"kq_first{c}" for c in range(NCH)), "scores", "probs", "p_free", "vst",
                "masked", "o_ev", "o_T", "o_free", "o_step", "mx_scores", "mx_used", "mx_col", "mx_T", "mx_step", "mx_row",
                "mx_dma")}

        def held(eng):
            eng.sem_inc(s_held, 1)

        def at_most(value, high):
            return nc.s_assert_within(value, 0, high, skip_runtime_bounds_check_because="the branch excludes the last pass")

        block = ctx.enter_context(nc.Block())

        @block.sync
        def _(sp):
            x_d = t["X"].rearrange("b (c t p) d -> b c p t d", p=P, t=TB)
            out_d = out.rearrange("b (c t p) d -> b c p t d", p=P, t=TB)
            for i, name in enumerate(t["weights"]):
                sp.dma_start(w_nat[:, i], name.rearrange("(m p) d -> p m d", p=P)).then_inc(s_w[i], 16)
            for c in range(NCH):
                sp.dma_start(x_res[:, TB * c:TB * (c + 1), :], x_d[0, c]).then_inc(s_x[c], 16)
            sp.dma_start(mu[:, 0, :], t["mu_r"].rearrange("(k p) -> p k", p=P),
                         allow_slow_non_contiguous=True).then_inc(s_par, 16)
            sp.dma_start(mu[:, 1, :], t["mu_k"].rearrange("(k p) -> p k", p=P),
                         allow_slow_non_contiguous=True).then_inc(s_par, 16)
            col = "a h b c -> h (a b c)"
            row = "a h b c -> (a b c) h"
            sp.dma_start(head_col[:, 0:1], t["beta"].rearrange(col)).then_inc(s_par, 16)
            sp.dma_start(head_col[:, 1:2], t["v_coef"].rearrange(col)).then_inc(s_par, 16)
            sp.dma_start(head_row[:, 0, :], t["key_scale"].rearrange(row)).then_inc(s_par, 16)
            sp.dma_start(head_row[:, 1, :], t["val_scale"].rearrange(row)).then_inc(s_par, 16)
            sp.wait_ge(s_rows_set, 1)
            sp.dma_start(rows_d[0], stage[0:3, 0, :]).then_inc(s_rows, 16)
            sp.dma_start(rows_d[1], stage[0:3, 1, :]).then_inc(s_rows, 16)
            sp.wait_ge(s_rows, 32)

            def load_parts(a, u, hg, cols, done):
                for side, r, part, n in PART_RUNS:
                    src = part_d[a][(1 - side) if a == "A" else 0, part * DK:(part + n) * DK,
                                    bass.ds(hg * HG, HG), cols]
                    dst = stage[r * DK:(r + n) * DK, 2 * u + side, :].rearrange("e (j n) -> e j n", j=HG)[:, :, cols]
                    sp.dma_start(dst, src).then_inc(att[a][done], 16)

            def load_rows(a, u, done):
                for side in range(2):
                    sp.dma_start(stage[MROW:KROWS, 2 * u + side, :], rows_d[side]).then_inc(att[a][done], 16)

            def load_group(a, u, hg, inst):
                sp.wait_ge(att[a]["p_free"], (inst + 1) * NG)
                held(sp)
                load_parts(a, u, hg, slice(0, S), f"kq{u}")
                load_rows(a, u, f"kq{u}")

            def maxima_rows(a, u, hg, inst):
                sm = att[a]
                grp = sp.value_load(flags[a][0:1, bass.ds(H + hg, 1)])
                with sp.If(grp > 0):
                    for j in range(HG):
                        flag = sp.value_load(flags[a][0:1, bass.ds(hg * HG + j, 1)])
                        with sp.If(flag > 0):
                            sp.wait_ge(sm["mx_row"], inst * HG + j + 1)
                            for r in range(3):
                                sp.dma_start(stage[MROW + r:MROW + r + 1, 2 * u + 1, j * S:(j + 1) * S]
                                             .rearrange("o (t q) -> o t q", t=NT),
                                             m_part[r][:, :]).then_inc(sm["mx_dma"], 16)
                        with sp.Else():
                            sp.sem_inc(sm["mx_dma"], 48)
                with sp.Else():
                    sp.sem_inc(sm["mx_dma"], 48 * HG)

            def attend(a, b):
                with sp.Fori(0, NHG // 2) as g:
                    inst = b * NHG + g * 2
                    maxima_rows(a, 0, g * 2, inst)
                    load_group(a, 1, g * 2 + 1, inst + 1)
                    maxima_rows(a, 1, g * 2 + 1, inst + 1)
                    with sp.If(g < NHG // 2 - 1):
                        load_group(a, 0, at_most(g * 2 + 2, NHG - 1), inst + 2)

            def store_part(a, side, m, i, c, done):
                for r in range(3):
                    sp.dma_start(part_d[a][side, r * DK:(r + 1) * DK, m * (H // KT):(m + 1) * (H // KT),
                                           c * CH:(c + 1) * CH].rearrange("e h n -> h e n"),
                                 parts[i][:, r, :]).then_inc(done, 16)

            def load_x(b, c):
                sp.dma_start(x_res[:, TB * c:TB * (c + 1), :],
                             x_d[bass.ds(b, 1), c].rearrange("o p t d -> (o p) t d")).then_inc(s_x[c], 16)

            with sp.Fori(0, B) as b:
                load_rows("A", 0, "kq_first0")
                for c in range(NCH):
                    for i in range(4):
                        sp.wait_ge(s_low, (b * NCH + c) * 4 + i + 1)
                        store_part("A", i % 2, i // 2, i, c, s_parts[i])
                        if i == (1 if c + 1 == NCH else 3):
                            for side in range(2):
                                sp.wait_ge(s_parts[side], (b * NCH + c + 1) * 48)
                            load_parts("A", 0, 0, slice(c * CH, (c + 1) * CH), f"kq_first{c}")
                for i in range(4):
                    sp.wait_ge(s_parts[i], (b + 1) * NCH * 48)
                sp.wait_ge(s_fl, b + 1)
                held(sp)
                attend("A", b)
                sp.wait_ge(s_kraw, (b + 1) * NCH)
                sp.wait_ge(s_x2, b * 2 * NCH + NCH)
                held(sp)
                load_rows("B", 0, "kq_first0")
                for c in range(NCH):
                    for i in range(2):
                        sp.wait_ge(s_lowB, (b * NCH + c) * 2 + i + 1)
                        buf = 2 * (c % 2) + i
                        store_part("B", 0, i, buf, c, s_partsB[buf])
                        if i == (0 if c + 1 == NCH else 1):
                            sp.wait_ge(s_partsB[2 * (c % 2)], (b * 2 + c // 2 + 1) * 48)
                            load_parts("B", 0, 0, slice(c * CH, (c + 1) * CH), f"kq_first{c}")
                for i in (1, 3):
                    sp.wait_ge(s_partsB[i], (b + 1) * 96)
                sp.wait_ge(s_vall, (b + 1) * NCH)
                held(sp)
                attend("B", b)
                for c in range(NCH):
                    sp.wait_ge(s_x2, b * 2 * NCH + NCH + c + 1)
                    sp.dma_start(out_d[bass.ds(b, 1), c].rearrange("o p t d -> (o p) t d"),
                                 x_res[:, TB * c:TB * (c + 1), :]).then_inc(s_out[c], 16)
                    with sp.If(b < B - 1):
                        sp.wait_ge(s_out[c], (b + 1) * 16)
                        load_x(at_most(b + 1, B - 1), c)
            for c in range(NCH):
                sp.wait_ge(s_out[c], B * 16)

        @block.gpsimd
        def _(pool):
            steps = [0]

            def step(ins):
                steps[0] += 1
                ins.then_inc(s_pool, 1)

            def settle():
                pool.wait_ge(s_pool, steps[0])

            step(pool.memset(ident[:, :], 0.0))
            settle()
            pool.affine_select(out=ident[:, :], in_=ident[:, :], compare_op=ALU.not_equal, fill=1.0, base=0,
                               pattern=[[-1, P]], channel_multiplier=1).then_inc(s_ident, 1)
            pool.wait_ge(s_ident, 1)
            step(pool.memset(stage[0:3, 0, :], 1.0))
            step(pool.memset(stage[0:3, 1, :], 0.0))
            settle()
            pool.sem_inc(s_rows_set, 1)
            for m in (mask_qk, mask_kq):
                for a in "AB":
                    step(pool.memset(m[a][:, :], 0.0))
            step(pool.memset(head_sel[:, :, :], 1.0))
            step(pool.memset(sel_ch[:, :], 1.0))
            step(pool.memset(ones_row[:, :], 1.0))
            step(pool.memset(xnT[:, :, 0:1], 0.0))
            step(pool.memset(pmax[:, :, :], FLOOR))
            settle()
            for m, sign in ((mask_qk, 1), (mask_kq, -1)):
                for a, op in (("A", ALU.is_ge), ("B", ALU.is_gt)):
                    step(pool.affine_select(out=m[a][:, :], in_=m[a][:, :], compare_op=op, fill=NEG, base=0,
                                            pattern=[[-sign, P]], channel_multiplier=sign))
            step(pool.affine_select(out=head_sel[:, :, :], in_=head_sel[:, :, :], compare_op=ALU.is_ge, fill=0.0,
                                    base=0, pattern=[[P, KT], [-DK, H]], channel_multiplier=1))
            step(pool.affine_select(out=sel_ch[:, :], in_=sel_ch[:, :], compare_op=ALU.is_ge, fill=0.0, base=0,
                                    pattern=[[1, D]], channel_multiplier=-DK))
            settle()
            step(pool.affine_select(out=head_sel[:, :, :], in_=head_sel[:, :, :], compare_op=ALU.is_ge, fill=0.0,
                                    base=DK - 1, pattern=[[-P, KT], [DK, H]], channel_multiplier=-1))
            step(pool.affine_select(out=sel_ch[:, :], in_=sel_ch[:, :], compare_op=ALU.is_ge, fill=0.0,
                                    base=DK - 1, pattern=[[-1, D]], channel_multiplier=DK))
            step(pool.tensor_copy(ident_b[:, :], ident[:, :]))
            settle()
            pool.sem_inc(s_const, 1)
            step(pool.memset(v_st[:, :, :, :, :].rearrange("p u t j e -> p (u t j) e"), 0.0))
            settle()
            step(pool.memset(v_st[:, :, :, :, DK:DK + 1].rearrange("p u t j e -> p (u t j) e"), 1.0))
            settle()

            def low_part(mid_ready, base, i, buf, done):
                pool.wait_ge(mid_ready, base + i + 1)
                pool.tensor_tensor(parts[buf][:, 2, :], rest[i % 2], parts[buf][:, 1, :],
                                   ALU.subtract).then_inc(done, 1)

            def attend(a, b, g):
                sm = att[a]
                for u in range(2):
                    inst = b * NHG + g * 2 + u
                    pool.wait_ge(sm["p_free"], (inst + 1) * NG)
                    held(pool)
                    for c in range(NCH):
                        pool.tensor_copy(
                            v_st[:, u, TB * c:TB * (c + 1), :, 0:DK],
                            v_all[:, TB * c:TB * (c + 1), bass.ds((g * 2 + u) * HG * DK, HG * DK)]
                            .rearrange("p t (j e) -> p t j e", j=HG)).then_inc(sm["vst"], 1)

            def mix(b, p):
                for c in range(NCH):
                    f = b * 2 * NCH + p * NCH + c
                    pool.wait_ge(s_lnC["ffn"], f + 1)
                    now, before = xnT[:, :, c * CH + 1:c * CH + 1 + CH], xnT[:, :, c * CH:c * CH + CH]
                    if c >= 1:
                        pool.wait_ge(s_xr, f)
                    for kt in range(KT):
                        pool.tensor_tensor(x_diff[:, kt, :], now[:, kt, :], before[:, kt, :],
                                           ALU.subtract).then_inc(s_diff, 1)
                    pool.wait_ge(s_relu, f + 1)
                    pool.tensor_tensor(k_act, k_act, k_act, ALU.mult).then_inc(s_kact, 1)

            with pool.Fori(0, B) as b:
                def low_keys(c):
                    for i in range(2):
                        low_part(s_midB, (b * NCH + c) * 2, i, 2 * (c % 2) + i, s_lowB)

                for c in range(NCH):
                    for i in range(4):
                        low_part(s_mid, (b * NCH + c) * 4, i, i, s_low)
                pool.wait_ge(s_vcopy, (b + 1) * NCH)
                held(pool)
                with pool.Fori(0, NHG // 2) as g:
                    attend("A", b, g)
                mix(b, 0)
                for c in range(NCH):
                    e = b * NCH + c
                    pool.wait_ge(s_vraw, b * NCH + min(c + 2, NCH))
                    held(pool)
                    if c >= 1:
                        pool.wait_ge(s_vm, e)
                        held(pool)
                    n = CH if c + 1 < NCH else CH - 1
                    if c + 1 == NCH:
                        pool.tensor_copy(v_diff[:, :, n:CH], vT[:, :, S - 1:S])
                    pool.tensor_tensor(v_diff[:, :, 0:n], vT[:, :, c * CH:c * CH + n],
                                       vT[:, :, c * CH + 1:c * CH + 1 + n], ALU.subtract).then_inc(s_vd, 1)
                for c in range(NCH):
                    if c >= 1:
                        low_keys(c - 1)
                    e = b * NCH + c
                    pool.wait_ge(s_vtok, e + 1)
                    held(pool)
                    pool.wait_ge(s_vfac, e + 1)
                    held(pool)
                    v_chunk = v_all[:, TB * c:TB * (c + 1), :].rearrange("p t (h e) -> p (t h) e", e=DK)
                    pool.tensor_tensor(v_chunk, v_chunk, v_fac[:, c % 2, :].unsqueeze(2)
                                       .to_broadcast([P, TB * H, DK]), ALU.mult).then_inc(s_vall, 1)
                low_keys(NCH - 1)
                pool.wait_ge(s_vall, (b + 1) * NCH)
                held(pool)
                with pool.Fori(0, NHG // 2) as g:
                    attend("B", b, g)
                mix(b, 1)

        @block.scalar
        def _(act):
            for i in range(10):
                act.wait_ge(s_wt_ps, i + 1)
                nc.scalar.copy(wT[:, i].rearrange("p k n -> p (k n)"), ps[:, i % 8, :]).then_inc(s_wt, 1)
            act.wait_ge(s_par, 6 * 16)
            nc.scalar.activation(head_col[:, 0:1], head_col[:, 0:1], ACT.Abs).then_inc(s_hp, 1)
            act.wait_ge(s_hp, 2)
            nc.scalar.activation(head_col[:, 0:1], head_col[:, 0:1], ACT.Exp, scale=-EXP_SCALING).then_inc(s_hp, 1)
            nc.scalar.activation(head_row[:, 0:2, :], head_row[:, 0:2, :], ACT.Exp,
                                 scale=EXP_SCALING).then_inc(s_hp, 1)

            def channel_major(dst, pair, ready, want, done):
                act.wait_ge(ready, want)
                nc.scalar.copy(dst, ps[:, pair:pair + 2, :]).then_inc(done, 1)

            def mid_part(rest_ready, base, i, buf, done):
                act.wait_ge(rest_ready, base + i + 1)
                nc.scalar.copy(parts[buf][:, 1, :], rest[i % 2]).then_inc(done, 1)

            def ln_copy(kind, n, pair, dst):
                channel_major(dst, pair, s_lnT[kind], n + 1, s_lnC[kind])

            def first_copy(b, p, gi):
                n = b * 2 + p
                f = n * NCH
                src = ps[:, FIRST_BANK, :]
                if gi == FIRST_O[0]:
                    act.wait_ge(s_first_oT, n + 1)
                    nc.scalar.copy(first_oT[:, 0, :], src).then_inc(s_first_oC, 1)
                elif gi == FIRST_O[1]:
                    act.wait_ge(s_oTp, f + 1)
                    nc.scalar.copy(first_oT[:, 1, :], src).then_inc(s_oTc, 1)
                elif gi == FIRST_LN[0]:
                    act.wait_ge(s_first_lnT, n + 1)
                    nc.scalar.copy(xnT[:, 0, 1:1 + CH], src).then_inc(s_first_lnC, 1)
                else:
                    act.wait_ge(s_lnT["ffn"], f + 1)
                    nc.scalar.copy(xnT[:, 1, 1:1 + CH], src).then_inc(s_lnC["ffn"], 1)

            def attend(a, b, g, left_used):
                sm = att[a]
                for u in range(2):
                    inst = b * NHG + g * 2 + u
                    for gi, grp in enumerate(GROUPS):
                        if u == 0 and gi == NP_BUF - 2:
                            act.wait_ge(*left_used)
                        if gi in DIAG_GROUPS:
                            act.wait_ge(sm["masked"], inst * ND + DIAG_GROUPS.index(gi) + 1)
                        else:
                            act.wait_ge(sm["scores"], inst * NG + gi + 1)
                        act.wait_ge(sm["p_free"], P_FREE_0 + inst * NG + gi + 1 - NP_BUF)
                        w = len(grp) * CH
                        nc.scalar.activation(
                            probs[:, (u * NG + gi) % NP_BUF, 0:w],
                            ps[:, GB * (gi % NS_BUF):GB * (gi % NS_BUF) + len(grp), :].rearrange("p a n -> p (a n)"),
                            ACT.Exp, scale=SCALE[a]).then_inc(sm["probs"], 1)
                        if u == 1 and gi - 2 in FIRST_O + FIRST_LN:
                            with act.If(g > NHG // 2 - 2):
                                first_copy(b, "AB".index(a), gi - 2)

            def b_squares(b, c):
                e = b * NCH + c
                if c >= 1:
                    act.wait_ge(s_len, 2 * e)
                act.wait_ge(s_kt, e + 1)
                nc.scalar.activation(sq_k, bank2(0), ACT.Square).then_inc(s_sqk, 1)
                act.wait_ge(s_vt, e + 1)
                nc.scalar.activation(sq_v, bank2(2), ACT.Square).then_inc(s_sqv, 1)
                if c >= 2:
                    act.wait_ge(s_knT, 2 * (e - 1))
                nc.scalar.copy(kn_tok[c % 2].rearrange("p t d -> p (t d)"), bank2(0)).then_inc(s_ktok, 1)
                nc.scalar.copy(v_all[:, TB * c:TB * (c + 1), :].rearrange("p t d -> p (t d)"),
                               bank2(2)).then_inc(s_vtok, 1)

            def mix(b, p):
                f0 = b * 2 * NCH + p * NCH
                e0 = b * NCH

                def o_copy(c):
                    channel_major(oT, 0, s_oTp, f0 + c + 1, s_oTc)

                def ffn_input(c):
                    ln_copy("ffn", f0 + c, 4, xnT[:, :, c * CH + 1:c * CH + 1 + CH])

                def b_inputs(c):
                    cols = slice(c * CH, (c + 1) * CH)
                    channel_major(vT[:, :, cols], 6, s_vb, e0 + c + 1, s_vraw)
                    channel_major(kT[:, :, cols], 4, s_kb, e0 + c + 1, s_kraw)

                for c in range(NCH):
                    f = f0 + c
                    if c + 1 < NCH:
                        o_copy(c + 1)
                    if p == 0 and c >= 1:
                        ffn_input(c)
                    if p == 0 and c + 1 == NCH:
                        b_inputs(c - 2)
                    act.wait_ge(s_kp, f + 1)
                    nc.scalar.activation(k_act, ps[:, 0:2, :], ACT.Relu).then_inc(s_relu, 1)
                    act.wait_ge(s_rp, f + 1)
                    if c >= 1:
                        act.wait_ge(s_x2, f)
                    nc.scalar.activation(r_gate.rearrange("p t d -> p (t d)"), bank2(6),
                                         ACT.Sigmoid).then_inc(s_sig, 1)
                    if p == 1 and c + 1 < NCH:
                        ffn_input(c + 1)
                    if p == 0 and c >= 1:
                        ln_copy("b", e0 + c - 1, 4, xn3T)
                        if c != NCH - 2:
                            b_inputs(c - 1)
                if p == 0:
                    b_squares(b, 0)
                    ln_copy("b", e0 + NCH - 1, 4, xn3T)
                    b_inputs(NCH - 1)

            with act.Fori(0, B) as b:
                ln_copy("a", b * NCH, 0, xnT[:, :, 1:1 + CH])
                for c in range(NCH):
                    e = b * NCH + c
                    if c >= 1:
                        act.wait_ge(s_nrm, e)
                    for i in range(4):
                        act.wait_ge(s_qk, e * 4 + i + 1)
                        if c >= 1:
                            act.wait_ge(s_parts[i], e * 48)
                        nc.scalar.copy(parts[i][:, 0, :], ps[:, 4 + i, :])
                        nc.scalar.activation(sq_b[i], ps[:, 4 + i, :], ACT.Square).then_inc(s_h, 1)
                        if i >= 1:
                            mid_part(s_r1, e * 4, i - 1, i - 1, s_mid)
                    if c + 1 < NCH:
                        ln_copy("a", e + 1, 0, xnT[:, :, (c + 1) * CH + 1:(c + 2) * CH + 1])
                    mid_part(s_r1, e * 4, 3, 3, s_mid)
                    act.wait_ge(s_v, e + 1)
                    nc.scalar.copy(v_all[:, TB * c:TB * (c + 1), :].rearrange("p t d -> p (t d)"),
                                   bank2(2)).then_inc(s_vcopy, 1)
                for i in range(2):
                    act.wait_ge(s_parts[i], (b + 1) * NCH * 48)
                held(act)
                with act.Fori(0, NHG // 2) as g:
                    attend("A", b, g, (s_low, (b + 1) * NCH * 4))
                mix(b, 0)
                for c in range(1, NCH + 2):
                    e = b * NCH + c
                    if c < NCH:
                        b_squares(b, c)
                    if c >= 2:
                        for i in range(2):
                            mid_part(s_r1B, (e - 2) * 2, i, 2 * (c % 2) + i, s_midB)
                    if c <= NCH:
                        buf = 2 * ((c - 1) % 2)
                        for i in range(2):
                            act.wait_ge(s_knT, (e - 1) * 2 + i + 1)
                            if c >= 3:
                                act.wait_ge(s_partsB[buf + i], (b * 2 + (c - 1) // 2) * 48)
                            nc.scalar.copy(parts[buf + i][:, 0, :], ps[:, 4 + buf + i, :]).then_inc(s_hB, 1)
                for i in range(2):
                    act.wait_ge(s_partsB[i], (b + 1) * 96)
                held(act)
                with act.Fori(0, NHG // 2) as g:
                    attend("B", b, g, (s_lowB, (b + 1) * NCH * 2))
                mix(b, 1)

        @block.tensor
        def _(pe):
            for a in "AB":
                pe.sem_inc(att[a]["p_free"], P_FREE_0)
            pe.wait_ge(s_ident, 1)
            for i in range(10):
                pe.wait_ge(s_w[i], 16)
                if i >= 8:
                    pe.wait_ge(s_wt, i - 7)
                for kt in range(KT):
                    for m in range(KT):
                        last = pe.transpose(ps[:, i % 8, kt * D + m * P:kt * D + (m + 1) * P],
                                            w_nat[:, i, m, kt * P:(kt + 1) * P], ident[:, :])
                last.then_inc(s_wt_ps, 1)
            pe.wait_ge(s_wt, 10)
            pe.wait_ge(s_hp, 4)
            pe.wait_ge(s_const, 1)
            for kt in range(KT):
                pe.matmul(ps[:, 0, 2 * kt:2 * kt + 2], sel_ch[:, kt * P:(kt + 1) * P], head_col[:, :],
                          start=True, stop=True)
            pe.matmul(ps[:, 1, 0:2 * H], ones_row[:, :], head_row[:, 0:2, :].rearrange("o k h -> o (k h)"),
                      start=True, stop=True).then_inc(s_hp_ps, 1)
            pe.wait_ge(s_setup, 1)

            def to_channels(bk, src):
                for kt in range(KT):
                    for tb in range(TB):
                        last = pe.transpose(ps[:, bk + kt, tb * P:(tb + 1) * P], src[:, tb, kt * P:(kt + 1) * P],
                                            ident[:, :])
                return last

            def to_tokens(bk, src):
                for tb in range(TB):
                    for kt in range(KT):
                        last = pe.transpose(tok_bank(bk, tb)[:, kt * P:(kt + 1) * P],
                                            src[:, kt, tb * P:(tb + 1) * P], ident[:, :])
                return last

            def project_channels(bk, w, m, src):
                for kt in range(KT):
                    last = pe.matmul(ps[:, bk, :], wT[:, w, kt, m * P:(m + 1) * P], src[:, kt, :],
                                     start=(kt == 0), stop=(kt == KT - 1))
                return last

            def project_tokens(bk, w, src):
                for tb in range(TB):
                    for kt in range(KT):
                        last = pe.matmul(tok_bank(bk, tb), src[:, kt, tb * P:(tb + 1) * P], wT[:, w, kt, :],
                                         start=(kt == 0), stop=(kt == KT - 1))
                return last

            def row_maxima(a, u, j, n, probs_before):
                sm = att[a]
                kk, qq = (stage[0:KROWS, 2 * u + s, j * S:(j + 1) * S] for s in range(2))
                for i, (qb, b0, nb) in enumerate(MAX_PIECES):
                    if i < MAX_BUF and probs_before is not None:
                        pe.wait_ge(sm["probs"], probs_before + i + 1 - NS_BUF)
                    if i >= MAX_BUF:
                        pe.wait_ge(sm["mx_used"], n * NMP + i + 1 - MAX_BUF)
                    for bk in range(b0, b0 + nb):
                        o = ps[:, MAX_GB * (i % MAX_BUF) + bk - b0, :]
                        w = min(CH, (qb + 1) * P - bk * CH)
                        diag = (bk == qb // TB)
                        last = pe.matmul(o[:, 0:w], qq[:, qb * P:(qb + 1) * P], kk[:, bk * CH:bk * CH + w],
                                         start=True, stop=True)
                        if diag:
                            last = pe.matmul(o[:, w - P:w], ident_b[:, :], mask_qk[a][:, :], start=False, stop=True,
                                             skip_group_check=True)
                    last.then_inc(sm["mx_scores"], 1)
                pe.wait_ge(sm["mx_col"], n + 1)
                pe.transpose(ps[0:NT, 6, 0:P], row_max[:, :], ident[:, :]).then_inc(sm["mx_T"], 1)
                pe.wait_ge(sm["mx_dma"], (n + 1) * 48)

            def first_chunk(b, p, inst, gi):
                n = b * 2 + p
                f = n * NCH
                o = ps[:, FIRST_BANK, :]

                def turn_half(src, kt):
                    for tb in range(TB):
                        last = pe.transpose(o[:, tb * P:(tb + 1) * P], src[:, tb, kt * P:(kt + 1) * P], ident[:, :])
                    return last

                def project_half(half):
                    for i in range(TB // 2):
                        tb = half * (TB // 2) + i
                        for kt in range(KT):
                            last = pe.matmul(o[:, i * D:(i + 1) * D], first_oT[:, kt, tb * P:(tb + 1) * P],
                                             wT[:, WO if p == 0 else BC, kt, :], start=(kt == 0), stop=(kt == KT - 1))
                    return last

                if gi == FIRST_O[0]:
                    pe.wait_ge(att["AB"[p]]["o_free"], inst * NCH + NCH + 1)
                    turn_half(o_tok[:, 0:TB, :], 0).then_inc(s_first_oT, 1)
                elif gi == FIRST_O[1]:
                    pe.wait_ge(s_first_oC, n + 1)
                    turn_half(o_tok[:, 0:TB, :], 1).then_inc(s_oTp, 1)
                elif gi == FIRST_PROJ[0]:
                    pe.wait_ge(s_oTc, f + 1)
                    project_half(0).then_inc(s_first_proj, 1)
                elif gi == FIRST_PROJ[1]:
                    pe.wait_ge(s_first_res, n + 1)
                    project_half(1).then_inc(s_oproj, 1)
                elif gi == FIRST_LN[0]:
                    pe.wait_ge(s_ln["ffn"], f + 1)
                    turn_half(xnt[0], 0).then_inc(s_first_lnT, 1)
                else:
                    pe.wait_ge(s_first_lnC, n + 1)
                    turn_half(xnt[0], 1).then_inc(s_lnT["ffn"], 1)

            def attend(a, b):
                sm = att[a]

                def first_there(c):
                    pe.wait_ge(sm[f"kq_first{c}"], (b + 1) * 16 * FIRST_LOADS[c])

                def begin(u, hg, inst, kq, fresh):
                    if fresh:
                        first_there(0)
                    else:
                        pe.wait_ge(sm[f"kq{u}"], kq)
                    held(pe)
                    grp = pe.value_load(flags[a][0:1, bass.ds(H + hg, 1)])
                    with pe.If(grp > 0):
                        if fresh:
                            for c in range(1, NCH):
                                first_there(c)
                            held(pe)
                        for j in range(HG):
                            flag = pe.value_load(flags[a][0:1, bass.ds(hg * HG + j, 1)])
                            with pe.If(flag > 0):
                                row_maxima(a, u, j, inst * HG + j, None if fresh else inst * NG)
                            with pe.Else():
                                pe.sem_inc(sm["mx_scores"], NMP)
                                pe.sem_inc(sm["mx_T"], 1)
                    with pe.Else():
                        pe.sem_inc(sm["mx_scores"], NMP * HG)
                        pe.sem_inc(sm["mx_T"], HG)

                def scores(u, inst, gi, fresh=False):
                    kk = stage[0:KROWS, 2 * u, :].rearrange("r (j n) -> r j n", j=HG)
                    qq = stage[0:KROWS, 2 * u + 1, :].rearrange("r (j n) -> r j n", j=HG)
                    if not fresh:
                        pe.wait_ge(sm["probs"], inst * NG + gi + 1 - NS_BUF)
                    if u == 0 and GROUPS[gi][0][0][0] != GROUPS[gi - 1][0][0][0] and gi:
                        first_there(GROUPS[gi][0][0][0])
                    for n, bk in enumerate(GROUPS[gi]):
                        for qc, kb, j, q0, w, col in bk:
                            o = ps[:, GB * (gi % NS_BUF) + n, col:col + w]
                            last = pe.matmul(o, kk[:, j, kb * P:(kb + 1) * P],
                                             qq[:, j, qc * CH + q0:qc * CH + q0 + w], start=True, stop=True)
                    last.then_inc(sm["scores"], 1)

                def products(u, inst, gi):
                    pe.wait_ge(sm["probs"], inst * NG + gi + 1)
                    for units, last_group, freed in VALUE_SETS:
                        if last_group != gi:
                            continue
                        qc, kb = units[0][1][0:2]
                        if kb == 0:
                            pe.wait_ge(sm["vst"], inst * NCH + qc + 1)
                            pe.wait_ge(sm["o_free"], inst * NCH + qc + 1)
                        for bank, (_, _, j, q0, w, col) in units:
                            grp, n = BANK_AT[bank]
                            slot = (u * NG + grp) % NP_BUF
                            at = n * CH + col
                            last = pe.matmul(ps[HS * j:HS * (j + 1), 6 + qc % 2, q0:q0 + w],
                                             v_st[:, u, kb, j, :], probs[:, slot, at:at + w],
                                             start=(kb == 0), stop=(kb >= TB * qc), skip_group_check=True)
                        if freed:
                            last.then_inc(sm["p_free"], freed)

                def turn(inst, qc):
                    pe.wait_ge(sm["o_ev"], inst * NCH + qc + 1)
                    for tb in range(TB):
                        last = pe.transpose(ps[:, 6 + qc % 2, tb * P:(tb + 1) * P],
                                            o_ev[:, qc % 2, tb * P:(tb + 1) * P], ident[:, :])
                    last.then_inc(sm["o_T"], 1)

                begin(0, 0, b * NHG, None, fresh=True)
                for gi in range(NS_BUF):
                    scores(0, b * NHG, gi, fresh=True)
                if a == "B":
                    pe.wait_ge(s_r1B, (b + 1) * NCH * 2)
                    held(pe)
                with pe.Fori(0, NHG // 2) as g:
                    for u in range(2):
                        hg = g * 2 + u
                        inst = b * NHG + hg

                        def ahead(gi):
                            n = gi + NS_BUF - NG
                            if n < 0:
                                scores(u, inst, gi + NS_BUF)
                            elif u == 0:
                                if n == 0:
                                    begin(1, hg + 1, inst + 1, (b * (NHG // 2) + g + 1) * 16 * LOADS, fresh=False)
                                scores(1, inst + 1, n)
                            else:
                                with pe.If(g < NHG // 2 - 1):
                                    if n == 0:
                                        begin(0, at_most(hg + 1, NHG - 1), inst + 1, (b * (NHG // 2 - 1) + g + 1) * 16 * LOADS,
                                              fresh=False)
                                    scores(0, inst + 1, n)

                        for gi in range(NG):
                            ahead(gi)
                            products(u, inst, gi)
                            for qc in range(NCH - 1):
                                if gi == TURN_GROUP[qc]:
                                    turn(inst, qc)
                            if u == 1 and gi in FIRST_O + FIRST_PROJ + FIRST_LN:
                                with pe.If(g > NHG // 2 - 2):
                                    first_chunk(b, "AB".index(a), inst, gi)
                            if gi == NS_BUF:
                                if u == 1:
                                    turn(inst - 1, NCH - 1)
                                else:
                                    with pe.If(g > 0):
                                        turn(inst - 1, NCH - 1)
                return lambda: turn(b * NHG + NHG - 1, NCH - 1)

            def b_tokens(b, c):
                e = b * NCH + c
                pe.wait_ge(s_scan, e + 1)
                if c >= 1:
                    pe.wait_ge(s_ktok, e)
                to_tokens(0, kT[:, :, c * CH:(c + 1) * CH]).then_inc(s_kt, 1)
                pe.wait_ge(s_vm, e + 1)
                if c == 0:
                    pe.wait_ge(s_gated, b * 2 * NCH + NCH)
                else:
                    pe.wait_ge(s_vtok, e)
                to_tokens(2, v_mix).then_inc(s_vt, 1)

            def mix(b, p, last_turn):
                f0 = b * 2 * NCH + p * NCH
                e0 = b * NCH

                def o_turn(c):
                    pe.wait_ge(att["AB"[p]]["o_free"], ((b + 1) * NHG - 1) * NCH + c + 3)
                    to_channels(0, o_tok[:, TB * c:TB * (c + 1), :]).then_inc(s_oTp, 1)

                def o_project(c):
                    pe.wait_ge(s_oTc, f0 + c + 1)
                    if c == 1 or p == 1:
                        pe.wait_ge(s_res, f0 + c)
                    else:
                        pe.wait_ge(s_gated, f0 + c - 1)
                    project_tokens(2, WO if p == 0 else BC, oT).then_inc(s_oproj, 1)

                def ln_turn(c):
                    pe.wait_ge(s_ln["ffn"], f0 + c + 1)
                    if p == 0 and c + 1 == NCH:
                        pe.wait_ge(s_lnC["b"], e0 + c - 1)
                    elif p == 0 and c >= 2:
                        pe.wait_ge(s_kraw, e0 + c - 1)
                    to_channels(4, xnt[0]).then_inc(s_lnT["ffn"], 1)

                def hidden(c):
                    pe.wait_ge(s_xk, f0 + c + 1)
                    project_channels(0, FK, 0, x_k)
                    project_channels(1, FK, 1, x_k).then_inc(s_kp, 1)
                    pe.wait_ge(s_xr, f0 + c + 1)
                    if p == 0 and c >= 2:
                        pe.wait_ge(s_vraw, e0 + c - 1)
                    elif p == 1 and c >= 1:
                        pe.wait_ge(s_gated, f0 + c)
                    project_tokens(6, FR, x_r).then_inc(s_rp, 1)

                def ffn_out(c):
                    pe.wait_ge(s_kact, f0 + c + 1)
                    if ffn_bank(p, c) == 6:
                        pe.wait_ge(s_sig, f0 + c + 1)
                    elif c + 1 < NCH:
                        pe.wait_ge(s_res, f0 + c + 2)
                    elif p == 0:
                        pe.wait_ge(s_gated, f0 + c)
                    else:
                        pe.wait_ge(s_res, f0 + c + 1)
                    project_tokens(ffn_bank(p, c), FV, k_act).then_inc(s_fv, 1)

                def b_turn(c):
                    pe.wait_ge(s_ln["b"], e0 + c + 1)
                    if c + 2 >= NCH:
                        pe.wait_ge(s_kraw, e0 + c)
                    to_channels(4, xnt[1]).then_inc(s_lnT["b"], 1)

                def b_project(c):
                    pe.wait_ge(s_lnC["b"], e0 + c + 1)
                    if c + 1 < NCH:
                        pe.wait_ge(s_sig, f0 + c + 2)
                    else:
                        pe.wait_ge(s_vraw, e0 + c)
                    project_channels(6, BV, 0, xn3T)
                    project_channels(7, BV, 1, xn3T).then_inc(s_vb, 1)
                    if c == NCH - 3:
                        pe.wait_ge(s_lnC["ffn"], f0 + NCH)
                    project_channels(4, BK, 0, xn3T)
                    project_channels(5, BK, 1, xn3T).then_inc(s_kb, 1)

                o_turn(1)
                last_turn()
                o_project(1)
                for c in range(NCH):
                    if p == 0 and 2 <= c + 1 < NCH:
                        o_turn(c + 1)
                    if p == 0 and c >= 1:
                        ln_turn(c)
                    if 2 <= c + 1 < NCH:
                        o_project(c + 1)
                    if p == 0 and c + 1 == NCH:
                        b_project(c - 2)
                    hidden(c)
                    if p == 0 and c >= 1:
                        b_turn(c - 1)
                    if p == 1 and c + 1 < NCH:
                        ln_turn(c + 1)
                    if p == 1 and c + 2 < NCH:
                        pe.wait_ge(s_relu, f0 + c + 1)
                        o_turn(c + 2)
                    ffn_out(c)
                    if p == 0 and c >= 1 and c != NCH - 2:
                        b_project(c - 1)
                if p == 0:
                    b_tokens(b, 0)
                    b_turn(NCH - 1)
                    b_project(NCH - 1)

            with pe.Fori(0, B) as b:
                def a_turn(c):
                    e = b * NCH + c
                    pe.wait_ge(s_ln["a"], e + 1)
                    if c == 1:
                        pe.wait_ge(s_r1, e * 4 - 3)
                    if c >= 2:
                        pe.wait_ge(s_nmax, e - 1)
                    to_channels(0, xnt_a[c % 2]).then_inc(s_lnT["a"], 1)

                a_turn(0)
                for c in range(NCH):
                    e = b * NCH + c
                    xc = xnT[:, :, c * CH + 1:c * CH + 1 + CH]
                    pe.wait_ge(s_lnC["a"], e + 1)
                    for i in range(4):
                        if c >= 1:
                            pe.wait_ge(s_r1, (e - 1) * 4 + i + 1)
                        project_channels(4 + i, WQ + i % 2, i // 2, xc).then_inc(s_qk, 1)
                    if c + 1 < NCH:
                        a_turn(c + 1)
                    if c >= 1:
                        pe.wait_ge(s_vcopy, e)
                    project_tokens(2, WV, xc).then_inc(s_v, 1)
                    pe.wait_ge(s_h, e * 4 + 4)
                    if c + 1 < NCH:
                        pe.wait_ge(s_lnC["a"], e + 2)
                    else:
                        pe.wait_ge(s_nmax, e)
                    for side in range(2):
                        for kt in range(KT):
                            last = pe.matmul(ps[0:H, side, :], head_sel[:, kt, :], sq_b[2 * kt + side],
                                             start=(kt == 0), stop=(kt == KT - 1))
                    last.then_inc(s_nrm, 1)
                pe.wait_ge(s_flc, b + 1)
                held(pe)
                pe.matmul(ps[0:1, 0, 0:H], fl_col[:, :], ident[0:H, 0:H], start=True, stop=True).then_inc(s_flr, 1)
                pe.wait_ge(s_fl, b + 1)
                held(pe)
                pe.wait_ge(s_vcopy, (b + 1) * NCH)
                last_turn = attend("A", b)
                mix(b, 0, last_turn)
                for c in range(1, NCH + 1):
                    e = b * NCH + c
                    if c < NCH:
                        b_tokens(b, c)
                    pe.wait_ge(s_kn, e)
                    if c == 1:
                        pe.wait_ge(s_kraw, (b + 1) * NCH)
                    for kt in range(KT):
                        if c >= 3:
                            pe.wait_ge(s_r1B, (e - 3) * 2 + kt + 1)
                        bk = 4 + 2 * ((c - 1) % 2) + kt
                        for tb in range(TB):
                            last = pe.transpose(ps[:, bk, tb * P:(tb + 1) * P],
                                                kn_tok[(c - 1) % 2][:, tb, kt * P:(kt + 1) * P], ident[:, :])
                        last.then_inc(s_knT, 1)
                pe.wait_ge(s_vtok, (b + 1) * NCH)
                pe.wait_ge(s_r1B, (b + 1) * NCH * 2 - 2)
                last_turn = attend("B", b)
                mix(b, 1, last_turn)

        @block.vector
        def _(dve):
            for a in "AB":
                dve.sem_inc(att[a]["o_free"], 2)
            steps, base = [0], [0]

            def step(ins):
                steps[0] += 1
                ins.then_inc(s_dve, 1)

            def wait_steps():
                dve.wait_ge(s_dve, base[0] + steps[0])

            settle = wait_steps

            def rsqrt(n, between=()):
                between = iter(between)

                def settle():
                    next(between, lambda: None)()
                    wait_steps()

                v, y, w = nw_v[:, 0:n], nw_y[:, 0:n], nw_u[:, 0:n]
                step(nc.vector.tensor_scalar(y.bitcast(I32), v.bitcast(I32), 1, None, ALU.arith_shift_right))
                settle()
                step(nc.vector.tensor_scalar(y.bitcast(I32), y.bitcast(I32), -1.0, float(RSQRT_MAGIC), ALU.mult,
                                             ALU.add))
                settle()
                for _ in range(3):
                    step(nc.vector.tensor_tensor(w, y, y, ALU.mult))
                    settle()
                    step(nc.vector.scalar_tensor_tensor(w, w, -0.5, v, ALU.mult, ALU.mult))
                    settle()
                    step(nc.vector.scalar_tensor_tensor(y, w, 1.5, y, ALU.add, ALU.mult))
                    settle()

            def layernorm(c, kind, n, dst, before):
                for tb in range(TB):
                    step(nc.vector.bn_stats(ln_st[:, tb, :], x_res[:, TB * c + tb, :]))
                settle()
                held(dve)
                for tb in range(TB):
                    step(nc.vector.bn_aggr(ln_mv[:, tb, :], ln_st[:, tb, :]))
                settle()
                step(nc.vector.tensor_scalar(nw_v[:, 0:TB], ln_mv[:, :, 1], EPS, None, ALU.add))
                settle()
                rsqrt(TB)
                if before:
                    dve.wait_ge(s_lnT[kind], n + 1 - before)
                for tb in range(TB):
                    last = nc.vector.tensor_scalar(dst[:, tb, :], x_res[:, TB * c + tb, :],
                                                   ln_mv[:, tb, 0:1], nw_y[:, tb:tb + 1], ALU.subtract, ALU.mult)
                last.then_inc(s_ln[kind], 1)
                dve.wait_ge(s_ln[kind], n + 1)

            def a_layernorm(b, c):
                dve.wait_ge(s_x[c], (b + 1) * 16)
                layernorm(c, "a", b * NCH + c, xnt_a[c % 2], 2 if c >= 2 else 0)

            for c in range(2):
                a_layernorm(0, c)
            steps_before = steps[0]

            dve.wait_ge(s_par, 6 * 16)
            nc.vector.tensor_scalar(head_row[:, 0, :], head_row[:, 0, :], KEY_SCALE_MAX / EXP_SCALING, None,
                                    ALU.min).then_inc(s_hp, 1)
            dve.wait_ge(s_hp, 4)
            nc.vector.tensor_tensor(head_row[:, 2, :], head_row[:, 0, :], head_row[:, 0, :],
                                    ALU.mult).then_inc(s_hp, 1)
            dve.wait_ge(s_hp, 5)
            nc.vector.tensor_scalar(flags["B"][:, 0:H], head_row[:, 2, :], SAFE, None, ALU.is_gt)
            nc.vector.tensor_reduce(fl_any[:, :], head_row[:, 2, :].rearrange("o (g j) -> o g j", j=HG), AX_X,
                                    ALU.max).then_inc(s_hp, 1)
            dve.wait_ge(s_hp, 6)
            nc.vector.tensor_scalar(flags["B"][:, H:H + NHG], fl_any[:, :], SAFE, None, ALU.is_gt)
            dve.wait_ge(s_hp_ps, 1)
            for kt in range(KT):
                nc.vector.tensor_copy(decay[:, kt:kt + 1], ps[:, 0, 2 * kt:2 * kt + 1])
                nc.vector.tensor_copy(v_coef[:, kt:kt + 1], ps[:, 0, 2 * kt + 1:2 * kt + 2])
            nc.vector.tensor_copy(scale_row[:, :, :].rearrange("p k h -> p (k h)"),
                                  ps[:, 1, 0:2 * H]).then_inc(s_setup, 1)
            dve.wait_ge(s_setup, 1)

            with dve.Fori(0, B) as b:
                steps[0], base[0] = 0, b * DVE_STEPS + steps_before

                def split_rest(bk, buf, high_ready, base, i, done, low_done, low_before):
                    dve.wait_ge(high_ready, base + i + 1)
                    if low_before:
                        dve.wait_ge(low_done, base + i - 1)
                    nc.vector.tensor_tensor(rest[i % 2], ps[:, bk, :], parts[buf][:, 0, :],
                                            ALU.subtract).then_inc(done, 1)

                def row_maxima(a, n):
                    sm = att[a]
                    for i, (qb, b0, nb) in enumerate(MAX_PIECES):
                        dve.wait_ge(sm["mx_scores"], n * NMP + i + 1)
                        w = min((b0 + nb) * CH, (qb + 1) * P) - b0 * CH
                        at = MAX_GB * (i % MAX_BUF)
                        src = ps[:, at:at + nb, :].rearrange("p a n -> p (a n)")[:, 0:w]
                        nc.vector.tensor_reduce(pmax[:, 1 if b0 else 0, qb:qb + 1], src, AX_X,
                                                ALU.max).then_inc(sm["mx_used"], 1)
                    dve.wait_ge(sm["mx_used"], (n + 1) * NMP)
                    nc.vector.tensor_tensor(row_max[:, :], pmax[:, 0, :], pmax[:, 1, :],
                                            ALU.max).then_inc(sm["mx_col"], 1)
                    dve.wait_ge(sm["mx_T"], n + 1)
                    mt = ps[0:NT, 6, 0:P]
                    nc.vector.tensor_scalar(m_part[0][:, :], mt, -1.0, None, ALU.mult).then_inc(sm["mx_step"], 1)
                    dve.wait_ge(sm["mx_step"], n * 3 + 1)
                    nc.vector.scalar_tensor_tensor(m_rest[:, :], mt, -1.0, m_part[0][:, :], ALU.mult,
                                                   ALU.subtract).then_inc(sm["mx_step"], 1)
                    dve.wait_ge(sm["mx_step"], n * 3 + 2)
                    nc.vector.tensor_copy(m_part[1][:, :], m_rest[:, :]).then_inc(sm["mx_step"], 1)
                    dve.wait_ge(sm["mx_step"], n * 3 + 3)
                    nc.vector.tensor_tensor(m_part[2][:, :], m_rest[:, :], m_part[1][:, :],
                                            ALU.subtract).then_inc(sm["mx_row"], 1)

                def first_residual(p):
                    n = b * 2 + p
                    for half, (ready, want, done) in enumerate(((s_first_proj, n + 1, s_first_res),
                                                                (s_oproj, n * NCH + 1, s_res))):
                        res = x_res[:, half * (TB // 2):(half + 1) * (TB // 2), :].rearrange("p t d -> p (t d)")
                        dve.wait_ge(ready, want)
                        nc.vector.tensor_tensor(res, res, ps[:, FIRST_BANK, :], ALU.add).then_inc(done, 1)
                    dve.wait_ge(s_res, n * NCH + 1)
                    layernorm(0, "ffn", n * NCH, xnt[0], 0)
                    held(dve)

                def attend(a):
                    sm = att[a]

                    def begin(hg):
                        inst = b * NHG + hg
                        grp = dve.value_load(flags[a][0:1, bass.ds(H + hg, 1)])
                        with dve.If(grp > 0):
                            for j in range(HG):
                                flag = dve.value_load(flags[a][0:1, bass.ds(hg * HG + j, 1)])
                                with dve.If(flag > 0):
                                    row_maxima(a, inst * HG + j)
                                with dve.Else():
                                    dve.sem_inc(sm["mx_used"], NMP)
                                    dve.sem_inc(sm["mx_col"], 1)
                                    dve.sem_inc(sm["mx_step"], 3)
                                    dve.sem_inc(sm["mx_row"], 1)
                        with dve.Else():
                            dve.sem_inc(sm["mx_used"], NMP * HG)
                            dve.sem_inc(sm["mx_col"], HG)
                            dve.sem_inc(sm["mx_step"], 3 * HG)
                            dve.sem_inc(sm["mx_row"], HG)

                    def masks(hg, groups):
                        inst = b * NHG + hg
                        for gi, at, n in groups:
                            dve.wait_ge(sm["scores"], inst * NG + gi + 1)
                            bk = GB * (gi % NS_BUF)
                            nb = len(GROUPS[gi])
                            units = ps[:, bk:bk + nb, :]
                            if n == 1:
                                units = units[:, :, 0:P]
                                mask = mask_kq[a][:, :].unsqueeze(1).to_broadcast([P, nb, P])
                            else:
                                units = units.rearrange("p b (n w) -> p b n w", w=P)[:, :, 0:at // P + 1:at // P, :]
                                mask = mask_kq[a][:, :].unsqueeze(1).unsqueeze(1).to_broadcast([P, nb, n, P])
                            nc.vector.tensor_tensor(units, units, mask, ALU.add).then_inc(sm["masked"], 1)

                    def take(hg, qc):
                        inst = b * NHG + hg
                        dve.wait_ge(sm["p_free"], P_FREE_0 + inst * NG + LAST_GROUP[qc] + 1)
                        nc.vector.tensor_copy(o_ev[:, qc % 2, :], ps[:, 6 + qc % 2, :]).then_inc(sm["o_ev"], 1)

                    def normalise(hg, qc):
                        k = (b * NHG + hg) * NCH + qc
                        dve.wait_ge(sm["o_T"], k + 1)
                        o = ps[:, 6 + qc % 2, :].rearrange("p (t j e) -> p t j e", t=TB, j=HG)
                        nc.vector.tensor_scalar(den[:, :, :], o[:, :, :, DK], 1.0e-37, None,
                                                ALU.max).then_inc(sm["o_step"], 1)
                        dve.wait_ge(sm["o_step"], k * 2 + 1)
                        nc.vector.reciprocal(rec[:, :, :], den[:, :, :]).then_inc(sm["o_step"], 1)
                        dve.wait_ge(sm["o_step"], k * 2 + 2)
                        dst = o_tok[:, TB * qc:TB * (qc + 1), bass.ds(hg * HG * DK, HG * DK)]
                        nc.vector.tensor_tensor(
                            dst.rearrange("p t (j e) -> p t j e", j=HG), o[:, :, :, 0:DK],
                            rec[:, :, :].unsqueeze(3).to_broadcast([P, TB, HG, DK]),
                            ALU.mult).then_inc(sm["o_free"], 1)

                    def ahead(hg):
                        begin(hg)
                        masks(hg, DIAG[0][:NS_BUF])

                    ahead(0)
                    with dve.Fori(0, NHG // 2) as g:
                        for u in range(2):
                            hg = g * 2 + u
                            masks(hg, DIAG[0][NS_BUF:])
                            if u == 1:
                                normalise(hg - 1, NCH - 1)
                            else:
                                with dve.If(g > 0):
                                    normalise(at_most(hg - 1, NHG - 1), NCH - 1)
                            for qc in range(NCH - 1):
                                take(hg, qc)
                                normalise(hg, qc)
                                if u == 1 and qc == NCH - 2:
                                    with dve.If(g > NHG // 2 - 2):
                                        first_residual("AB".index(a))
                                masks(hg, DIAG[qc + 1])
                            if u == 0:
                                ahead(hg + 1)
                            else:
                                with dve.If(g < NHG // 2 - 1):
                                    ahead(at_most(hg + 1, NHG - 1))
                            take(hg, NCH - 1)
                    normalise(NHG - 1, NCH - 1)

                def scan(c):
                    e = b * NCH + c
                    cols = slice(c * CH, (c + 1) * CH)
                    dve.wait_ge(s_kraw, e + 1)
                    if c >= 1:
                        dve.wait_ge(s_scan, e)
                    for kt in range(KT):
                        last = nc.vector.tensor_tensor_scan(
                            kT[:, kt, cols], decay[:, kt:kt + 1].to_broadcast([P, CH]), kT[:, kt, cols],
                            0.0 if c == 0 else kT[:, kt, c * CH - 1:c * CH], ALU.mult, ALU.add)
                    last.then_inc(s_scan, 1)

                def mix_values(c):
                    e = b * NCH + c
                    dve.wait_ge(s_vd, e + 1)
                    if c >= 1:
                        dve.wait_ge(s_vt, e)
                    n = CH if c + 1 < NCH else CH - 1
                    for kt in range(KT):
                        last = nc.vector.scalar_tensor_tensor(
                            v_mix[:, kt, 0:n], v_diff[:, kt, 0:n], v_coef[:, kt:kt + 1],
                            vT[:, kt, c * CH + 1:c * CH + 1 + n], ALU.mult, ALU.add)
                        if n < CH:
                            last = nc.vector.tensor_scalar(v_mix[:, kt, n:CH], v_diff[:, kt, n:CH],
                                                           v_coef[:, kt:kt + 1], None, ALU.mult)
                    last.then_inc(s_vm, 1)

                def mix(p):
                    f0 = b * 2 * NCH + p * NCH

                    def chunk(c):
                        return x_res[:, TB * c:TB * (c + 1), :].rearrange("p t d -> p (t d)")

                    def attention_residual(c):
                        dve.wait_ge(s_oproj, f0 + c + 1)
                        nc.vector.tensor_tensor(chunk(c), chunk(c), bank2(2), ALU.add).then_inc(s_res, 1)
                        dve.wait_ge(s_res, f0 + c + 1)
                        layernorm(c, "ffn", f0 + c, xnt[0], min(c, 1))

                    def token_shift(c):
                        f = f0 + c
                        before = xnT[:, :, c * CH:c * CH + CH]
                        if c >= 1:
                            dve.wait_ge(s_rp, f)
                        for kt in range(KT):
                            dve.wait_ge(s_diff, 2 * f + kt + 1)
                            last = nc.vector.scalar_tensor_tensor(x_k[:, kt, :], x_diff[:, kt, :], mu[:, 1, kt:kt + 1],
                                                                  before[:, kt, :], ALU.mult, ALU.add)
                        last.then_inc(s_xk, 1)
                        for kt in range(KT):
                            last = nc.vector.scalar_tensor_tensor(x_r[:, kt, :], x_diff[:, kt, :], mu[:, 0, kt:kt + 1],
                                                                  before[:, kt, :], ALU.mult, ALU.add)
                        last.then_inc(s_xr, 1)

                    def ffn_residual(c):
                        f = f0 + c
                        dve.wait_ge(s_fv, f + 1)
                        dve.wait_ge(s_sig, f + 1)
                        gate = r_gate.rearrange("p t d -> p (t d)")
                        nc.vector.tensor_tensor(gate, gate, bank2(ffn_bank(p, c)), ALU.mult).then_inc(s_gated, 1)
                        dve.wait_ge(s_gated, f + 1)
                        nc.vector.tensor_tensor(chunk(c), chunk(c), gate, ALU.add).then_inc(s_x2, 1)
                        dve.wait_ge(s_x2, f + 1)

                    def b_layernorm(c):
                        layernorm(c, "b", b * NCH + c, xnt[1], min(c, 1))

                    for c in range(NCH):
                        if p == 0 or c == 0:
                            token_shift(c)
                        if p == 0 and c >= 1:
                            b_layernorm(c - 1)
                        if c + 1 < NCH:
                            attention_residual(c + 1)
                            if p == 1:
                                token_shift(c + 1)
                        elif p == 0:
                            scan(0)
                            scan(1)
                            mix_values(0)
                        else:
                            now = steps[0]
                            held(dve)
                            with dve.If(b < B - 1):
                                for n in range(2):
                                    a_layernorm(b + 1, n)
                                held(dve)
                            with dve.Else():
                                dve.sem_inc(s_dve, steps[0] - now)
                        ffn_residual(c)
                    if p == 0:
                        b_layernorm(NCH - 1)

                for c in range(NCH):
                    e = b * NCH + c
                    for i in range(4):
                        split_rest(4 + i, i, s_h, e * 4, i, s_r1, s_low, low_before=(c >= 1 or i >= 2))
                    if c + 2 < NCH:
                        a_layernorm(b, c + 2)
                    dve.wait_ge(s_nrm, e + 1)
                    nc.vector.tensor_reduce(n_max[:, :, c:c + 1], ps[0:H, 0:2, :], AX_X, ALU.max).then_inc(s_nmax, 1)
                dve.wait_ge(s_nmax, (b + 1) * NCH)
                step(nc.vector.tensor_reduce(n_top[:, :], n_max[:, :, :], AX_X, ALU.max))
                settle()
                step(nc.vector.tensor_tensor(fl_prod[:, :], n_top[:, 0:1], n_top[:, 1:2], ALU.mult))
                settle()
                nc.vector.tensor_scalar(fl_col[:, :], fl_prod[:, :], 1.1 * SCALE["A"] ** 2, SAFE * SAFE, ALU.mult,
                                        ALU.is_gt).then_inc(s_flc, 1)
                dve.wait_ge(s_flr, b + 1)
                nc.vector.tensor_copy(flags["A"][:, 0:H], ps[0:1, 0, 0:H])
                step(nc.vector.tensor_reduce(fl_any[:, :], ps[0:1, 0, 0:H].rearrange("o (g j) -> o g j", j=HG), AX_X,
                                             ALU.max))
                settle()
                held(dve)
                nc.vector.tensor_copy(flags["A"][:, H:H + NHG], fl_any[:, :]).then_inc(s_fl, 1)
                dve.wait_ge(s_fl, b + 1)
                held(dve)
                attend("A")
                mix(0)
                def norm(c):
                    e = b * NCH + c
                    nh = TB * H
                    for side, (ready, sq) in enumerate(((s_sqk, sq_k), (s_sqv, sq_v))):
                        dve.wait_ge(ready, e + 1)
                        nc.vector.tensor_reduce(nw_v[:, side * nh:(side + 1) * nh],
                                                sq.rearrange("p (g e) -> p g e", e=DK), AX_X,
                                                ALU.add).then_inc(s_len, 1)
                    dve.wait_ge(s_len, 2 * (e + 1))
                    step(nc.vector.tensor_scalar(nw_v[:, :], nw_v[:, :], 1.0e-30, None, ALU.max))
                    settle()
                    rsqrt(P, [lambda i=i: split_key(c - 1, i) for i in range(2)] if c >= 1 else ())
                    step(nc.vector.tensor_tensor(nw_u[:, :], nw_v[:, :], nw_y[:, :], ALU.mult))
                    settle()
                    step(nc.vector.tensor_scalar(nw_u[:, :], nw_u[:, :], NORM_EPS, None, ALU.add))
                    settle()
                    step(nc.vector.reciprocal(nw_y[:, :], nw_u[:, :]))
                    settle()
                    key_fac = nw_y[:, 0:nh]
                    if c >= 2:
                        dve.wait_ge(s_vall, e - 1)
                    for side, dst in enumerate((key_fac, v_fac[:, c % 2, :])):
                        last = nc.vector.tensor_tensor(
                            dst.rearrange("p (t h) -> p t h", t=TB),
                            nw_y[:, side * nh:(side + 1) * nh].rearrange("p (t h) -> p t h", t=TB),
                            scale_row[:, side, :].unsqueeze(1).to_broadcast([P, TB, H]), ALU.mult)
                        if side == 0:
                            step(last)
                        else:
                            last.then_inc(s_vfac, 1)
                    settle()
                    dve.wait_ge(s_ktok, e + 1)
                    keys = kn_tok[c % 2].rearrange("p t (h e) -> p (t h) e", e=DK)
                    nc.vector.tensor_tensor(keys, keys, key_fac.unsqueeze(2).to_broadcast([P, nh, DK]),
                                            ALU.mult).then_inc(s_kn, 1)

                def split_key(c, i):
                    buf = 2 * (c % 2) + i
                    split_rest(4 + buf, buf, s_hB, (b * NCH + c) * 2, i, s_r1B, s_lowB, low_before=(c >= 1))

                mix_values(1)
                for c in range(NCH):
                    norm(c)
                    if c + 2 < NCH:
                        scan(c + 2)
                        mix_values(c + 2)
                for i in range(2):
                    split_key(NCH - 1, i)
                attend("B")
                mix(1)
                assert steps[0] <= DVE_STEPS
                dve.sem_inc(s_dve, DVE_STEPS - steps[0])


_WEIGHTS = ["L0_attn_a_q_proj", "L0_attn_a_k_proj", "L0_attn_a_v_proj", "L0_attn_a_o_proj", "L0_ffn_W_r", "L0_ffn_W_k",
            "L0_ffn_W_v", "L0_attn_b_W_k", "L0_attn_b_W_v", "L0_attn_b_W_c"]
_OTHERS = {"X": "L0_attn_a_X", "beta": "L0_attn_b_leaky_key_beta", "key_scale": "L0_attn_b_key_scale",
           "v_coef": "L0_attn_b_v_coef", "val_scale": "L0_attn_b_val_scale", "mu_r": "L0_ffn_mu_r",
           "mu_k": "L0_ffn_mu_k"}


def kernel(**inputs):
    import numpy as _np
    import concourse.bacc as _bacc
    from concourse import mybir as _mybir
    from concourse.bass_utils import run_bass_kernel_spmd as _run

    nc = _bacc.Bacc("TRN2", target_bir_lowering=False, num_devices=1)
    arrays, aps = {}, {}
    for name in _WEIGHTS + list(_OTHERS.values()):
        a = _np.ascontiguousarray(inputs[name])
        arrays[f"in_{name}"] = a
        aps[name] = nc.dram_tensor(f"in_{name}", a.shape, _mybir.dt.from_np(a.dtype), kind="ExternalInput").ap()
    out = nc.dram_tensor("out_0", (B, S, D), F32, kind="ExternalOutput").ap()
    tensors = {short: aps[name] for short, name in _OTHERS.items()}
    tensors["weights"] = [aps[name] for name in _WEIGHTS]
    hybrid_kernel(nc, tensors, out)
    r = _run(nc, [arrays], core_ids=[0])
    return r.results[0]["out_0"]
```
